# Optimizing a Trainium2 kernel written in Bass

```python
import numpy as np
import jax
import jax.numpy as jnp

def _softmax(x, axis=-1):
    return jax.nn.softmax(x, axis=axis)

def _gelu(x):
    return jax.nn.gelu(x, approximate=True)

def _silu(x):
    return jax.nn.silu(x)

def _sigmoid(x):
    return jax.nn.sigmoid(x)

def _layernorm(x, axis=-1, eps=1e-05):
    m = jnp.mean(x, axis=axis, keepdims=True)
    v = jnp.var(x, axis=axis, keepdims=True)
    return (x - m) / jnp.sqrt(v + eps)

def _scatter_add(tgt, idx, src, axis=0):
    return tgt.at[idx].add(src)

def _segment_sum(src, seg, n):
    return jax.ops.segment_sum(src, seg, n)
kernel_name = 'mk_vit_tower_postln_d1_tok_img768_r4_a65661'

def setup_inputs(seed: int=0):
    np.random.seed(seed)
    _w = jnp.asarray

    def _rec_inputs():
        import jax
        import jax.numpy as jnp
        _rk = jax.random.key(seed)
        x = 1.64766e-05 + 1.00005 * jax.random.normal(jax.random.fold_in(_rk, 1), (16, 3, 512, 192), jnp.float32)
        return x
    x = _rec_inputs()

    def _L0_tok_setup():
        import jax, jax.numpy as jnp
        import numpy as np
        NUM_BANDS = 6
        D_MODEL = 192
        B, N = (2, 512)
        IN_FEATURES = 3 * NUM_BANDS * 2 * D_MODEL
        key = jax.random.key(seed)
        k_xyz, k_w = jax.random.split(key)
        xyz = jax.random.normal(k_xyz, (B, 3, N, D_MODEL), dtype=jnp.float32)
        freq_bands = 2.0 ** jnp.linspace(0.0, NUM_BANDS - 1, NUM_BANDS).astype(jnp.float32)
        bound = 1.0 / np.sqrt(IN_FEATURES)
        W = jax.random.uniform(k_w, (D_MODEL, IN_FEATURES), dtype=jnp.float32, minval=-bound, maxval=bound)
        return {'xyz': xyz, 'freq_bands': freq_bands, 'W': W}
    _L0_tok_all = _L0_tok_setup()
    _L0_tok_in = {k: v for k, v in _L0_tok_all.items() if k in ('freq_bands', 'W')}
    del _L0_tok_all

    def _L0_attn_setup():
        import jax, jax.numpy as jnp
        import numpy as np
        NUM_HEADS = 12
        OT_REG = 0.1
        SINKHORN_ITERS = 10
        DIAG_VAL = 1000.0

        def _sot(q):
            N = q.shape[-2]
            qn = q / (jnp.linalg.norm(q, axis=-1, keepdims=True) + 1e-08)
            C = 1.0 - jnp.einsum('bhnd,bhmd->bhnm', qn, qn)
            eye = jnp.eye(N, dtype=bool)
            C = jnp.where(eye, DIAG_VAL, C)
            log_K = -C / OT_REG
            log_marg = -jnp.log(jnp.float32(N))
            log_v = jnp.zeros(q.shape[:2] + (N,), dtype=q.dtype)
            for _ in range(SINKHORN_ITERS):
                log_u = log_marg - jax.nn.logsumexp(log_K + log_v[..., None, :], axis=-1)
                log_v = log_marg - jax.nn.logsumexp(log_K + log_u[..., :, None], axis=-2)
            log_T = log_u[..., :, None] + log_K + log_v[..., None, :]
            z = jnp.exp(log_T)
            z = z / jnp.max(z, axis=(-2, -1), keepdims=True)
            z = jnp.where(eye, 1.0, z)
            return z
        key = jax.random.key(seed)
        k1, k2, k3 = jax.random.split(key, 3)
        B, N, C = (64, 64, 192)
        x = jax.random.normal(k1, (B, N, C), dtype=jnp.float32)
        w_qkv = jax.random.normal(k2, (3 * C, C), dtype=jnp.float32) * C ** (-0.5)
        w_proj = jax.random.normal(k3, (C, C), dtype=jnp.float32) * C ** (-0.5)
        b_proj = jnp.zeros((C,), dtype=jnp.float32)
        return {'x': x, 'w_qkv': w_qkv, 'w_proj': w_proj, 'b_proj': b_proj}
    _L0_attn_all = _L0_attn_setup()
    _L0_attn_in = {k: v for k, v in _L0_attn_all.items() if k in ('w_qkv', 'w_proj', 'b_proj')}
    del _L0_attn_all

    def _L0_ffn_setup():
        import jax, jax.numpy as jnp
        import numpy as np
        E = 8
        K = 2
        D = 192
        F = 4 * D
        key = jax.random.key(seed)
        ks = jax.random.split(key, 10)
        s_exp = 0.02
        return {'x': jax.random.normal(ks[0], (4, 256, D), jnp.float32), 'W1': jax.random.normal(ks[1], (E, F, D), jnp.float32) * s_exp, 'b1': jax.random.normal(ks[2], (E, F), jnp.float32) * s_exp, 'W2': jax.random.normal(ks[3], (E, D, F), jnp.float32) * s_exp, 'b2': jax.random.normal(ks[4], (E, D), jnp.float32) * s_exp, 'Wr1': jax.random.normal(ks[5], (D, D), jnp.float32) * s_exp, 'br1': jax.random.normal(ks[6], (D,), jnp.float32) * s_exp, 'Wr2': jax.random.normal(ks[7], (E, D), jnp.float32) * s_exp, 'br2': jax.random.normal(ks[8], (E,), jnp.float32) * s_exp}
    _L0_ffn_all = _L0_ffn_setup()
    _L0_ffn_in = {k: v for k, v in _L0_ffn_all.items() if k in ('W1', 'b1', 'W2', 'b2', 'Wr1', 'br1', 'Wr2', 'br2')}
    del _L0_ffn_all
    return {'x': x, 'L0_tok_freq_bands': _L0_tok_in['freq_bands'], 'L0_tok_W': _L0_tok_in['W'], 'L0_attn_w_qkv': _L0_attn_in['w_qkv'], 'L0_attn_w_proj': _L0_attn_in['w_proj'], 'L0_attn_b_proj': _L0_attn_in['b_proj'], 'L0_ffn_W1': _L0_ffn_in['W1'], 'L0_ffn_b1': _L0_ffn_in['b1'], 'L0_ffn_W2': _L0_ffn_in['W2'], 'L0_ffn_b2': _L0_ffn_in['b2'], 'L0_ffn_Wr1': _L0_ffn_in['Wr1'], 'L0_ffn_br1': _L0_ffn_in['br1'], 'L0_ffn_Wr2': _L0_ffn_in['Wr2'], 'L0_ffn_br2': _L0_ffn_in['br2']}

def reference(x, L0_tok_freq_bands, L0_tok_W, L0_attn_w_qkv, L0_attn_w_proj, L0_attn_b_proj, L0_ffn_W1, L0_ffn_b1, L0_ffn_W2, L0_ffn_b2, L0_ffn_Wr1, L0_ffn_br1, L0_ffn_Wr2, L0_ffn_br2):
    import jax
    import jax.numpy as jnp

    def _L0_tok_ref(xyz, freq_bands, W):
        import jax, jax.numpy as jnp
        import numpy as np
        NUM_BANDS = 6
        D_MODEL = 192
        B, N = (2, 512)
        IN_FEATURES = 3 * NUM_BANDS * 2 * D_MODEL
        b, c, n, d = xyz.shape
        xb = 2.0 * jnp.pi * xyz[..., None] * freq_bands
        feat = jnp.concatenate([jnp.sin(xb), jnp.cos(xb)], axis=-1)
        feat = feat.reshape(b, n, -1)
        return jnp.einsum('bnf,of->bno', feat, W)

    def _L0_attn_ref(x, w_qkv, w_proj, b_proj):
        import jax, jax.numpy as jnp
        import numpy as np
        NUM_HEADS = 12
        OT_REG = 0.1
        SINKHORN_ITERS = 10
        DIAG_VAL = 1000.0

        def _sot(q):
            N = q.shape[-2]
            qn = q / (jnp.linalg.norm(q, axis=-1, keepdims=True) + 1e-08)
            C = 1.0 - jnp.einsum('bhnd,bhmd->bhnm', qn, qn)
            eye = jnp.eye(N, dtype=bool)
            C = jnp.where(eye, DIAG_VAL, C)
            log_K = -C / OT_REG
            log_marg = -jnp.log(jnp.float32(N))
            log_v = jnp.zeros(q.shape[:2] + (N,), dtype=q.dtype)
            for _ in range(SINKHORN_ITERS):
                log_u = log_marg - jax.nn.logsumexp(log_K + log_v[..., None, :], axis=-1)
                log_v = log_marg - jax.nn.logsumexp(log_K + log_u[..., :, None], axis=-2)
            log_T = log_u[..., :, None] + log_K + log_v[..., None, :]
            z = jnp.exp(log_T)
            z = z / jnp.max(z, axis=(-2, -1), keepdims=True)
            z = jnp.where(eye, 1.0, z)
            return z
        B, N, C = x.shape
        H = NUM_HEADS
        hd = C // H
        scale = hd ** (-0.5)
        qkv = jnp.einsum('bnc,oc->bno', x, w_qkv)
        qkv = qkv.reshape(B, N, 3, H, hd).transpose(2, 0, 3, 1, 4)
        q, k, v = (qkv[0], qkv[1], qkv[2])
        attn = _sot(q)
        attn = jax.nn.softmax(attn * scale, axis=-1)
        out = jnp.einsum('bhnm,bhmd->bhnd', attn, v)
        out = out.transpose(0, 2, 1, 3).reshape(B, N, C)
        out = jnp.einsum('bnc,oc->bno', out, w_proj) + b_proj
        return out

    def _L0_ffn_ref(x, W1, b1, W2, b2, Wr1, br1, Wr2, br2):
        import jax, jax.numpy as jnp
        import numpy as np
        E = 8
        K = 2
        D = 192
        F = 4 * D
        h = jax.nn.relu(jnp.einsum('bsd,hd->bsh', x, Wr1) + br1)
        score = jnp.einsum('bsd,ed->bse', h, Wr2) + br2
        _, idx = jax.lax.top_k(score, K)
        mask = (jax.nn.one_hot(idx, E) > 0).any(axis=-2)
        w = jax.nn.softmax(jnp.where(mask, score, -jnp.inf), axis=-1)
        out = jnp.zeros_like(x)
        for e in range(E):
            mid = jax.nn.relu(jnp.einsum('bsd,fd->bsf', x, W1[e]) + b1[e])
            ye = jnp.einsum('bsf,df->bsd', mid, W2[e]) + b2[e]
            out = out + w[..., e:e + 1] * ye
        return out
    h = _L0_tok_ref(x, L0_tok_freq_bands, L0_tok_W)
    h = _layernorm(h + _L0_attn_ref(h, L0_attn_w_qkv, L0_attn_w_proj, L0_attn_b_proj), axis=-1)
    h = _layernorm(h + _L0_ffn_ref(h, L0_ffn_W1, L0_ffn_b1, L0_ffn_W2, L0_ffn_b2, L0_ffn_Wr1, L0_ffn_br1, L0_ffn_Wr2, L0_ffn_br2), axis=-1)
    return h

_drawn_inputs = setup_inputs


def setup_inputs(seed=0):
    import zlib

    import numpy as np

    out = dict(_drawn_inputs(seed))
    spreads = {'L0_attn_b_proj': (0.0, 0.1)}
    factors = {'L0_ffn_b1': 8.0, 'L0_ffn_b2': 4.057, 'L0_ffn_br1': 3.119}
    for name, (base, spread) in spreads.items():
        noise = np.random.default_rng([zlib.crc32(name.encode()), seed]).standard_normal(out[name].shape)
        drawn = base * np.exp(spread * noise) if base else spread * noise
        out[name] = jnp.asarray(drawn.astype(out[name].dtype))
    for name, factor in factors.items():
        out[name] = (out[name] * factor).astype(out[name].dtype)
    return out
```

```python
from contextlib import ExitStack

import numpy as np

import concourse.bass as bass
from concourse import mybir

F32 = mybir.dt.float32
F16 = mybir.dt.float16
BF16 = mybir.dt.bfloat16
I32 = mybir.dt.int32
U32 = mybir.dt.uint32
ALU = mybir.AluOpType
ACT = mybir.ActivationFunctionType
AX_X = mybir.AxisListType.X
RMAX = bass.bass_isa.ReduceOp.max

P = 128
IMAGES, TOKENS, DIM, HEADS, BANDS = 16, 512, 192, 12, 6
HD = DIM // HEADS
EXPERTS, FFN = 8, 4 * DIM
PATCH = 3 * TOKENS * DIM // TOKENS
FULL = PATCH // P
TB = TOKENS // P
SLOTS = FULL + 1
CHUNKS = [(b, s) for b in range(BANDS) for s in range(FULL + b % 2)]
NCH = 2 * len(CHUNKS)
WIDE = SLOTS * TOKENS
Q_SCALE = 64.0
TURN = float(np.nextafter(np.float32(2 * np.pi), np.float32(0)))


class Done:

    def __init__(self, engine, sem):
        self.engine, self.sem, self.n = engine, sem, 0

    def __call__(self, instruction):
        self.n += 1
        instruction.then_inc(self.sem, 1)
        self.engine.wait_ge(self.sem, self.n)


def power_of_two_scale(vector, done, own, scale, unscale, tmp):
    done(vector.tensor_scalar(tmp.bitcast(I32), own.bitcast(I32), 0x7F800000, None, ALU.bitwise_and))
    done(vector.tensor_scalar(tmp, tmp, 1e-30, None, ALU.max))
    done(vector.tensor_scalar(unscale, tmp, 2.0 ** -13, None, ALU.mult))
    done(vector.reciprocal(scale, unscale))


def embed(nc, x, freqs, w, h):
    with ExitStack() as ctx:
        sb = lambda name, shape, dt: ctx.enter_context(nc.sbuf_tensor(name, shape, dt))
        sem = lambda name: ctx.enter_context(nc.semaphore(name))
        xt = sb("xt", [P, WIDE], F32)
        fr = sb("fr", [P, BANDS + BANDS // 2], F32)
        work = sb("work", [P, 8 * WIDE], F32)
        turns = [work[:, i * WIDE:(i + 1) * WIDE] for i in range(2)]
        absturns = [work[:, (2 + i) * WIDE:(3 + i) * WIDE] for i in range(2)]
        waves = [work[:, (4 + 2 * i) * WIDE:(6 + 2 * i) * WIDE].rearrange("p (t n) -> p t n", t=2) for i in range(2)]
        feat_h = [sb(f"feat_h{i}", [P, 2, WIDE], F16) for i in range(2)]
        feat_l = [sb(f"feat_l{i}", [P, 2, WIDE], F16) for i in range(2)]
        w_hl = sb("w_hl", [P, NCH, 2, DIM], F16)
        wabs = sb("wabs", [P, 1], F32)
        wmax = sb("wmax", [P, 1], F32)
        scale = sb("scale", [P, 1], F32)
        unscale = sb("unscale", [P, 1], F32)
        tmp = sb("tmp", [P, 1], F32)
        quarter = sb("quarter", [P, 1], F32)
        h_sb = sb("h_sb", [P, TB, DIM], F32)
        h_lo = sb("h_lo", [P, TB, DIM], F32)
        acc = [ctx.enter_context(nc.psum_tensor(f"acc{i}", [P, TB, 512], F32)) for i in range(2)]

        w_in, fr_in = sem("w_in"), sem("fr_in")
        x_in, x_used = sem("x_in"), sem("x_used")
        own, maxed, w_max_ready, w_ready, quarter_ready = (
            sem("own"), sem("maxed"), sem("w_max_ready"), sem("w_ready"), sem("quarter_ready"))
        angle_steps, halves_split = sem("angle_steps"), sem("halves_split")
        turns_ready = [sem(f"turns_ready{i}") for i in range(2)]
        waves_ready = [sem(f"waves_ready{i}") for i in range(2)]
        high_ready = [sem(f"high_ready{i}") for i in range(2)]
        low_ready = [sem(f"low_ready{i}") for i in range(2)]
        feat_used = [sem(f"feat_used{i}") for i in range(2)]
        h_ready, h_out = sem("h_ready"), sem("h_out")
        UNITS = BANDS // 2
        w_raw = work[:, 0:NCH * DIM]
        block = ctx.enter_context(nc.Block())

        @block.sync
        def _(sp):
            sp.dma_start(w_raw, w).then_inc(w_in, 16)
            sp.dma_start(fr[:, :], freqs).then_inc(fr_in, 16)
            with sp.Fori(0, IMAGES) as i:
                sp.wait_ge(angle_steps, i * (2 * BANDS))
                sp.dma_start(xt[:, :], x[bass.ds(i, 1), :, :].rearrange("a p n -> (a p) n")).then_inc(x_in, 16)
                sp.wait_ge(h_ready, i + 1)
                sp.dma_start(h[bass.ds(i, 1), :, :, :].rearrange("a p b d -> (a p) b d"), h_sb[:, :, :]).then_inc(h_out, 16)
            sp.wait_ge(h_out, 16 * IMAGES)

        @block.gpsimd
        def _(pool):
            pool.wait_ge(maxed, 1)
            nc.gpsimd.partition_all_reduce(wmax[:, :], wabs[:, :], P, RMAX).then_inc(w_max_ready, 1)

        @block.vector
        def _(dve):
            done = Done(dve, own)
            nc.vector.memset(quarter[:, :], float(np.pi / 2)).then_inc(quarter_ready, 1)
            dve.wait_ge(w_in, 16)
            nc.vector.tensor_reduce(wabs[:, :], w_raw, AX_X, ALU.max, apply_absolute_value=True).then_inc(maxed, 1)
            dve.wait_ge(w_max_ready, 1)
            power_of_two_scale(nc.vector, done, wmax[:, :], scale[:, :], unscale[:, :], tmp[:, :])
            raw = w_raw.rearrange("p (c d) -> p c d", c=NCH)
            done(nc.vector.tensor_scalar(w_hl[:, :, 0, :], raw, scale[:, 0:1], None, ALU.mult))
            done(nc.vector.scalar_tensor_tensor(w_hl[:, :, 1, :], raw, scale[:, 0:1], w_hl[:, :, 0, :],
                                                ALU.mult, ALU.subtract))
            nc.vector.memset(tmp[:, :], 0.0).then_inc(w_ready, 1)
            dve.wait_ge(fr_in, 16)

            def angles(i, b):
                n, last = b % 2, None
                parts = [(0, FULL * TOKENS, b)] + ([(FULL * TOKENS, WIDE, BANDS + b // 2)] if b % 2 else [])
                whole = absturns[n].bitcast(I32)
                if b == 0:
                    dve.wait_ge(x_in, (i + 1) * 16)
                dve.wait_ge(waves_ready[n], (i * UNITS + b // 2) * 2)
                for lo, hi, f in parts:
                    last = nc.vector.tensor_scalar(whole[:, lo:hi], xt[:, lo:hi], fr[:, f:f + 1], None, ALU.mult)
                last.then_inc(angle_steps, 1)
                dve.wait_ge(angle_steps, i * (2 * BANDS) + (2 * b + 1))
                for lo, hi, f in parts:
                    last = nc.vector.scalar_tensor_tensor(turns[n][:, lo:hi], xt[:, lo:hi], fr[:, f:f + 1],
                                                          whole[:, lo:hi], ALU.mult, ALU.subtract)
                last.then_inc(angle_steps, 1)
                dve.wait_ge(angle_steps, i * (2 * BANDS) + (2 * b + 2))
                hi = parts[-1][1]
                nc.vector.tensor_scalar(whole[:, 0:hi], turns[n].bitcast(I32)[:, 0:hi], 0x7FFFFFFF, None,
                                        ALU.bitwise_and).then_inc(turns_ready[n], 1)

            def low_parts(i, b):
                n, hi = b % 2, (FULL + b % 2) * TOKENS
                dve.wait_ge(high_ready[n], i * UNITS + (b // 2 + 1))
                dve.wait_ge(feat_used[n], i * UNITS + b // 2)
                nc.vector.tensor_tensor(feat_l[n][:, :, 0:hi], waves[n][:, :, 0:hi], feat_h[n][:, :, 0:hi],
                                        ALU.subtract).then_inc(low_ready[n], 1)

            with dve.Fori(0, IMAGES // 2) as pair:
                for a in range(2):
                    i = pair * 2 + a
                    for b in range(BANDS):
                        angles(i, b)
                        if b > 0:
                            low_parts(i, b - 1)
                    low_parts(i, BANDS - 1)
                    dve.wait_ge(feat_used[1], (i + 1) * UNITS)
                    dve.wait_ge(h_out, i * 16)
                    nc.vector.tensor_scalar(h_lo[:, :, :], acc[a][:, :, DIM:2 * DIM], unscale[:, 0:1], None,
                                            ALU.mult).then_inc(halves_split, 1)
                    dve.wait_ge(halves_split, i + 1)
                    nc.vector.scalar_tensor_tensor(h_sb[:, :, :], acc[a][:, :, 0:DIM], unscale[:, 0:1], h_lo[:, :, :],
                                                   ALU.mult, ALU.add).then_inc(h_ready, 1)

        @block.scalar
        def _(act):
            act.wait_ge(quarter_ready, 1)
            act.wait_ge(w_ready, 1)
            with act.Fori(0, IMAGES) as i:
                for b in range(BANDS):
                    n, hi = b % 2, (FULL + b % 2) * TOKENS
                    act.wait_ge(turns_ready[n], i * UNITS + (b // 2 + 1))
                    act.wait_ge(low_ready[n], i * UNITS + b // 2)
                    nc.scalar.activation(waves[n][:, 0, 0:hi], turns[n][:, 0:hi], ACT.Sin,
                                         scale=TURN).then_inc(waves_ready[n], 1)
                    nc.scalar.activation(waves[n][:, 1, 0:hi], absturns[n][:, 0:hi], ACT.Sin, bias=quarter[:, 0:1],
                                         scale=-TURN).then_inc(waves_ready[n], 1)
                    act.wait_ge(waves_ready[n], i * (2 * UNITS) + (2 * (b // 2) + 2))
                    act.wait_ge(feat_used[n], i * UNITS + b // 2)
                    nc.scalar.activation(feat_h[n][:, :, 0:hi], waves[n][:, :, 0:hi], ACT.Copy).then_inc(high_ready[n], 1)

        @block.tensor
        def _(pe):
            pe.wait_ge(w_ready, 1)
            with pe.Fori(0, IMAGES // 2) as pair:
                for a in range(2):
                    i = pair * 2 + a
                    pe.wait_ge(h_ready, i)
                    for b in range(BANDS):
                        n = b % 2
                        chunks = [(2 * k + t, s, t) for k, (band, s) in enumerate(CHUNKS) if band == b for t in range(2)]
                        pe.wait_ge(high_ready[n], i * UNITS + (b // 2 + 1))
                        for k, s, t in chunks:
                            for q in range(TB):
                                block_of = feat_h[n][:, t, s * TOKENS + q * P:s * TOKENS + (q + 1) * P]
                                nc.tensor.matmul(acc[a][:, q, 0:2 * DIM], block_of, w_hl[:, k, :, :].rearrange("p a d -> p (a d)"),
                                                 start=(k == 0), stop=False)
                        pe.wait_ge(low_ready[n], i * UNITS + (b // 2 + 1))
                        for k, s, t in chunks:
                            for q in range(TB):
                                block_of = feat_l[n][:, t, s * TOKENS + q * P:s * TOKENS + (q + 1) * P]
                                last = nc.tensor.matmul(acc[a][:, q, 0:DIM], block_of, w_hl[:, k, 0, :],
                                                        start=False, stop=(k == NCH - 1))
                        last.then_inc(feat_used[n], 1)


def project(nc, h, wq, wv, group_ones, ident, q_parts, v_parts):
    with ExitStack() as ctx:
        sb = lambda name, shape, dt: ctx.enter_context(nc.sbuf_tensor(name, shape, dt))
        ps = lambda name, shape, dt: ctx.enter_context(nc.psum_tensor(name, shape, dt))
        sem = lambda name: ctx.enter_context(nc.semaphore(name))
        REST, HALF = DIM - P, DIM // 2
        eye = sb("eye", [P, P], F32)
        wq_a, wq_b = sb("wq_a", [P, DIM], F32), sb("wq_b", [REST, DIM], F32)
        wv_a, wv_b = sb("wv_a", [P, DIM], F32), sb("wv_b", [REST, DIM], F32)
        ones = sb("ones", [HALF, HALF], F32)
        h_in_sb = [sb(f"h_in_sb{i}", [P, TB, DIM], F32) for i in range(2)]
        ht_a, ht_b = sb("ht_a", [P, TOKENS], F32), sb("ht_b", [REST, TOKENS], F32)
        squares = sb("squares", [HALF, 2, TOKENS], F32)
        norm = sb("norm", [HALF, 2, TOKENS], F32)
        inv = sb("inv", [HALF, 2, TOKENS], F32)
        qn = sb("qn", [HALF, 2, TOKENS], F32)
        q_hl = [sb(f"q_hl{i}", [HALF, 2, 2, TOKENS], F16) for i in range(2)]
        v_rest = sb("v_rest", [P, TB, HEADS, HD], F32)
        v_sb = [sb(f"v_sb{i}", [P, TB, HEADS, 3 * HD + 1], BF16) for i in range(2)]
        pt_a, pt_b = ps("pt_a", [P, TOKENS], F32), ps("pt_b", [REST, TOKENS], F32)
        pq = ps("pq", [HALF, 2, TOKENS], F32)
        psum_sq = ps("psum_sq", [HALF, 2, TOKENS], F32)
        pv = ps("pv", [P, TB, 256], F32)
        pv4 = pv[:, :, 0:DIM].rearrange("p b (h d) -> p b h d", h=HEADS)

        consts_in = sem("consts_in")
        h_in = [sem(f"h_in{i}") for i in range(2)]
        turned, ht_ready = sem("turned"), sem("ht_ready")
        q_ready, v_ready, squared, summed, rooted = (
            sem("q_ready"), sem("v_ready"), sem("squared"), sem("summed"), sem("rooted"))
        steps = sem("steps")
        v_high, ones_set = sem("v_high"), sem("ones_set")
        q_split, v_split = sem("q_split"), sem("v_split")
        out = [sem(f"out{i}") for i in range(2)]
        CONSTS = 6
        STEPS = 6
        block = ctx.enter_context(nc.Block())

        @block.sync
        def _(sp):
            for dst, src in ((eye, ident), (wq_a, wq[0:P, :]), (wq_b, wq[P:DIM, :]), (wv_a, wv[0:P, :]),
                             (wv_b, wv[P:DIM, :]), (ones, group_ones)):
                sp.dma_start(dst[:, :], src).then_inc(consts_in, 16)
            with sp.Fori(0, IMAGES // 2) as pair:
                for a in range(2):
                    i = pair * 2 + a
                    sp.wait_ge(turned, pair * 2)
                    sp.dma_start(h_in_sb[a][:, :, :], h[bass.ds(i, 1), :, :, :].rearrange("a p b d -> (a p) b d")).then_inc(h_in[a], 16)
                for a in range(2):
                    i = pair * 2 + a
                    sp.wait_ge(q_split, i + 1)
                    for part in range(2):
                        sp.dma_start(q_parts[bass.ds(i, 1), :, part, :, :].rearrange("a h p n -> p (a h) n"),
                                     q_hl[a][:, part, :, :]).then_inc(out[a], 16)
                    sp.wait_ge(v_split, i + 1)
                    sp.dma_start(v_parts[bass.ds(i, 1), :, :].rearrange("a p n -> (a p) n"),
                                 v_sb[a][:, :, :, :].rearrange("p b h d -> p (b h d)")).then_inc(out[a], 16)
            for a in range(2):
                sp.wait_ge(out[a], 48 * IMAGES // 2)

        @block.tensor
        def _(pe):
            pe.wait_ge(consts_in, 16 * CONSTS)
            with pe.Fori(0, IMAGES // 2) as pair:
                for a in range(2):
                    i = pair * 2 + a
                    pe.wait_ge(h_in[a], (pair + 1) * 16)
                    pe.wait_ge(ht_ready, i * 2)
                    for b in range(TB):
                        nc.tensor.transpose(pt_a[:, b * P:(b + 1) * P], h_in_sb[a][:, b, 0:P], eye[:, :])
                        last = nc.tensor.transpose(pt_b[:, b * P:(b + 1) * P], h_in_sb[a][:, b, P:DIM], eye[:, :])
                    last.then_inc(turned, 1)
                    pe.wait_ge(ht_ready, i * 2 + 2)
                    pe.wait_ge(q_split, i)
                    for half in range(2):
                        cols = slice(half * HALF, (half + 1) * HALF)
                        nc.tensor.matmul(pq[:, half, :], wq_a[:, cols], ht_a[:, :], start=True, stop=False)
                        last = nc.tensor.matmul(pq[:, half, :], wq_b[:, cols], ht_b[:, :], start=False, stop=True)
                    last.then_inc(q_ready, 1)
                    pe.wait_ge(v_split, i)
                    for b in range(TB):
                        rows = slice(b * P, (b + 1) * P)
                        nc.tensor.matmul(pv[:, b, 0:DIM], ht_a[:, rows], wv_a[:, :], start=True, stop=False)
                        last = nc.tensor.matmul(pv[:, b, 0:DIM], ht_b[:, rows], wv_b[:, :], start=False, stop=True)
                    last.then_inc(v_ready, 1)
                    pe.wait_ge(squared, i + 1)
                    for half in range(2):
                        last = nc.tensor.matmul(psum_sq[:, half, :], ones[:, :], squares[:, half, :], start=True, stop=True)
                    last.then_inc(summed, 1)

        @block.scalar
        def _(act):
            act.wait_ge(ones_set, 2)
            with act.Fori(0, IMAGES // 2) as pair:
                for a in range(2):
                    i = pair * 2 + a
                    act.wait_ge(turned, i + 1)
                    act.wait_ge(v_ready, i)
                    nc.scalar.activation(ht_a[:, :], pt_a[:, :], ACT.Copy).then_inc(ht_ready, 1)
                    nc.scalar.activation(ht_b[:, :], pt_b[:, :], ACT.Copy).then_inc(ht_ready, 1)
                    act.wait_ge(q_ready, i + 1)
                    act.wait_ge(summed, i)
                    nc.scalar.activation(squares[:, :, :], pq[:, :, :], ACT.Square).then_inc(squared, 1)
                    act.wait_ge(v_ready, i + 1)
                    act.wait_ge(out[a], pair * 48)
                    act.wait_ge(v_split, i)
                    nc.scalar.activation(v_sb[a][:, :, :, 0:HD], pv4, ACT.Copy).then_inc(v_high, 1)
                    act.wait_ge(summed, i + 1)
                    act.wait_ge(steps, i * STEPS)
                    nc.scalar.activation(norm[:, :, :], psum_sq[:, :, :], ACT.Sqrt).then_inc(rooted, 1)

        @block.vector
        def _(dve):
            for a in range(2):
                nc.vector.memset(v_sb[a][:, :, :, 3 * HD:3 * HD + 1], 1.0).then_inc(ones_set, 1)
            with dve.Fori(0, IMAGES // 2) as pair:
                for a in range(2):
                    i = pair * 2 + a

                    def step(k, instruction):
                        instruction.then_inc(steps, 1)
                        dve.wait_ge(steps, i * STEPS + k)

                    dve.wait_ge(rooted, i + 1)
                    step(1, nc.vector.tensor_scalar(norm[:, :, :], norm[:, :, :], 1e-8, None, ALU.add))
                    step(2, nc.vector.reciprocal(inv[:, :, :], norm[:, :, :]))
                    step(3, nc.vector.scalar_tensor_tensor(qn[:, :, :], pq[:, :, :], Q_SCALE, inv[:, :, :], ALU.mult, ALU.mult))
                    dve.wait_ge(out[a], pair * 48)
                    step(4, nc.vector.tensor_copy(q_hl[a][:, 0, :, :], qn[:, :, :]))
                    nc.vector.tensor_tensor(q_hl[a][:, 1, :, :], qn[:, :, :], q_hl[a][:, 0, :, :],
                                            ALU.subtract).then_inc(q_split, 1)
                    dve.wait_ge(v_high, i + 1)
                    step(5, nc.vector.tensor_tensor(v_rest[:, :, :, :], pv4, v_sb[a][:, :, :, 0:HD], ALU.subtract))
                    step(6, nc.vector.tensor_copy(v_sb[a][:, :, :, HD:2 * HD], v_rest[:, :, :, :]))
                    nc.vector.tensor_tensor(v_sb[a][:, :, :, 2 * HD:3 * HD], v_rest[:, :, :, :], v_sb[a][:, :, :, HD:2 * HD],
                                            ALU.subtract).then_inc(v_split, 1)

UH = HEADS // 2
GH = UH // 2
REG, ITERS = 0.1, 10
STEPS_X = 2 * ITERS - 1
K_SHIFT = float(15 * np.log(2))
HIDE = -60000.0
ATT_SCALE = HD ** -0.5
VW = 3 * HD + 1


def attend(nc, q_parts, v_parts, ident, att):
    with ExitStack() as ctx:
        sb = lambda name, shape, dt: ctx.enter_context(nc.sbuf_tensor(name, shape, dt))
        ps = lambda name, shape, dt: ctx.enter_context(nc.psum_tensor(name, shape, dt))
        sem = lambda name: ctx.enter_context(nc.semaphore(name))
        eye = sb("eye3", [P, P], F32)
        eye_h, eye_hide = sb("eye_h", [P, P], F16), sb("eye_hide", [P, P], F16)
        eye_bf = sb("eye_bf", [P, P], BF16)
        XR = UH * TB * 3
        pick = sb("pick3", [XR, UH * TB, P], BF16)
        xt_sb = sb("xt_sb", [XR, P], BF16)
        lift = sb("lift", [P, 2, P], F16)
        ones = sb("ones3", [P, P], BF16)
        k_bias, p_bias = sb("k_bias", [P, 1], F32), sb("p_bias", [P, 1], F32)
        q_left = [sb(f"q_left{s}", [P, UH, TOKENS], F16) for s in range(2)]
        q_right = [sb(f"q_right{s}", [P, UH, TOKENS], F16) for s in range(2)]
        v_sb = [sb(f"v_in_sb{s}", [P, TB, UH, VW], BF16) for s in range(2)]
        k_h = [sb(f"k_h{s}", [P, UH, TB * TOKENS], F16) for s in range(2)]
        k_l = [sb(f"k_l{s}", [P, UH, TB * TOKENS], F16) for s in range(2)]
        row_sums = [sb(f"row_sums{s}", [P, UH * TB], F32) for s in range(2)]
        x_sb = [sb(f"x_sb{s}", [P, UH * TB, 3], BF16) for s in range(2)]
        v_last = [sb(f"v_last{s}", [P, UH * TB], F32) for s in range(2)]
        k_new = sb("k_new", [P, TB, TOKENS], F32)
        plan = sb("plan", [P, TB, TOKENS], F32)
        probs = sb("probs", [P, TB, TOKENS], F32)
        p_h, p_l = sb("p_h", [P, TB, TOKENS], F16), sb("p_l", [P, TB, TOKENS], F16)
        sums = [sb(f"sums{g}", [P, GH * TB], F32) for g in range(2)]
        recs = [sb(f"recs{g}", [P, GH * TB], F32) for g in range(2)]
        rest = [sb(f"rest{g}", [P, GH * TB], F32) for g in range(2)]
        idle, idle_pool = sb("idle", [P, 1], F32), sb("idle_pool", [P, 3], F32)
        row_max, weighted = sb("row_max", [P, TB], F32), sb("weighted", [P, TB], F32)
        head_max, all_max, inv_max = sb("head_max", [P, 1], F32), sb("all_max", [P, 1], F32), sb("inv_max", [P, 1], F32)
        p_scale = sb("p_scale", [P, TB], F32)
        num, den = sb("num", [P, TB, HD], F32), sb("den", [P, TB, 1], F32)
        att_sb = [sb(f"att_sb{s}", [P, TB, UH, HD], F32) for s in range(2)]
        kx = [ps(f"kx{g}", [P, GH * TB, 3], F32) for g in range(2)]
        cos = ps("cos", [P, 2, TOKENS], F32)
        u_rows = ps("u_rows", [P, TOKENS], F32)
        xt_ps = ps("xt_ps", [XR, P], F32)
        pv = ps("pv3", [P, TB, VW], F32)

        eye_in, consts, ones_set = sem("eye_in"), sem("consts"), sem("ones3_set")
        q_in = [sem(f"q_in{s}") for s in range(2)]
        v_in = [sem(f"v_in{s}") for s in range(2)]
        att_out = [sem(f"att_out{s}") for s in range(2)]
        kx_ready = [sem(f"kx_ready{g}") for g in range(2)]
        x_ready = [sem(f"x_ready{g}") for g in range(2)]
        sum_steps = [sem(f"sum_steps{g}") for g in range(2)]
        x_steps = [sem(f"x_steps{g}") for g in range(2)]
        cos_ready, k_exp, k_high, k_built = sem("cos_ready"), sem("k_exp"), sem("k_high"), sem("k_built")
        pick_steps, x_turned, xt_ready = sem("pick_steps"), sem("x_turned3"), sem("xt_ready3")
        u_rows_ready, k_joined = sem("u_rows_ready"), sem("k_joined")
        plan_ready, weighed, head_max_ready, all_max_ready = (
            sem("plan_ready"), sem("weighed"), sem("head_max_ready"), sem("all_max_ready"))
        inv_ready, scale_ready, p_exp, p_high, p_ready = (
            sem("inv_ready"), sem("scale_ready"), sem("p_exp"), sem("p_high"), sem("p_ready"))
        pv_ready, summed_up, att_ready = sem("pv_ready"), sem("summed_up"), sem("att_ready")
        block = ctx.enter_context(nc.Block())

        def units(eng, head, last=None, first=None):
            with eng.Fori(0, UH) as k:
                head(None, None, (0, 0, 0), k)
            if first:
                first()

            def unit(n, f, b):
                with eng.Fori(0, UH) as k:
                    head(n, f, b, k)
                if last:
                    last(n, b)

            unit((0, 0, 0), None, (1, 1, 0))
            with eng.Fori(0, IMAGES - 1) as t:
                unit((t * 2 + 1, 1, t), (t * 2, 0, t), (t * 2 + 2, 0, t + 1))
                unit((t * 2 + 2, 0, t + 1), (t * 2 + 1, 1, t), (t * 2 + 3, 1, t + 1))
            unit((2 * IMAGES - 1, 1, IMAGES - 1), (2 * IMAGES - 2, 0, IMAGES - 1), None)
            with eng.Fori(0, UH) as k:
                head(None, (2 * IMAGES - 1, 1, IMAGES - 1), None, k)

        @block.sync
        def _(sp):
            sp.dma_start(eye[:, :], ident).then_inc(eye_in, 16)

            def load_q(image, s):
                for g in range(4):
                    for dst, part in ((q_left, g // 2), (q_right, g % 2)):
                        sp.dma_start(dst[s][32 * g:32 * g + HD, :, :],
                                     q_parts[bass.ds(image, 1), s, part, :, :].rearrange("a (k d) n -> d (a k) n", d=HD)).then_inc(q_in[s], 16)

            def load_v(image, s):
                src = v_parts[bass.ds(image, 1), :, :].rearrange("a p (b h w) -> (a p) b h w", b=TB, h=HEADS)
                sp.dma_start(v_sb[s][:, :, :, :], src[:, :, s * UH:(s + 1) * UH, :]).then_inc(v_in[s], 16)

            def store(image, s):
                dst = att[bass.ds(image, 1), :, :, :].rearrange("a p b (s n) -> (a p) b s n", s=2)[:, :, s, :]
                sp.dma_start(dst, att_sb[s][:, :, :, :].rearrange("p b h d -> p b (h d)")).then_inc(att_out[s], 16)

            sp.wait_ge(ones_set, 1)
            load_q(0, 0)
            load_q(0, 1)
            load_v(0, 0)
            sp.wait_ge(cos_ready, 2 * UH)
            load_q(1, 0)
            sp.wait_ge(cos_ready, 2 * UH * 2)
            load_q(1, 1)
            load_v(0, 1)
            with sp.Fori(0, IMAGES - 2) as t:
                for s in range(2):
                    u = t * 2 + s
                    sp.wait_ge(att_ready, (u + 1) * UH)
                    store(t, s)
                    sp.wait_ge(cos_ready, (u + 3) * (2 * UH))
                    load_q(t + 2, s)
                    sp.wait_ge(pv_ready, (u + 1) * UH)
                    load_v(t + 1, s)
            for t, s in ((IMAGES - 2, 0), (IMAGES - 2, 1), (IMAGES - 1, 0), (IMAGES - 1, 1)):
                sp.wait_ge(att_ready, (2 * t + s + 1) * UH)
                store(t, s)
                if t == IMAGES - 2:
                    load_v(t + 1, s)
            for s in range(2):
                sp.wait_ge(att_out[s], 16 * IMAGES)

        @block.gpsimd
        def _(pool):
            nc.gpsimd.memset(pick[:, :, :], 1.0).then_inc(pick_steps, 1)
            pool.wait_ge(pick_steps, 1)
            nc.gpsimd.affine_select(out=pick[:, :, :], in_=pick[:, :, :], compare_op=ALU.is_ge, fill=0.0, base=0,
                                    pattern=[[-3, UH * TB], [0, P]], channel_multiplier=1).then_inc(pick_steps, 1)
            pool.wait_ge(pick_steps, 2)
            nc.gpsimd.affine_select(out=pick[:, :, :], in_=pick[:, :, :], compare_op=ALU.is_ge, fill=0.0, base=2,
                                    pattern=[[3, UH * TB], [0, P]], channel_multiplier=-1).then_inc(pick_steps, 1)
            pool.wait_ge(consts, 7)

            def head(n, f, b, k):
                if f:
                    F = f[0] * UH + k
                    pool.wait_ge(p_exp, F * TB)
                    nc.gpsimd.tensor_tensor(idle_pool[:, 0:1], k_bias[:, :], k_bias[:, :], ALU.add)
                    nc.gpsimd.tensor_tensor(plan[:, :, :].rearrange("p b n -> p (b n)"),
                                            k_h[f[1]][:, bass.ds(k, 1), :].rearrange("p a n -> p (a n)"),
                                            k_l[f[1]][:, bass.ds(k, 1), :].rearrange("p a n -> p (a n)"), ALU.add).then_inc(k_joined, 1)
                    pool.wait_ge(head_max_ready, F + 1)
                    nc.gpsimd.tensor_tensor(idle_pool[:, 1:2], k_bias[:, :], k_bias[:, :], ALU.add)
                    nc.gpsimd.partition_all_reduce(all_max[:, :], head_max[:, :], P, RMAX).then_inc(all_max_ready, 1)
                if b:
                    pool.wait_ge(k_high, b[0] * UH + k + 1)
                    nc.gpsimd.tensor_tensor(idle_pool[:, 2:3], k_bias[:, :], k_bias[:, :], ALU.add)
                    nc.gpsimd.tensor_tensor(k_l[b[1]][:, bass.ds(k, 1), :].rearrange("p a n -> p (a n)"),
                                            k_new[:, :, :].rearrange("p b n -> p (b n)"),
                                            k_h[b[1]][:, bass.ds(k, 1), :].rearrange("p a n -> p (a n)"), ALU.subtract).then_inc(k_built, 1)

            units(pool, head)

        @block.tensor
        def _(pe):
            pe.wait_ge(consts, 7)
            pe.wait_ge(pick_steps, 3)

            def product(n, g, m, first=False):
                pe.wait_ge(x_ready[g], n[0] * STEPS_X + m)
                if first:
                    pe.wait_ge(sum_steps[g], n[0] * STEPS_X + (m - 1))
                for h in range(g * GH, (g + 1) * GH):
                    for i in range(TB):
                        out = kx[g][:, (h - g * GH) * TB + i, :]
                        for j in range(TB):
                            cols = slice(j * TOKENS + i * P, j * TOKENS + (i + 1) * P)
                            x = x_sb[n[1]][:, h * TB + j, :]
                            nc.tensor.matmul(out, k_h[n[1]][:, h, cols], x, start=(j == 0), stop=False)
                            last = nc.tensor.matmul(out, k_l[n[1]][:, h, cols], x, start=False, stop=(j == TB - 1))
                last.then_inc(kx_ready[g], 1)

            def cosines(b, k, half):
                G = b[0] * UH + k
                if half == 0:
                    pe.wait_ge(q_in[b[1]], (b[2] + 1) * (8 * 16))
                pe.wait_ge(k_exp, G * TB + 2 * half)
                for c in (2 * half, 2 * half + 1):
                    nc.tensor.matmul(cos[:, c % 2, :], q_left[b[1]][:, bass.ds(k, 1), c * P:(c + 1) * P].rearrange("p a n -> p (a n)"),
                                     q_right[b[1]][:, bass.ds(k, 1), :].rearrange("p a n -> p (a n)"), start=True, stop=False)
                    last = nc.tensor.matmul(cos[:, c % 2, c * P:(c + 1) * P], eye_h[:, :], eye_hide[:, :], start=False, stop=True)
                last.then_inc(cos_ready, 1)

            def u_to_rows(f, k):
                F = f[0] * UH + k
                pe.wait_ge(xt_ready, f[0] + 1)
                pe.wait_ge(plan_ready, F)
                for c in range(TB):
                    last = nc.tensor.matmul(u_rows[:, c * P:(c + 1) * P],
                                            pick[:, bass.ds(k * TB + c, 1), :].rearrange("p a n -> p (a n)"), xt_sb[:, :],
                                            start=True, stop=True)
                last.then_inc(u_rows_ready, 1)

            def times_v(f, k):
                F = f[0] * UH + k
                pe.wait_ge(p_ready, F * 2 + 2)
                pe.wait_ge(v_in[f[1]], (f[2] + 1) * 16)
                pe.wait_ge(att_ready, F)
                for i in range(TB):
                    for j in range(TB):
                        v = v_sb[f[1]][:, j, bass.ds(k, 1), :].rearrange("p a n -> p (a n)")
                        nc.tensor.matmul(pv[:, i, :], p_h[:, j, i * P:(i + 1) * P], v, start=(j == 0), stop=False)
                        nc.tensor.matmul(pv[:, i, :], p_l[:, j, i * P:(i + 1) * P], v, start=False, stop=False)
                    v = v_sb[f[1]][:, i, bass.ds(k, 1), :].rearrange("p a n -> p (a n)")
                    nc.tensor.matmul(pv[:, i, :], lift[:, 0, :], v, start=False, stop=False)
                    last = nc.tensor.matmul(pv[:, i, :], lift[:, 1, :], v, start=False, stop=True)
                last.then_inc(pv_ready, 1)

            def head(n, f, b, k):
                if f:
                    u_to_rows(f, k)
                if n:
                    product(n, 0, k * 3 + 1, True)
                if b:
                    cosines(b, k, 0)
                if n:
                    product(n, 1, k * 3 + 1, True)
                if b:
                    cosines(b, k, 1)
                if n:
                    for m in (2, 3):
                        for g in range(2):
                            product(n, g, k * 3 + m)
                if f:
                    times_v(f, k)

            def last(n, b):
                product(n, 0, STEPS_X)
                pe.wait_ge(xt_ready, n[0])
                pe.wait_ge(x_ready[1], (n[0] + 1) * STEPS_X)
                nc.tensor.matmul(xt_ps[:, :], x_sb[n[1]][:, :, :].rearrange("p c w -> p (c w)"), eye_bf[:, :],
                                 start=True, stop=True).then_inc(x_turned, 1)
                product(n, 1, STEPS_X)

            units(pe, head, last)

        @block.scalar
        def _(act):
            act.wait_ge(consts, 7)

            def head(n, f, b, k):
                if b:
                    G = b[0] * UH + k
                    act.wait_ge(k_built, G)
                    for c in range(TB):
                        if c % 2 == 0:
                            act.wait_ge(cos_ready, G * 2 + (c // 2 + 1))
                        nc.scalar.activation(k_new[:, c, :], cos[:, c % 2, :], ACT.Exp, bias=k_bias[:, 0:1],
                                             scale=1.0 / (REG * Q_SCALE ** 2),
                                             accum_out=row_sums[b[1]][:, bass.ds(k * TB + c, 1)]).then_inc(k_exp, 1)
                    act.wait_ge(k_exp, (G + 1) * TB)
                    if f:
                        act.wait_ge(k_joined, f[0] * UH + k + 1)
                    nc.scalar.activation(k_h[b[1]][:, bass.ds(k, 1), :].rearrange("p a n -> p (a n)"),
                                         k_new[:, :, :].rearrange("p b n -> p (b n)"), ACT.Copy).then_inc(k_high, 1)
                if f:
                    F = f[0] * UH + k
                    act.wait_ge(scale_ready, F + 1)
                    act.wait_ge(p_ready, F * 2)
                    act.wait_ge(pv_ready, F)
                    for half in range(2):
                        for c in (2 * half, 2 * half + 1):
                            nc.scalar.activation(probs[:, c, :], plan[:, c, :], ACT.Exp, bias=p_bias[:, 0:1],
                                                 scale=p_scale[:, c:c + 1]).then_inc(p_exp, 1)
                        act.wait_ge(p_exp, F * TB + (2 * half + 2))
                        c = slice(2 * half, 2 * half + 2)
                        nc.scalar.activation(p_h[:, c, :], probs[:, c, :], ACT.Copy).then_inc(p_high, 1)

            def last(n, b):
                act.wait_ge(x_turned, n[0] + 1)
                act.wait_ge(u_rows_ready, n[0] * UH)
                nc.scalar.activation(xt_sb[:, :], xt_ps[:, :], ACT.Copy).then_inc(xt_ready, 1)

            units(act, head, last)

        @block.vector
        def _(dve):
            for s in range(2):
                nc.vector.memset(q_left[s][:, :, :], 0.0)
                nc.vector.memset(q_right[s][:, :, :], 0.0)
            nc.vector.memset(ones[:, :], 1.0).then_inc(ones_set, 1)
            nc.vector.memset(k_bias[:, :], K_SHIFT - 1.0 / REG).then_inc(consts, 1)
            nc.vector.memset(p_bias[:, :], -ATT_SCALE).then_inc(consts, 1)
            dve.wait_ge(eye_in, 16)
            on_diag = float(1.0 - np.exp(-ATT_SCALE))
            on_diag_h = float(np.float16(on_diag))
            nc.vector.tensor_copy(eye_h[:, :], eye[:, :]).then_inc(consts, 1)
            nc.vector.tensor_copy(eye_bf[:, :], eye[:, :]).then_inc(consts, 1)
            nc.vector.tensor_scalar(eye_hide[:, :], eye[:, :], HIDE, None, ALU.mult).then_inc(consts, 1)
            nc.vector.tensor_scalar(lift[:, 0, :], eye[:, :], on_diag_h, None, ALU.mult).then_inc(consts, 1)
            nc.vector.tensor_scalar(lift[:, 1, :], eye[:, :], on_diag - on_diag_h, None, ALU.mult).then_inc(consts, 1)
            dve.wait_ge(consts, 7)

            def next_x(n, g, m, source, keep=True):
                cols = slice(g * GH * TB, (g + 1) * GH * TB)
                if not keep:
                    nc.vector.reciprocal(v_last[n[1]][:, cols], source)
                    return
                base = n[0] * (4 * STEPS_X) + (m * 4)
                x = x_sb[n[1]]
                nc.vector.reciprocal(recs[g][:, :], source).then_inc(x_steps[g], 1)
                with nc.allow_low_precision("the leading part of three"):
                    nc.vector.reciprocal(x[:, cols, 0], source).then_inc(x_steps[g], 1)
                dve.wait_ge(x_steps[g], base + 2)
                nc.vector.tensor_tensor(x[:, cols, 1], recs[g][:, :], x[:, cols, 0], ALU.subtract).then_inc(x_steps[g], 1)
                nc.vector.tensor_tensor(rest[g][:, :], recs[g][:, :], x[:, cols, 0], ALU.subtract).then_inc(x_steps[g], 1)
                dve.wait_ge(x_steps[g], base + 4)
                nc.vector.tensor_tensor(x[:, cols, 2], rest[g][:, :], x[:, cols, 1], ALU.subtract).then_inc(x_ready[g], 1)

            def turn(n, g, m, keep=True):
                done = n[0] * STEPS_X + m
                dve.wait_ge(kx_ready[g], done)
                nc.vector.tensor_reduce(sums[g][:, :], kx[g][:, :, :], AX_X, ALU.add).then_inc(sum_steps[g], 1)
                dve.wait_ge(sum_steps[g], done)
                next_x(n, g, m, sums[g][:, :], keep)

            def first_x(n):
                dve.wait_ge(k_built, (n[0] + 1) * UH)
                for g in range(2):
                    next_x(n, g, 0, row_sums[n[1]][:, g * GH * TB:(g + 1) * GH * TB])

            def times_u(f, k, chunks):
                F = f[0] * UH + k
                if chunks[0] == 0:
                    dve.wait_ge(k_joined, F + 1)
                    dve.wait_ge(u_rows_ready, F + 1)
                    nc.vector.memset(idle[:, :], 0.0)
                for c in chunks:
                    last = nc.vector.tensor_tensor_reduce(plan[:, c, :], plan[:, c, :], u_rows[:, :], 1.0, 0.0,
                                                          ALU.mult, ALU.max, row_max[:, c:c + 1])
                if c == TB - 1:
                    last.then_inc(plan_ready, 1)
                    dve.wait_ge(plan_ready, F + 1)
                    nc.vector.tensor_tensor(weighted[:, :], row_max[:, :], v_last[f[1]][:, bass.ds(k * TB, TB)], ALU.mult).then_inc(weighed, 1)
                    dve.wait_ge(weighed, F + 1)
                    nc.vector.tensor_reduce(head_max[:, :], weighted[:, :], AX_X, ALU.max).then_inc(head_max_ready, 1)

            def scale_plan(f, k):
                F = f[0] * UH + k
                dve.wait_ge(all_max_ready, F + 1)
                nc.vector.reciprocal(inv_max[:, :], all_max[:, :]).then_inc(inv_ready, 1)
                dve.wait_ge(inv_ready, F + 1)
                dve.wait_ge(p_exp, F * TB)
                nc.vector.tensor_scalar(p_scale[:, :], v_last[f[1]][:, bass.ds(k * TB, TB)], ATT_SCALE, inv_max[:, 0:1],
                                        ALU.mult, ALU.mult).then_inc(scale_ready, 1)

            def p_low_part(f, k, half):
                dve.wait_ge(p_high, f[0] * (2 * UH) + k * 2 + (half + 1))
                if half == 0:
                    dve.wait_ge(pv_ready, f[0] * UH + k)
                c = slice(half * TB // 2, (half + 1) * TB // 2)
                nc.vector.tensor_tensor(p_l[:, c, :], probs[:, c, :], p_h[:, c, :], ALU.subtract).then_inc(p_ready, 1)

            def normalise(f, k):
                F = f[0] * UH + k
                dve.wait_ge(pv_ready, F + 1)
                nc.vector.tensor_reduce(num[:, :, :], pv[:, :, 0:3 * HD].rearrange("p b (w d) -> p b d w", w=3), AX_X,
                                        ALU.add).then_inc(summed_up, 1)
                nc.vector.reciprocal(den[:, :, :], pv[:, :, 3 * HD:VW]).then_inc(summed_up, 1)
                dve.wait_ge(summed_up, F * 2 + 2)
                dve.wait_ge(att_out[f[1]], f[2] * 16)
                nc.vector.tensor_tensor(att_sb[f[1]][:, :, bass.ds(k, 1), :].rearrange("p b a d -> p b (a d)"), num[:, :, :],
                                        den[:, :, :].to_broadcast([P, TB, HD]), ALU.mult).then_inc(att_ready, 1)

            def head(n, f, b, k):
                if f:
                    times_u(f, k, (0, 1))
                if n:
                    turn(n, 0, k * 3 + 1)
                if f:
                    times_u(f, k, (2, 3))
                if n:
                    turn(n, 1, k * 3 + 1)
                if f:
                    scale_plan(f, k)
                if n:
                    turn(n, 0, k * 3 + 2)
                    turn(n, 1, k * 3 + 2)
                if f:
                    p_low_part(f, k, 0)
                if n:
                    turn(n, 0, k * 3 + 3)
                if f:
                    p_low_part(f, k, 1)
                if n:
                    turn(n, 1, k * 3 + 3)
                if f:
                    normalise(f, k)

            def last(n, b):
                if b:
                    first_x(b)
                for g in range(2):
                    turn(n, g, STEPS_X, keep=False)

            units(dve, head, last, lambda: first_x((0, 0)))

FB = FFN // P
LN_EPS = 1e-5


def mix(nc, h, att, ident, w):
    with ExitStack() as ctx:
        sb = lambda name, shape, dt: ctx.enter_context(nc.sbuf_tensor(name, shape, dt))
        ps = lambda name, shape, dt: ctx.enter_context(nc.psum_tensor(name, shape, dt))
        sem = lambda name: ctx.enter_context(nc.semaphore(name))
        REST, HALF = DIM - P, DIM // 2
        raw = sb("raw", [P, EXPERTS * FB * DIM], F32)
        raw1_a = raw[:, 0:EXPERTS * FFN].rearrange("p (e f) -> p e f", e=EXPERTS)
        raw2 = raw[:, :].rearrange("p (e d) -> p e d", d=DIM)
        raw1_b = sb("raw1_b", [P, EXPERTS, FFN], F32)
        w1 = sb("w1", [P, EXPERTS, 3, FFN], F16)
        w2 = sb("w2", [P, EXPERTS * FB, 2, DIM], F16)
        maxes, all_maxes = sb("maxes", [P, 3], F32), sb("all_maxes", [P, 3], F32)
        scale, unscale, tmp = sb("scale4", [P, 2], F32), sb("unscale4", [P, 2], F32), sb("tmp4", [P, 2], F32)
        small = {}
        for name, src in w["small"].items():
            small[name] = sb("c_" + name, list(src.shape), F32)
        eye = sb("eye4", [P, P], F32)
        eps, idle = sb("eps", [P, 1], F32), sb("idle4", [P, 1], F32)
        h_sb, att_sb = sb("h_sb4", [P, TB, DIM], F32), sb("att_sb4", [P, TB, DIM], F32)
        at_a, at_b = sb("at_a", [P, TOKENS], F32), sb("at_b", [REST, TOKENS], F32)
        z = sb("z", [P, TB, DIM], F32)
        stats, mean_var = sb("stats", [P, TB, 6], F32), sb("mean_var", [P, TB, 2], F32)
        std, inv_std = sb("std", [P, TB], F32), sb("inv_std", [P, TB], F32)
        x = sb("x4", [P, TB, 2 * P], F32)
        xt_a, xt_m = sb("xt_a", [P, TOKENS], F32), sb("xt_m", [P, TOKENS], F32)
        xh_a = [sb(f"xh_a{a}", [P, TOKENS], F16) for a in range(2)]
        xl_a = [sb(f"xl_a{a}", [P, TOKENS], F16) for a in range(2)]
        xh_m = [sb(f"xh_m{a}", [P, TOKENS], F16) for a in range(2)]
        xl_m = [sb(f"xl_m{a}", [REST, TOKENS], F16) for a in range(2)]
        hidden = sb("hidden", [HALF, 2, TOKENS], F32)
        score = sb("score", [P, TB, EXPERTS], F32)
        best, where = sb("best", [P, TB, 8], F32), sb("where", [P, TB, 8], U32)
        pick = sb("pick", [P, TB, 2], F32)
        gap, ratio, total = sb("gap", [P, TB], F32), sb("ratio", [P, TB], F32), sb("total", [P, TB], F32)
        share = sb("share", [P, 2, TB], F32)
        route, route2 = sb("route", [P, TB, EXPERTS], F32), sb("route2", [P, TB, EXPERTS], F32)
        route_t = sb("route_t", [EXPERTS, TOKENS], F32)
        gate = [sb(f"gate{a}", [P, TB, EXPERTS], F32) for a in range(2)]
        acc = [sb(f"acc4{a}", [P, TB, DIM], F32) for a in range(2)]
        mid = [sb(f"mid{a}", [P, TOKENS], F32) for a in range(2)]
        mid_h = [sb(f"mid_h{a}", [P, TOKENS], F16) for a in range(2)]
        mid_l = [sb(f"mid_l{a}", [P, TOKENS], F16) for a in range(2)]
        stats2, mean_var2 = sb("stats2", [P, TB, 6], F32), sb("mean_var2", [P, TB, 2], F32)
        std2, inv_std2 = sb("std2", [P, TB], F32), sb("inv_std2", [P, TB], F32)
        out_sb = sb("out_sb", [P, TB, DIM], F32)
        up_ps = [ps(f"up_ps{a}", [P, TOKENS], F32) for a in range(2)]
        down = ps("down", [P, TB, 512], F32)
        misc = ps("misc", [P, 2, 512], F32)
        rows4 = misc[:, :, :].rearrange("p a (b n) -> p (a b) n", b=2)[:, :, 0:DIM]

        raw_in, maxed, all_maxed, own, w_ready, eps_set = (
            sem("raw_in"), sem("maxed4"), sem("all_maxed"), sem("own4"), sem("w_ready4"), sem("eps_set"))
        small_in, w1_split, raw2_in = sem("small_in"), sem("w1_split"), sem("raw2_in")
        h_in, att_in, out_done = sem("h_in4"), sem("att_in4"), sem("out_done")
        turned, turned_read = sem("turned4"), sem("turned_read")
        projected, z_steps, z_ready, std_ready = sem("projected"), sem("z_steps"), sem("z_ready"), sem("std_ready")
        x_steps, x_ready = sem("x_steps4"), sem("x_ready4")
        x_turned, xt_ready, x_split = sem("x_turned"), sem("xt_ready"), sem("x_split")
        hidden_up, hidden_ready, scored, score_steps, gap_ready, ratio_ready = (
            sem("hidden_up"), sem("hidden_ready"), sem("scored"), sem("score_steps"), sem("gap_ready"), sem("ratio_ready"))
        route_steps, route_ready, route_turned, route_t_ready, biased, acc_ready = (
            sem("route_steps"), sem("route_ready"), sem("route_turned"), sem("route_t_ready"), sem("biased"), sem("acc_ready"))
        down_ready = sem("down_ready")
        acc_steps, end_steps, end_var, end_std, out_ready = (
            sem("acc_steps"), sem("end_steps"), sem("end_var"), sem("end_std"), sem("out_ready"))
        by_turns = lambda name: [sem(f"{name}{a}") for a in range(2)]
        up_ready, mid_ready, mid_high, mid_split, mid_used = (
            by_turns("up_ready"), by_turns("mid_ready"), by_turns("mid_high"), by_turns("mid_split"), by_turns("mid_used"))
        NB = EXPERTS * FB
        block = ctx.enter_context(nc.Block())

        def images(eng, step, front, end=None):
            for t in sorted(front):
                front[t](0, 0)

            def image(i, a, ahead):
                for t in range(NB):
                    step(i, a, t)
                    if ahead and t in front:
                        front[t](i + 1, 1 - a)
                if end:
                    end(i, a)

            with eng.Fori(0, IMAGES // 2 - 1) as pair:
                for a in range(2):
                    image(pair * 2 + a, a, True)
            image(IMAGES - 2, 0, True)
            image(IMAGES - 1, 1, False)

        @block.sync
        def _(sp):
            sp.dma_start(raw[:, 0:EXPERTS * FFN], w["w1_a"]).then_inc(raw_in, 16)
            sp.dma_start(raw1_b[:, :, :].rearrange("p a b -> p (a b)"), w["w1_b"]).then_inc(raw_in, 16)
            for name, src in w["small"].items():
                sp.dma_start(small[name][:, :] if len(src.shape) == 2 else small[name][:, :, :], src).then_inc(small_in, 16)
            sp.dma_start(eye[:, :], ident).then_inc(small_in, 16)

            def load(j):
                sp.dma_start(h_sb[:, :, :], (h[bass.ds(j, 1), :, :, :]).rearrange("a p b d -> (a p) b d")).then_inc(h_in, 16)
                sp.dma_start(att_sb[:, :, :], att[bass.ds(j, 1), :, :, :].rearrange("a p b d -> (a p) b d")).then_inc(att_in, 16)

            def store(i):
                sp.wait_ge(out_ready, i + 1)
                sp.dma_start(w["out"][bass.ds(i, 1), :, :, :].rearrange("a p b d -> (a p) b d"), out_sb[:, :, :]).then_inc(out_done, 16)

            load(0)
            sp.wait_ge(w1_split, 1)
            sp.dma_start(raw[:, :], w["w2"]).then_inc(raw2_in, 16)
            with sp.Fori(0, IMAGES - 1) as i:
                sp.wait_ge(z_ready, i + 1)
                load(i + 1)
                store(i)
            store(IMAGES - 1)
            sp.wait_ge(out_done, 16 * IMAGES)

        @block.gpsimd
        def _(pool):
            pool.wait_ge(maxed, 2)
            nc.gpsimd.partition_all_reduce(all_maxes[:, 0:2], maxes[:, 0:2], P, RMAX).then_inc(all_maxed, 1)
            pool.wait_ge(maxed, 3)
            nc.gpsimd.partition_all_reduce(all_maxes[:, 2:3], maxes[:, 2:3], P, RMAX).then_inc(all_maxed, 1)

        @block.tensor
        def _(pe):
            pe.wait_ge(w_ready, 1)
            pe.wait_ge(small_in, 16 * (len(small) + 1))

            def up(i, a, t):
                e, f, n = t // FB, t % FB, t % 2
                if t == 0:
                    pe.wait_ge(x_split, (i + 1) * 4)
                pe.wait_ge(mid_ready[n], i * (NB // 2) + t // 2)
                cols = slice(f * P, (f + 1) * P)
                nc.tensor.matmul(up_ps[n][:, :], w1[:, e, 0, cols], xh_a[a][:, :], start=True, stop=False)
                nc.tensor.matmul(up_ps[n][:, :], w1[:, e, 0, cols], xl_a[a][:, :], start=False, stop=False)
                nc.tensor.matmul(up_ps[n][:, :], w1[:, e, 1, cols], xh_a[a][:, :], start=False, stop=False)
                nc.tensor.matmul(up_ps[n][:, :], w1[:, e, 2, cols], xh_m[a][:, :], start=False, stop=False)
                nc.tensor.matmul(up_ps[n][:, :], w1[0:REST, e, 2, cols], xl_m[a][:, :], start=False, stop=True).then_inc(up_ready[n], 1)

            def down_block(i, a, t):
                e, f, n = t // FB, t % FB, t % 2
                pe.wait_ge(mid_split[n], i * (NB // 2) + (t // 2 + 1))
                for b in range(TB):
                    if f == 0:
                        before = (e - 1) * TB + b + 1 if e else b + 1 - TB
                        pe.wait_ge(acc_steps, i * (2 * EXPERTS * TB) + 2 * max(before, 0))
                    rows = slice(b * P, (b + 1) * P)
                    nc.tensor.matmul(down[:, b, 0:2 * DIM], mid_h[n][:, rows], w2[:, t, :, :].rearrange("p a d -> p (a d)"),
                                     start=(f == 0), stop=False)
                    last = nc.tensor.matmul(down[:, b, 0:DIM], mid_l[n][:, rows], w2[:, t, 0, :], start=False, stop=(f == FB - 1))
                    if f == FB - 1:
                        last.then_inc(down_ready, 1)
                if f < FB - 1:
                    last.then_inc(mid_used[n], 1)

            def step(i, a, t):
                if t == 0:
                    up(i, a, 0)
                if t < NB - 1:
                    up(i, a, t + 1)
                down_block(i, a, t)

            def turn_att(j, a):
                pe.wait_ge(att_in, (j + 1) * 16)
                pe.wait_ge(acc_ready, j)
                for b in range(TB):
                    nc.tensor.transpose(misc[:, 0, b * P:(b + 1) * P], att_sb[:, b, 0:P], eye[:, :])
                    last = nc.tensor.transpose(misc[0:REST, 1, b * P:(b + 1) * P], att_sb[:, b, P:DIM], eye[:, :])
                last.then_inc(turned, 1)

            def project_att(j, a):
                pe.wait_ge(turned_read, j * 2 + 2)
                for b in range(TB):
                    rows = slice(b * P, (b + 1) * P)
                    nc.tensor.matmul(rows4[:, b, :], at_a[:, rows], small["wp_a"][:, :], start=True, stop=False)
                    last = nc.tensor.matmul(rows4[:, b, :], at_b[:, rows], small["wp_b"][:, :], start=False, stop=True)
                last.then_inc(projected, 1)

            def turn_x(j, a):
                pe.wait_ge(x_ready, j + 1)
                for b in range(TB):
                    nc.tensor.transpose(misc[:, 0, b * P:(b + 1) * P], x[:, b, 0:P], eye[:, :])
                    last = nc.tensor.transpose(misc[:, 1, b * P:(b + 1) * P], x[:, b, P:2 * P], eye[:, :])
                last.then_inc(x_turned, 1)

            def router_hidden(j, a):
                pe.wait_ge(xt_ready, j * 2 + 2)
                for half in range(2):
                    cols = slice(half * HALF, (half + 1) * HALF)
                    nc.tensor.matmul(misc[0:HALF, half, :], small["wr1_a"][:, cols], xt_a[:, :], start=True, stop=False)
                    last = nc.tensor.matmul(misc[0:HALF, half, :], small["wr1_b"][:, cols], xt_m[0:REST, :], start=False, stop=True)
                last.then_inc(hidden_up, 1)

            def router_score(j, a):
                pe.wait_ge(hidden_ready, j * 2 + 2)
                for b in range(TB):
                    for half in range(2):
                        last = nc.tensor.matmul(misc[:, 0, b * EXPERTS:(b + 1) * EXPERTS], hidden[:, half, b * P:(b + 1) * P],
                                                small["wr2"][:, half, :], start=(half == 0), stop=(half == 1))
                last.then_inc(scored, 1)

            def turn_route(j, a):
                pe.wait_ge(route_ready, j + 1)
                for b in range(TB):
                    last = nc.tensor.transpose(misc[0:EXPERTS, 0, b * P:(b + 1) * P], route[:, b, :], eye[:, :])
                last.then_inc(route_turned, 1)

            def mixed_bias(j, a):
                pe.wait_ge(route_t_ready, j + 1)
                for b in range(TB):
                    last = nc.tensor.matmul(rows4[:, b, :], route_t[:, b * P:(b + 1) * P], small["b2"][:, :], start=True, stop=True)
                last.then_inc(biased, 1)

            images(pe, step, {0: turn_att, 6: project_att, 16: turn_x, 20: router_hidden, 25: router_score,
                              34: turn_route, 38: mixed_bias})

        @block.scalar
        def _(act):
            act.wait_ge(w_ready, 1)
            act.wait_ge(small_in, 16 * (len(small) + 1))

            def step(i, a, t):
                n = t % 2
                act.wait_ge(up_ready[n], i * (NB // 2) + (t // 2 + 1))
                act.wait_ge(mid_split[n], i * (NB // 2) + t // 2)
                nc.scalar.activation(mid[n][:, :], up_ps[n][:, :], ACT.Relu, bias=small["b1"][:, t:t + 1],
                                     scale=unscale[:, 0:1]).then_inc(mid_ready[n], 1)

            def read_turned(j, a):
                act.wait_ge(turned, j + 1)
                act.wait_ge(projected, j)
                nc.scalar.activation(at_a[:, :], misc[:, 0, :], ACT.Copy).then_inc(turned_read, 1)
                nc.scalar.activation(at_b[:, :], misc[0:REST, 1, :], ACT.Copy).then_inc(turned_read, 1)

            def deviation(j, a):
                act.wait_ge(z_ready, j + 1)
                nc.scalar.activation(std[:, :], mean_var[:, :, 1], ACT.Sqrt, bias=eps[:, 0:1]).then_inc(std_ready, 1)

            def read_x(j, a):
                act.wait_ge(x_turned, j + 1)
                act.wait_ge(hidden_up, j)
                act.wait_ge(x_split, j * 4)
                nc.scalar.activation(xt_a[:, :], misc[:, 0, :], ACT.Copy).then_inc(xt_ready, 1)
                nc.scalar.activation(xt_m[:, :], misc[:, 1, :], ACT.Copy).then_inc(xt_ready, 1)

            def router_relu(j, a):
                act.wait_ge(hidden_up, j + 1)
                act.wait_ge(scored, j)
                for half in range(2):
                    nc.scalar.activation(hidden[:, half, :], misc[0:HALF, half, :], ACT.Relu,
                                         bias=small["br1"][:, half:half + 1]).then_inc(hidden_ready, 1)

            def gap_exp(j, a):
                act.wait_ge(gap_ready, j + 1)
                nc.scalar.activation(ratio[:, :], gap[:, :], ACT.Exp).then_inc(ratio_ready, 1)

            def read_route(j, a):
                act.wait_ge(route_turned, j + 1)
                act.wait_ge(biased, j)
                nc.scalar.activation(route_t[:, :], misc[0:EXPERTS, 0, :], ACT.Copy).then_inc(route_t_ready, 1)

            def end(i, a):
                act.wait_ge(end_var, i + 1)
                nc.scalar.activation(std2[:, :], mean_var2[:, :, 1], ACT.Sqrt, bias=eps[:, 0:1]).then_inc(end_std, 1)

            images(act, step, {3: read_turned, 11: deviation, 18: read_x, 22: router_relu, 29: gap_exp, 36: read_route}, end)

        @block.vector
        def _(dve):
            done = Done(dve, own)
            nc.vector.memset(eps[:, :], LN_EPS).then_inc(eps_set, 1)
            dve.wait_ge(raw_in, 32)
            for c, part in enumerate((raw1_a, raw1_b[:, :, :])):
                nc.vector.tensor_reduce(maxes[:, c:c + 1], part.rearrange("p a b -> p (a b)"), AX_X, ALU.max,
                                        apply_absolute_value=True).then_inc(maxed, 1)
            dve.wait_ge(all_maxed, 1)
            done(nc.vector.tensor_tensor(all_maxes[:, 1:2], all_maxes[:, 0:1], all_maxes[:, 1:2], ALU.max))
            power_of_two_scale(nc.vector, done, all_maxes[:, 1:2], scale[:, 0:1], unscale[:, 0:1], tmp[:, 0:1])
            done(nc.vector.tensor_scalar(w1[:, :, 0, :], raw1_a, scale[:, 0:1], None, ALU.mult))
            done(nc.vector.scalar_tensor_tensor(w1[:, :, 1, :], raw1_a, scale[:, 0:1], w1[:, :, 0, :], ALU.mult, ALU.subtract))
            nc.vector.memset(tmp[:, 1:2], 0.0).then_inc(w1_split, 1)
            done(nc.vector.tensor_scalar(w1[:, :, 2, :], raw1_b[:, :, :], scale[:, 0:1], None, ALU.mult))
            done(nc.vector.scalar_tensor_tensor(w1[REST:P, :, 2, :], raw1_b[REST:P, :, :], scale[REST:P, 0:1], w1[REST:P, :, 2, :],
                                                ALU.mult, ALU.subtract))
            dve.wait_ge(raw2_in, 16)
            nc.vector.tensor_reduce(maxes[:, 2:3], raw[:, :], AX_X, ALU.max, apply_absolute_value=True).then_inc(maxed, 1)
            dve.wait_ge(all_maxed, 2)
            power_of_two_scale(nc.vector, done, all_maxes[:, 2:3], scale[:, 1:2], unscale[:, 1:2], tmp[:, 1:2])
            done(nc.vector.tensor_scalar(w2[:, :, 0, :], raw2, scale[:, 1:2], None, ALU.mult))
            nc.vector.scalar_tensor_tensor(w2[:, :, 1, :], raw2, scale[:, 1:2], w2[:, :, 0, :],
                                           ALU.mult, ALU.subtract).then_inc(w_ready, 1)
            dve.wait_ge(w_ready, 1)
            dve.wait_ge(small_in, 16 * (len(small) + 1))

            def read_down(i, a, e):
                for b in range(TB):
                    dve.wait_ge(down_ready, i * (EXPERTS * TB) + (e * TB + b + 1))
                    for half in range(2):
                        last = nc.vector.scalar_tensor_tensor(acc[a][:, b, :], down[:, b, half * DIM:(half + 1) * DIM],
                                                              gate[a][:, b, e:e + 1], acc[a][:, b, :], ALU.mult, ALU.add)
                        last.then_inc(acc_steps, 1)
                        dve.wait_ge(acc_steps, i * (2 * EXPERTS * TB) + (2 * (e * TB + b) + half + 1))

            def step(i, a, t):
                n, e = t % 2, t // FB
                dve.wait_ge(mid_ready[n], i * (NB // 2) + (t // 2 + 1))
                before = t - 2
                if n == 0:
                    dve.wait_ge(mid_used[0], i * (NB // 2) + t // 2)
                elif before % FB == FB - 1:
                    dve.wait_ge(down_ready, i * (EXPERTS * TB) + (before + 1) // FB * TB)
                else:
                    dve.wait_ge(mid_used[1], i * (NB // 2 - EXPERTS) + (before // FB * (FB // 2 - 1) + before % FB // 2 + 1))
                nc.vector.tensor_copy(mid_h[n][:, :], mid[n][:, :]).then_inc(mid_high[n], 1)
                dve.wait_ge(mid_high[n], i * (NB // 2) + (t // 2 + 1))
                nc.vector.tensor_tensor(mid_l[n][:, :], mid[n][:, :], mid_h[n][:, :], ALU.subtract).then_inc(mid_split[n], 1)
                if t % FB == 0 and t:
                    read_down(i, a, e - 1)
                if t == NB - 1:
                    read_down(i, a, e)

            def residual(j, a):
                dve.wait_ge(projected, j + 1)
                dve.wait_ge(h_in, (j + 1) * 16)
                nc.vector.tensor_tensor(z[:, :, :], rows4, h_sb[:, :, :], ALU.add).then_inc(z_steps, 1)
                dve.wait_ge(z_steps, j * 6 + 1)
                nc.vector.tensor_tensor(z[:, :, :], z[:, :, :], small["b_proj"][:, :].unsqueeze(1).to_broadcast([P, TB, DIM]),
                                        ALU.add).then_inc(z_steps, 1)
                dve.wait_ge(z_steps, j * 6 + 2)
                for b in range(TB):
                    nc.vector.bn_stats(stats[:, b, :], z[:, b, :]).then_inc(z_steps, 1)
                dve.wait_ge(z_steps, j * 6 + 6)
                nc.vector.memset(idle[:, :], 0.0)
                for b in range(TB):
                    last = nc.vector.bn_aggr(mean_var[:, b, :], stats[:, b, :])
                last.then_inc(z_ready, 1)
                dve.wait_ge(z_ready, j + 1)

            def normalise(j, a):
                dve.wait_ge(std_ready, j + 1)
                nc.vector.reciprocal(inv_std[:, :], std[:, :]).then_inc(x_steps, 1)
                dve.wait_ge(x_steps, j * 2 + 1)
                dve.wait_ge(x_turned, j)
                for b in range(TB):
                    last = nc.vector.tensor_scalar(x[:, b, 0:DIM], z[:, b, :], mean_var[:, b, 0:1], inv_std[:, b:b + 1],
                                                   ALU.subtract, ALU.mult)
                last.then_inc(x_steps, 1)
                dve.wait_ge(x_steps, j * 2 + 2)
                nc.vector.tensor_copy(x[:, :, DIM:2 * P], x[:, :, P:DIM]).then_inc(x_ready, 1)

            def split_x(j, a):
                dve.wait_ge(xt_ready, j * 2 + 2)
                if not (isinstance(j, int) and j == 0):
                    last_used = (j - 1) * (NB // 2)
                    for n in range(2):
                        dve.wait_ge(up_ready[n], last_used)
                nc.vector.tensor_copy(xh_a[a][:, :], xt_a[:, :]).then_inc(x_split, 1)
                nc.vector.tensor_copy(xh_m[a][:, :], xt_m[:, :]).then_inc(x_split, 1)
                dve.wait_ge(x_split, j * 4 + 2)
                nc.vector.tensor_tensor(xl_a[a][:, :], xt_a[:, :], xh_a[a][:, :], ALU.subtract).then_inc(x_split, 1)
                nc.vector.tensor_tensor(xl_m[a][:, :], xt_m[0:REST, :], xh_m[a][0:REST, :], ALU.subtract).then_inc(x_split, 1)

            def best_two(j, a):
                S = 10
                dve.wait_ge(scored, j + 1)
                nc.vector.tensor_tensor(score[:, :, :], misc[:, 0, 0:TB * EXPERTS].rearrange("p (b e) -> p b e", b=TB),
                                        small["br2"][:, :].unsqueeze(1).to_broadcast([P, TB, EXPERTS]), ALU.add).then_inc(score_steps, 1)
                dve.wait_ge(score_steps, j * S + 1)
                nc.vector.memset(idle[:, :], 0.0)
                for b in range(TB):
                    nc.vector.max(best[:, b, :], score[:, b, :]).then_inc(score_steps, 1)
                dve.wait_ge(score_steps, j * S + 5)
                nc.vector.memset(idle[:, :], 0.0)
                for b in range(TB):
                    nc.vector.max_index(where[:, b, :], best[:, b, :], score[:, b, :]).then_inc(score_steps, 1)
                nc.vector.tensor_tensor(gap[:, :], best[:, :, 1], best[:, :, 0], ALU.subtract).then_inc(gap_ready, 1)
                dve.wait_ge(score_steps, j * S + 9)
                nc.vector.tensor_copy(pick[:, :, :], where[:, :, 0:2]).then_inc(score_steps, 1)
                dve.wait_ge(score_steps, j * S + 10)

            def routing(j, a):
                S = 5
                dve.wait_ge(ratio_ready, j + 1)
                nc.vector.tensor_scalar(total[:, :], ratio[:, :], 1.0, None, ALU.add).then_inc(route_steps, 1)
                dve.wait_ge(route_steps, j * S + 1)
                nc.vector.reciprocal(share[:, 0, :], total[:, :]).then_inc(route_steps, 1)
                dve.wait_ge(route_steps, j * S + 2)
                nc.vector.tensor_tensor(share[:, 1, :], ratio[:, :], share[:, 0, :], ALU.mult).then_inc(route_steps, 1)
                dve.wait_ge(route_steps, j * S + 3)
                for b in range(TB):
                    nc.vector.tensor_scalar(route[:, b, :], small["numbers"][:, :], pick[:, b, 0:1], share[:, 0, b:b + 1],
                                            ALU.is_equal, ALU.mult)
                    last = nc.vector.tensor_scalar(route2[:, b, :], small["numbers"][:, :], pick[:, b, 1:2], share[:, 1, b:b + 1],
                                                   ALU.is_equal, ALU.mult)
                last.then_inc(route_steps, 1)
                dve.wait_ge(route_steps, j * S + 4)
                nc.vector.tensor_tensor(route[:, :, :], route[:, :, :], route2[:, :, :], ALU.add).then_inc(route_ready, 1)
                dve.wait_ge(route_ready, j + 1)
                nc.vector.tensor_scalar(gate[a][:, :, :], route[:, :, :], unscale[:, 1:2], None, ALU.mult).then_inc(route_steps, 1)

            def begin_acc(j, a):
                dve.wait_ge(biased, j + 1)
                nc.vector.tensor_tensor(acc[a][:, :, :], x[:, :, 0:DIM], rows4, ALU.add).then_inc(acc_ready, 1)

            def end(i, a):
                S = 5
                for b in range(TB):
                    nc.vector.bn_stats(stats2[:, b, :], acc[a][:, b, :]).then_inc(end_steps, 1)
                dve.wait_ge(end_steps, i * S + 4)
                nc.vector.memset(idle[:, :], 0.0)
                for b in range(TB):
                    last = nc.vector.bn_aggr(mean_var2[:, b, :], stats2[:, b, :])
                last.then_inc(end_var, 1)
                dve.wait_ge(end_std, i + 1)
                nc.vector.reciprocal(inv_std2[:, :], std2[:, :]).then_inc(end_steps, 1)
                dve.wait_ge(end_steps, i * S + 5)
                dve.wait_ge(out_done, i * 16)
                for b in range(TB):
                    last = nc.vector.tensor_scalar(out_sb[:, b, :], acc[a][:, b, :], mean_var2[:, b, 0:1], inv_std2[:, b:b + 1],
                                                   ALU.subtract, ALU.mult)
                last.then_inc(out_ready, 1)

            images(dve, step, {9: residual, 13: normalise, 20: split_x, 27: best_two, 31: routing, 41: begin_acc}, end)


def tower(nc, x, freqs, w_tok, wq, wv, group_ones, ident, mix_w):
    scratch = lambda name, shape, dt: nc.dram_tensor(name, shape, dt, kind="Internal").ap()
    h = scratch("h_tokens", (IMAGES, P, TB, DIM), F32)
    q_parts = scratch("q_parts", (IMAGES, 2, 2, DIM // 2, TOKENS), F16)
    v_parts = scratch("v_parts", (IMAGES, P, TB * HEADS * VW), BF16)
    att = scratch("att_tokens", (IMAGES, P, TB, DIM), F32)
    embed(nc, x, freqs, w_tok, h)
    project(nc, h, wq, wv, group_ones, ident, q_parts, v_parts)
    attend(nc, q_parts, v_parts, ident, att)
    mix(nc, h, att, ident, mix_w)


def layouts(x, L0_tok_freq_bands, L0_tok_W, L0_attn_w_qkv, L0_attn_w_proj, L0_attn_b_proj, L0_ffn_W1, L0_ffn_b1,
            L0_ffn_W2, L0_ffn_b2, L0_ffn_Wr1, L0_ffn_br1, L0_ffn_Wr2, L0_ffn_br2):
    whole = np.ascontiguousarray
    xt = x.reshape(IMAGES, TOKENS, PATCH).transpose(0, 2, 1)
    blocks = xt[:, :FULL * P].reshape(IMAGES, FULL, P, TOKENS).transpose(0, 2, 1, 3)
    rest = np.concatenate([xt[:, FULL * P:]] * 2, axis=1)[:, :, None]
    freqs = np.zeros((P, BANDS + BANDS // 2), np.float32)
    freqs[:, :BANDS] = L0_tok_freq_bands
    freqs[:P // 2, BANDS:] = L0_tok_freq_bands[0::2]
    freqs[P // 2:, BANDS:] = L0_tok_freq_bands[1::2]
    w = L0_tok_W.reshape(DIM, PATCH, 2 * BANDS)
    w_tok = []
    for b, s in CHUNKS:
        for t in range(2):
            if s < FULL:
                w_tok.append(w[:, s * P:(s + 1) * P, b + BANDS * t].T)
            else:
                w_tok.append(np.concatenate([w[:, FULL * P:, b - 1 + BANDS * t].T, w[:, FULL * P:, b + BANDS * t].T]))
    w1 = L0_ffn_W1.transpose(2, 0, 1)
    rows = lambda a: whole(np.broadcast_to(a, (P, a.size)))
    return {
        "x": whole(np.concatenate([blocks, rest], axis=2).reshape(IMAGES, P, WIDE)),
        "freqs": freqs,
        "w_tok": whole(np.stack(w_tok, axis=1).reshape(P, NCH * DIM)),
        "wq": whole(L0_attn_w_qkv[:DIM].T),
        "wv": whole(L0_attn_w_qkv[2 * DIM:].T),
        "group_ones": np.kron(np.eye(HEADS // 2), np.ones((HD, HD))).astype(np.float32),
        "ident": np.eye(P, dtype=np.float32),
        "w1_a": whole(w1[:P].reshape(P, -1)),
        "w1_b": whole(np.concatenate([w1[P:], w1[P:]]).reshape(P, -1)),
        "w2": whole(L0_ffn_W2.reshape(EXPERTS, DIM, FB, P).transpose(3, 0, 2, 1).reshape(P, -1)),
        "small_b1": whole(L0_ffn_b1.reshape(EXPERTS * FB, P).T),
        "small_b2": whole(L0_ffn_b2),
        "small_wp_a": whole(L0_attn_w_proj.T[:P]),
        "small_wp_b": whole(L0_attn_w_proj.T[P:]),
        "small_wr1_a": whole(L0_ffn_Wr1.T[:P]),
        "small_wr1_b": whole(L0_ffn_Wr1.T[P:]),
        "small_br1": whole(L0_ffn_br1.reshape(2, DIM // 2).T),
        "small_wr2": whole(L0_ffn_Wr2.T.reshape(2, DIM // 2, EXPERTS).transpose(1, 0, 2)),
        "small_br2": rows(L0_ffn_br2),
        "small_b_proj": rows(L0_attn_b_proj),
        "small_numbers": rows(np.arange(EXPERTS, dtype=np.float32)),
    }


def kernel(**inputs):
    import concourse.bacc as bacc
    from concourse.bass_utils import run_bass_kernel_spmd as run

    nc = bacc.Bacc("TRN2", target_bir_lowering=False, num_devices=1)
    arrays, aps = {}, {}
    for name, a in layouts(**{n: np.asarray(a) for n, a in inputs.items()}).items():
        arrays[f"in_{name}_dram"] = a
        aps[name] = nc.dram_tensor(f"in_{name}_dram", a.shape, mybir.dt.from_np(a.dtype), kind="ExternalInput").ap()
    out = nc.dram_tensor("out_0_dram", (IMAGES, P, TB, DIM), F32, kind="ExternalOutput").ap()
    mix_w = {n: aps[n] for n in ("w1_a", "w1_b", "w2")}
    mix_w["small"] = {n[len("small_"):]: a for n, a in aps.items() if n.startswith("small_")}
    mix_w["out"] = out
    tower(nc, aps["x"], aps["freqs"], aps["w_tok"], aps["wq"], aps["wv"], aps["group_ones"], aps["ident"], mix_w)
    got = run(nc, [arrays], core_ids=[0]).results[0]["out_0_dram"]
    return got.transpose(0, 2, 1, 3).reshape(IMAGES, TOKENS, DIM)
```

```python
from contextlib import ExitStack

import numpy as np

import concourse.bass as bass
from concourse import mybir

F32 = mybir.dt.float32
F16 = mybir.dt.float16
BF16 = mybir.dt.bfloat16
I32 = mybir.dt.int32
U32 = mybir.dt.uint32
ALU = mybir.AluOpType
ACT = mybir.ActivationFunctionType
AX_X = mybir.AxisListType.X
RMAX = bass.bass_isa.ReduceOp.max

P = 128
START = 1
IMAGES, TOKENS, DIM, HEADS, BANDS = 16, 512, 192, 12, 6
HD = DIM // HEADS
EXPERTS, FFN = 8, 4 * DIM
PATCH = 3 * TOKENS * DIM // TOKENS
VW = 3 * HD + 1
FULL = PATCH // P
TB = TOKENS // P
SLOTS = FULL + 1
CHUNKS = [(b, s) for b in range(BANDS) for s in range(FULL + b % 2)]
NCH = 2 * len(CHUNKS)
WIDE = SLOTS * TOKENS
Q_SCALE = 64.0
TURN = float(np.nextafter(np.float32(2 * np.pi), np.float32(0)))


class Done:

    def __init__(self, engine, sem):
        self.engine, self.sem, self.n = engine, sem, 0

    def __call__(self, instruction):
        self.n += 1
        instruction.then_inc(self.sem, 1)
        self.engine.wait_ge(self.sem, START + self.n)


def power_of_two_scale(vector, done, own, scale, unscale, tmp):
    done(vector.tensor_scalar(tmp.bitcast(I32), own.bitcast(I32), 0x7F800000, None, ALU.bitwise_and))
    done(vector.tensor_scalar(tmp, tmp, 1e-30, None, ALU.max))
    done(vector.tensor_scalar(unscale, tmp, 2.0 ** -13, None, ALU.mult))
    done(vector.reciprocal(scale, unscale))


def embed(nc, x, freqs, w, h):
    with ExitStack() as ctx:
        sb = lambda name, shape, dt: ctx.enter_context(nc.sbuf_tensor(name, shape, dt))
        counters = []

        def sem(name):
            counters.append(ctx.enter_context(nc.semaphore(name)))
            return counters[-1]

        xt = [sb(f"xt{a}", [P, WIDE], F32) for a in range(2)]
        fr = sb("fr", [P, BANDS + BANDS // 2], F32)
        work = sb("work", [P, 8 * WIDE], F32)
        turns = [work[:, i * WIDE:(i + 1) * WIDE] for i in range(2)]
        absturns = [work[:, (2 + i) * WIDE:(3 + i) * WIDE] for i in range(2)]
        waves = [work[:, (4 + 2 * i) * WIDE:(6 + 2 * i) * WIDE].rearrange("p (t n) -> p t n", t=2) for i in range(2)]
        feat_h = [sb(f"feat_h{i}", [P, 2, WIDE], F16) for i in range(2)]
        feat_l = [sb(f"feat_l{i}", [P, 2, WIDE], F16) for i in range(2)]
        w_hl = sb("w_hl", [P, NCH, 2, DIM], F16)
        wabs = sb("wabs", [P, 1], F32)
        wmax = sb("wmax", [P, 1], F32)
        scale = sb("scale", [P, 1], F32)
        unscale = sb("unscale", [P, 1], F32)
        tmp = sb("tmp", [P, 1], F32)
        quarter = sb("quarter", [P, 1], F32)
        h_sb = sb("h_sb", [P, TB, DIM], F32)
        h_lo = sb("h_lo", [P, TB, DIM], F32)
        acc = [ctx.enter_context(nc.psum_tensor(f"acc{i}", [P, TB, 512], F32)) for i in range(2)]

        w_in, fr_in = sem("w_in"), sem("fr_in")
        x_in = [sem(f"x_in{a}") for a in range(2)]
        own, maxed, w_max_ready, w_ready, quarter_ready = (
            sem("own"), sem("maxed"), sem("w_max_ready"), sem("w_ready"), sem("quarter_ready"))
        angle_steps, halves_split = sem("angle_steps"), sem("halves_split")
        turns_ready = [sem(f"turns_ready{i}") for i in range(2)]
        waves_ready = [sem(f"waves_ready{i}") for i in range(2)]
        high_ready = [sem(f"high_ready{i}") for i in range(2)]
        low_sin_ready = [sem(f"low_sin_ready{i}") for i in range(2)]
        low_cos_ready = [sem(f"low_cos_ready{i}") for i in range(2)]
        feat_used = [sem(f"feat_used{i}") for i in range(2)]
        h_ready, h_out = sem("h_ready"), sem("h_out")
        UNITS = BANDS // 2
        w_raw = work[:, 0:NCH * DIM]
        block = ctx.enter_context(nc.Block())

        @block.sync
        def _(sp):
            for counter in counters:
                sp.sem_inc(counter, START)
            sp.dma_start(w_raw, w).then_inc(w_in, 16)
            sp.dma_start(fr[:, :], freqs).then_inc(fr_in, 16)

            def load(i, a):
                sp.dma_start(xt[a][:, :], x[bass.ds(i, 1), :, :].rearrange("a p n -> (a p) n")).then_inc(x_in[a], 16)

            def store(i):
                sp.wait_ge(h_ready, START + i + 1)
                sp.dma_start(h[bass.ds(i, 1), :, :, :].rearrange("a p b d -> (a p) b d"), h_sb[:, :, :]).then_inc(h_out, 16)

            load(0, 0)
            load(1, 1)
            with sp.Fori(0, IMAGES // 2 - 1) as pair:
                for a in range(2):
                    i = pair * 2 + a
                    store(i)
                    sp.wait_ge(angle_steps, START + (i + 1) * (2 * BANDS))
                    load(i + 2, a)
            store(IMAGES - 2)
            store(IMAGES - 1)
            sp.wait_ge(h_out, START + 16 * IMAGES)

        @block.gpsimd
        def _(pool):
            pool.wait_ge(maxed, START + 1)
            nc.gpsimd.partition_all_reduce(wmax[:, :], wabs[:, :], P, RMAX).then_inc(w_max_ready, 1)
            with pool.Fori(0, IMAGES) as i:
                for b in range(BANDS):
                    n, hi = b % 2, (FULL + b % 2) * TOKENS
                    pool.wait_ge(high_ready[n], START + i * UNITS + (b // 2 + 1))
                    pool.wait_ge(feat_used[n], START + i * UNITS + b // 2)
                    nc.gpsimd.tensor_tensor(feat_l[n][:, 1, 0:hi], waves[n][:, 1, 0:hi], feat_h[n][:, 1, 0:hi],
                                            ALU.subtract).then_inc(low_cos_ready[n], 1)

        @block.vector
        def _(dve):
            done = Done(dve, own)
            nc.vector.memset(quarter[:, :], float(np.pi / 2)).then_inc(quarter_ready, 1)
            dve.wait_ge(w_in, START + 16)
            nc.vector.tensor_reduce(wabs[:, :], w_raw, AX_X, ALU.max, apply_absolute_value=True).then_inc(maxed, 1)
            dve.wait_ge(w_max_ready, START + 1)
            power_of_two_scale(nc.vector, done, wmax[:, :], scale[:, :], unscale[:, :], tmp[:, :])
            raw = w_raw.rearrange("p (c d) -> p c d", c=NCH)
            done(nc.vector.tensor_scalar(w_hl[:, :, 0, :], raw, scale[:, 0:1], None, ALU.mult))
            done(nc.vector.scalar_tensor_tensor(w_hl[:, :, 1, :], raw, scale[:, 0:1], w_hl[:, :, 0, :],
                                                ALU.mult, ALU.subtract))
            nc.vector.memset(tmp[:, :], 0.0).then_inc(w_ready, 1)
            dve.wait_ge(fr_in, START + 16)

            def angles(i, a, b):
                n, last = b % 2, None
                parts = [(0, FULL * TOKENS, b)] + ([(FULL * TOKENS, WIDE, BANDS + b // 2)] if b % 2 else [])
                whole = absturns[n].bitcast(I32)
                if b == 0:
                    dve.wait_ge(x_in[a], START + i * 8 + (16 - 8 * a))
                dve.wait_ge(waves_ready[n], START + (i * UNITS + b // 2) * 2)
                for lo, hi, f in parts:
                    last = nc.vector.tensor_scalar(whole[:, lo:hi], xt[a][:, lo:hi], fr[:, f:f + 1], None, ALU.mult)
                last.then_inc(angle_steps, 1)
                dve.wait_ge(angle_steps, START + i * (2 * BANDS) + (2 * b + 1))
                for lo, hi, f in parts:
                    last = nc.vector.scalar_tensor_tensor(turns[n][:, lo:hi], xt[a][:, lo:hi], fr[:, f:f + 1],
                                                          whole[:, lo:hi], ALU.mult, ALU.subtract)
                last.then_inc(angle_steps, 1)
                dve.wait_ge(angle_steps, START + i * (2 * BANDS) + (2 * b + 2))
                hi = parts[-1][1]
                nc.vector.tensor_scalar(whole[:, 0:hi], turns[n].bitcast(I32)[:, 0:hi], 0x7FFFFFFF, None,
                                        ALU.bitwise_and).then_inc(turns_ready[n], 1)

            def low_sines(i, b):
                n, hi = b % 2, (FULL + b % 2) * TOKENS
                dve.wait_ge(high_ready[n], START + i * UNITS + (b // 2 + 1))
                dve.wait_ge(feat_used[n], START + i * UNITS + b // 2)
                nc.vector.tensor_tensor(feat_l[n][:, 0, 0:hi], waves[n][:, 0, 0:hi], feat_h[n][:, 0, 0:hi],
                                        ALU.subtract).then_inc(low_sin_ready[n], 1)

            def tokens(i, a):
                dve.wait_ge(feat_used[1], START + (i + 1) * UNITS)
                dve.wait_ge(h_out, START + i * 16)
                nc.vector.tensor_scalar(h_lo[:, :, :], acc[a][:, :, DIM:2 * DIM], unscale[:, 0:1], None,
                                        ALU.mult).then_inc(halves_split, 1)
                dve.wait_ge(halves_split, START + i + 1)
                nc.vector.scalar_tensor_tensor(h_sb[:, :, :], acc[a][:, :, 0:DIM], unscale[:, 0:1], h_lo[:, :, :],
                                               ALU.mult, ALU.add).then_inc(h_ready, 1)

            def image(i, a, before=True, after=True):
                for b in range(BANDS):
                    if b < BANDS - 1:
                        angles(i, a, b + 1)
                    elif after:
                        angles(i + 1, 1 - a, 0)
                    low_sines(i, b)
                    if before and b == 1:
                        tokens(i - 1, 1 - a)

            angles(0, 0, 0)
            image(0, 0, before=False)
            with dve.Fori(0, IMAGES // 2 - 1) as pair:
                image(pair * 2 + 1, 1)
                image(pair * 2 + 2, 0)
            image(IMAGES - 1, 1, after=False)
            tokens(IMAGES - 1, 1)

        @block.scalar
        def _(act):
            act.wait_ge(quarter_ready, START + 1)
            act.wait_ge(w_ready, START + 1)
            with act.Fori(0, IMAGES) as i:
                for b in range(BANDS):
                    n, hi = b % 2, (FULL + b % 2) * TOKENS
                    act.wait_ge(turns_ready[n], START + i * UNITS + (b // 2 + 1))
                    act.wait_ge(low_sin_ready[n], START + i * UNITS + b // 2)
                    act.wait_ge(low_cos_ready[n], START + i * UNITS + b // 2)
                    nc.scalar.activation(waves[n][:, 0, 0:hi], turns[n][:, 0:hi], ACT.Sin,
                                         scale=TURN).then_inc(waves_ready[n], 1)
                    nc.scalar.activation(waves[n][:, 1, 0:hi], absturns[n][:, 0:hi], ACT.Sin, bias=quarter[:, 0:1],
                                         scale=-TURN).then_inc(waves_ready[n], 1)
                    act.wait_ge(waves_ready[n], START + i * (2 * UNITS) + (2 * (b // 2) + 2))
                    act.wait_ge(feat_used[n], START + i * UNITS + b // 2)
                    nc.scalar.activation(feat_h[n][:, :, 0:hi], waves[n][:, :, 0:hi], ACT.Copy).then_inc(high_ready[n], 1)

        @block.tensor
        def _(pe):
            pe.wait_ge(w_ready, START + 1)
            with pe.Fori(0, IMAGES // 2) as pair:
                for a in range(2):
                    i = pair * 2 + a
                    pe.wait_ge(h_ready, START + i)
                    for b in range(BANDS):
                        n = b % 2
                        chunks = [(2 * k + t, s, t) for k, (band, s) in enumerate(CHUNKS) if band == b for t in range(2)]
                        pe.wait_ge(high_ready[n], START + i * UNITS + (b // 2 + 1))
                        for k, s, t in chunks:
                            for q in range(TB):
                                block_of = feat_h[n][:, t, s * TOKENS + q * P:s * TOKENS + (q + 1) * P]
                                nc.tensor.matmul(acc[a][:, q, 0:2 * DIM], block_of, w_hl[:, k, :, :].rearrange("p a d -> p (a d)"),
                                                 start=(k == 0), stop=False)
                        pe.wait_ge(low_sin_ready[n], START + i * UNITS + (b // 2 + 1))
                        pe.wait_ge(low_cos_ready[n], START + i * UNITS + (b // 2 + 1))
                        for k, s, t in chunks:
                            for q in range(TB):
                                block_of = feat_l[n][:, t, s * TOKENS + q * P:s * TOKENS + (q + 1) * P]
                                last = nc.tensor.matmul(acc[a][:, q, 0:DIM], block_of, w_hl[:, k, 0, :],
                                                        start=False, stop=(k == NCH - 1))
                        last.then_inc(feat_used[n], 1)


def project(nc, h, wqv, ident, q_parts, v_parts):
    with ExitStack() as ctx:
        sb = lambda name, shape, dt: ctx.enter_context(nc.sbuf_tensor(name, shape, dt))
        ps = lambda name, shape, dt: ctx.enter_context(nc.psum_tensor(name, shape, dt))
        counters = []

        def sem(name):
            counters.append(ctx.enter_context(nc.semaphore(name)))
            return counters[-1]

        REST, HALF, GROUPS = DIM - P, DIM // 2, TB * HEADS
        two = lambda name, shape, dt: [sb(f"{name}{a}", shape, dt) for a in range(2)]
        eye, eye_h = sb("eye", [P, P], F32), sb("eye_h2", [P, P], F16)
        w_a, w_b = sb("wqv_a", [P, 2 * DIM], F32), sb("wqv_b", [REST, 2 * DIM], F32)
        h_in_sb = two("h_in_sb", [P, TB, DIM], F32)
        ht_a, ht_b = two("ht_a", [P, TOKENS], F32), two("ht_b", [REST, TOKENS], F32)
        q_sb, v_full = two("q_sb", [P, GROUPS, HD], F32), two("v_full", [P, GROUPS, HD], F32)
        squares = sb("squares", [P, GROUPS, HD], F32)
        sums, root, inv = sb("sums2", [P, GROUPS], F32), sb("root", [P, GROUPS], F32), sb("inv", [P, GROUPS, 1], F32)
        qn = sb("qn", [P, GROUPS, HD], F32)
        q_nat = two("q_nat", [P, 2, TB, DIM], F16)
        q_hl = two("q_hl", [HALF, 2, 2, TOKENS], F16)
        v_rest = sb("v_rest", [P, GROUPS, HD], F32)
        v_sb = two("v_sb", [P, GROUPS, VW], BF16)
        pt_a, pt_b = ps("pt_a", [P, TOKENS], F32), ps("pt_b", [REST, TOKENS], F32)
        pqv = ps("pqv", [P, TB, 512], F32)
        pq_t = ps("pq_t", [HALF, 2, 2, TOKENS], F16)

        consts_in, consts_set = sem("consts_in"), sem("consts_set")
        h_in = [sem(f"h_in{a}") for a in range(2)]
        turned, ht_ready, qv_ready, q_out_ps, v_out_ps = (
            sem("turned"), sem("ht_ready"), sem("qv_ready"), sem("q_out_ps"), sem("v_out_ps"))
        squared, summed, rooted, inv_steps, scaled, q_high, q_split = (
            sem("squared"), sem("summed"), sem("rooted"), sem("inv_steps"), sem("scaled"), sem("q_high"), sem("q_split"))
        v_high, v_rest_ready, v_mid, v_split = sem("v_high"), sem("v_rest_ready"), sem("v_mid"), sem("v_split")
        parts_turned, parts_read = sem("parts_turned"), sem("parts_read")
        out = [sem(f"out{a}") for a in range(2)]
        CONSTS = 3
        block = ctx.enter_context(nc.Block())

        def images(eng, *stages):
            full = 2 * (len(stages) // 2)
            for i in range(full):
                for lag in range(min(i + 1, len(stages))):
                    stages[lag](i - lag, (i - lag) % 2)
            with eng.Fori(0, (IMAGES - full) // 2) as pair:
                for a in range(2):
                    for lag in range(len(stages)):
                        stages[lag](pair * 2 + (full + a - lag), (a - lag) % 2)
            for i in range(IMAGES, IMAGES + len(stages) - 1):
                for lag in range(i - IMAGES + 1, len(stages)):
                    stages[lag](i - lag, (i - lag) % 2)

        def nothing(i, a):
            pass

        @block.sync
        def _(sp):
            for counter in counters:
                sp.sem_inc(counter, START)
            for dst, src in ((eye, ident), (w_a, wqv[0:P, :]), (w_b, wqv[P:DIM, :])):
                sp.dma_start(dst[:, :], src).then_inc(consts_in, 16)

            def load(i, a):
                if not (isinstance(i, int) and i < 2):
                    sp.wait_ge(turned, START + i - 1)
                sp.dma_start(h_in_sb[a][:, :, :], h[bass.ds(i, 1), :, :, :].rearrange("a p b d -> (a p) b d")).then_inc(h_in[a], 16)

            def store_v(i, a):
                sp.wait_ge(v_split, START + i + 1)
                sp.dma_start(v_parts[bass.ds(i, 1), :, :].rearrange("a p n -> (a p) n"),
                             v_sb[a][:, :, :].rearrange("p g w -> p (g w)")).then_inc(out[a], 16)

            def store_q(i, a):
                sp.wait_ge(parts_read, START + i * 2 + 2)
                for part in range(2):
                    sp.dma_start(q_parts[bass.ds(i, 1), :, part, :, :].rearrange("a h p n -> p (a h) n"),
                                 q_hl[a][:, part, :, :]).then_inc(out[a], 16)

            images(sp, load, nothing, store_v, store_q)
            for a in range(2):
                sp.wait_ge(out[a], START + 48 * IMAGES // 2)

        def stored(eng, i, a):
            if isinstance(i, int):
                if i >= 2:
                    eng.wait_ge(out[a], START + (i - a) * 24)
            else:
                eng.wait_ge(out[a], START + i * 24 - 24 * a)

        @block.tensor
        def _(pe):
            pe.wait_ge(consts_in, START + 16 * CONSTS)
            pe.wait_ge(consts_set, START + 3)

            def turn(i, a):
                if isinstance(i, int):
                    pe.wait_ge(h_in[a], START + (i - a) * 8 + 16)
                else:
                    pe.wait_ge(h_in[a], START + i * 8 + (16 - 8 * a))
                pe.wait_ge(ht_ready, START + i * 2)
                for b in range(TB):
                    nc.tensor.transpose(pt_a[:, b * P:(b + 1) * P], h_in_sb[a][:, b, 0:P], eye[:, :])
                    last = nc.tensor.transpose(pt_b[:, b * P:(b + 1) * P], h_in_sb[a][:, b, P:DIM], eye[:, :])
                last.then_inc(turned, 1)

            def multiply(i, a):
                pe.wait_ge(ht_ready, START + i * 2 + 2)
                pe.wait_ge(q_out_ps, START + i)
                pe.wait_ge(v_out_ps, START + i)
                for b in range(TB):
                    rows = slice(b * P, (b + 1) * P)
                    nc.tensor.matmul(pqv[:, b, 0:2 * DIM], ht_a[a][:, rows], w_a[:, :], start=True, stop=False)
                    last = nc.tensor.matmul(pqv[:, b, 0:2 * DIM], ht_b[a][:, rows], w_b[:, :], start=False, stop=True)
                last.then_inc(qv_ready, 1)

            def turn_parts(i, a):
                pe.wait_ge(q_split, START + i + 1)
                pe.wait_ge(parts_read, START + i * 2)
                for part in range(2):
                    for half in range(2):
                        for b in range(TB):
                            last = nc.tensor.transpose(pq_t[:, part, half, b * P:(b + 1) * P],
                                                       q_nat[a][:, part, b, half * HALF:(half + 1) * HALF], eye_h[:, :])
                last.then_inc(parts_turned, 1)

            images(pe, turn, multiply, turn_parts)

        @block.scalar
        def _(act):
            def read_turned(i, a):
                act.wait_ge(turned, START + i + 1)
                if not (isinstance(i, int) and i < 2):
                    act.wait_ge(qv_ready, START + i - 1)
                nc.scalar.activation(ht_a[a][:, :], pt_a[:, :], ACT.Copy).then_inc(ht_ready, 1)
                nc.scalar.activation(ht_b[a][:, :], pt_b[:, :], ACT.Copy).then_inc(ht_ready, 1)

            def read_q(i, a):
                act.wait_ge(qv_ready, START + i + 1)
                act.wait_ge(scaled, START + i)
                act.wait_ge(summed, START + i)
                nc.scalar.activation(q_sb[a][:, :, :].rearrange("p (b g) d -> p b (g d)", b=TB), pqv[:, :, 0:DIM],
                                     ACT.Copy).then_inc(q_out_ps, 1)
                act.wait_ge(q_out_ps, START + i + 1)
                nc.scalar.activation(squares[:, :, :], q_sb[a][:, :, :], ACT.Square).then_inc(squared, 1)
                act.wait_ge(summed, START + i + 1)
                act.wait_ge(inv_steps, START + i * 2)
                nc.scalar.activation(root[:, :], sums[:, :], ACT.Sqrt).then_inc(rooted, 1)

            def read_high(i, a):
                act.wait_ge(parts_turned, START + i + 1)
                stored(act, i, a)
                nc.scalar.activation(q_hl[a][:, 0, :, :], pq_t[:, 0, :, :], ACT.Copy).then_inc(parts_read, 1)

            images(act, read_turned, read_q, read_high)

        @block.gpsimd
        def _(pool):
            def v_parts_two(i, a):
                pool.wait_ge(v_high, START + i + 1)
                pool.wait_ge(v_split, START + i)
                nc.gpsimd.tensor_tensor(v_rest[:, :, :], v_full[a][:, :, :], v_sb[a][:, :, 0:HD], ALU.subtract).then_inc(v_rest_ready, 1)
                pool.wait_ge(v_mid, START + i + 1)
                nc.gpsimd.tensor_tensor(v_sb[a][:, :, 2 * HD:3 * HD], v_rest[:, :, :], v_sb[a][:, :, HD:2 * HD],
                                        ALU.subtract).then_inc(v_split, 1)

            images(pool, nothing, v_parts_two, nothing)

        @block.vector
        def _(dve):
            for a in range(2):
                nc.vector.memset(v_sb[a][:, :, 3 * HD:VW], 1.0).then_inc(consts_set, 1)
            dve.wait_ge(consts_in, START + 16 * CONSTS)
            nc.vector.tensor_copy(eye_h[:, :], eye[:, :]).then_inc(consts_set, 1)

            def split(i, a):
                dve.wait_ge(q_out_ps, START + i + 1)
                if not (isinstance(i, int) and i < 2):
                    dve.wait_ge(v_split, START + i - 1)
                nc.vector.tensor_copy(v_full[a][:, :, :].rearrange("p (b g) d -> p b (g d)", b=TB),
                                      pqv[:, :, DIM:2 * DIM]).then_inc(v_out_ps, 1)
                dve.wait_ge(v_out_ps, START + i + 1)
                stored(dve, i, a)
                nc.vector.tensor_copy(v_sb[a][:, :, 0:HD], v_full[a][:, :, :]).then_inc(v_high, 1)
                dve.wait_ge(squared, START + i + 1)
                dve.wait_ge(rooted, START + i)
                nc.vector.tensor_reduce(sums[:, :], squares[:, :, :], AX_X, ALU.add).then_inc(summed, 1)
                dve.wait_ge(v_rest_ready, START + i + 1)
                nc.vector.tensor_copy(v_sb[a][:, :, HD:2 * HD], v_rest[:, :, :]).then_inc(v_mid, 1)
                dve.wait_ge(rooted, START + i + 1)
                nc.vector.tensor_scalar(root[:, :], root[:, :], 1e-8, None, ALU.add).then_inc(inv_steps, 1)
                dve.wait_ge(inv_steps, START + i * 2 + 1)
                nc.vector.reciprocal(inv[:, :, 0], root[:, :]).then_inc(inv_steps, 1)
                dve.wait_ge(inv_steps, START + i * 2 + 2)
                nc.vector.scalar_tensor_tensor(qn[:, :, :], q_sb[a][:, :, :], Q_SCALE, inv[:, :, :].to_broadcast([P, GROUPS, HD]),
                                               ALU.mult, ALU.mult).then_inc(scaled, 1)
                dve.wait_ge(scaled, START + i + 1)
                if not (isinstance(i, int) and i < 2):
                    dve.wait_ge(parts_turned, START + i - 1)
                parts = q_nat[a][:, :, :, :].rearrange("p w b (g d) -> p w (b g) d", d=HD)
                nc.vector.tensor_copy(parts[:, 0], qn[:, :, :]).then_inc(q_high, 1)
                dve.wait_ge(q_high, START + i + 1)
                nc.vector.tensor_tensor(parts[:, 1], qn[:, :, :], parts[:, 0], ALU.subtract).then_inc(q_split, 1)

            def read_low(i, a):
                dve.wait_ge(parts_turned, START + i + 1)
                stored(dve, i, a)
                nc.vector.tensor_copy(q_hl[a][:, 1, :, :], pq_t[:, 1, :, :]).then_inc(parts_read, 1)

            images(dve, nothing, split, read_low)

UH = HEADS // 2
GH = UH // 2
REG, ITERS = 0.1, 10
STEPS_X = 2 * ITERS - 1
K_SHIFT = float(15 * np.log(2))
HIDE = -60000.0
ATT_SCALE = HD ** -0.5


def attend(nc, q_parts, v_parts, ident, att):
    with ExitStack() as ctx:
        sb = lambda name, shape, dt: ctx.enter_context(nc.sbuf_tensor(name, shape, dt))
        ps = lambda name, shape, dt: ctx.enter_context(nc.psum_tensor(name, shape, dt))
        counters = []

        def sem(name):
            counters.append(ctx.enter_context(nc.semaphore(name)))
            return counters[-1]

        eye = sb("eye3", [P, P], F32)
        eye_h, eye_hide = sb("eye_h", [P, P], F16), sb("eye_hide", [P, P], F16)
        eye_bf = sb("eye_bf", [P, P], BF16)
        XR = UH * TB * 3
        pick = sb("pick3", [XR, UH * TB, P], BF16)
        xt_sb = sb("xt_sb", [XR, P], BF16)
        lift = sb("lift", [P, 2, P], F16)
        ones = sb("ones3", [P, P], BF16)
        k_bias, p_bias = sb("k_bias", [P, 1], F32), sb("p_bias", [P, 1], F32)
        q_left = [sb(f"q_left{s}", [P, UH, TOKENS], F16) for s in range(2)]
        q_right = [sb(f"q_right{s}", [P, UH, TOKENS], F16) for s in range(2)]
        v_sb = [sb(f"v_in_sb{s}", [P, TB, UH, VW], BF16) for s in range(2)]
        k_h = [sb(f"k_h{s}", [P, UH, TB * TOKENS], F16) for s in range(2)]
        k_l = [sb(f"k_l{s}", [P, UH, TB * TOKENS], F16) for s in range(2)]
        row_sums = [sb(f"row_sums{s}", [P, UH * TB], F32) for s in range(2)]
        x_sb = [sb(f"x_sb{s}", [P, UH * TB, 3], BF16) for s in range(2)]
        v_last = [sb(f"v_last{s}", [P, UH * TB], F32) for s in range(2)]
        k_new = sb("k_new", [P, TB, TOKENS], F32)
        plan = sb("plan", [P, TB, TOKENS], F32)
        probs = sb("probs", [P, TB, TOKENS], F32)
        p_h, p_l = sb("p_h", [P, TB, TOKENS], F16), sb("p_l", [P, TB, TOKENS], F16)
        sums = [sb(f"sums{g}", [P, GH * TB], F32) for g in range(2)]
        recs = [sb(f"recs{g}", [P, GH * TB], F32) for g in range(2)]
        rest = [sb(f"rest{g}", [P, GH * TB], F32) for g in range(2)]
        idle, idle_pool = sb("idle", [P, 1], F32), sb("idle_pool", [P, 3], F32)
        row_max, weighted = sb("row_max", [P, TB], F32), sb("weighted", [P, TB], F32)
        head_max, all_max, inv_max = sb("head_max", [P, 1], F32), sb("all_max", [P, 1], F32), sb("inv_max", [P, 1], F32)
        p_scale = sb("p_scale", [P, TB], F32)
        num, den = sb("num", [P, TB, HD], F32), sb("den", [P, TB, 1], F32)
        att_sb = [sb(f"att_sb{s}", [P, TB, UH, HD], F32) for s in range(2)]
        kx = [ps(f"kx{g}", [P, GH * TB, 3], F32) for g in range(2)]
        cos = ps("cos", [P, 2, TOKENS], F32)
        u_rows = ps("u_rows", [P, TOKENS], F32)
        xt_ps = ps("xt_ps", [XR, P], F32)
        pv = ps("pv3", [P, TB, VW], F32)

        eye_in, consts, ones_set = sem("eye_in"), sem("consts"), sem("ones3_set")
        q_in = [sem(f"q_in{s}") for s in range(2)]
        v_in = [sem(f"v_in{s}") for s in range(2)]
        att_out = [sem(f"att_out{s}") for s in range(2)]
        kx_ready = [sem(f"kx_ready{g}") for g in range(2)]
        x_ready = [sem(f"x_ready{g}") for g in range(2)]
        sum_steps = [sem(f"sum_steps{g}") for g in range(2)]
        x_steps = [sem(f"x_steps{g}") for g in range(2)]
        cos_ready, k_exp, k_high, k_built = sem("cos_ready"), sem("k_exp"), sem("k_high"), sem("k_built")
        pick_steps, x_turned, xt_ready = sem("pick_steps"), sem("x_turned3"), sem("xt_ready3")
        u_rows_ready, k_joined = sem("u_rows_ready"), sem("k_joined")
        plan_ready, weighed, head_max_ready, all_max_ready = (
            sem("plan_ready"), sem("weighed"), sem("head_max_ready"), sem("all_max_ready"))
        inv_ready, scale_ready, p_exp, p_high, p_ready = (
            sem("inv_ready"), sem("scale_ready"), sem("p_exp"), sem("p_high"), sem("p_ready"))
        pv_ready, summed_up, att_ready = sem("pv_ready"), sem("summed_up"), sem("att_ready")
        block = ctx.enter_context(nc.Block())

        def units(eng, head, last=None, first=None):
            with eng.Fori(0, UH) as k:
                head(None, None, (0, 0, 0), k)
            if first:
                first()

            def unit(n, f, b):
                with eng.Fori(0, UH) as k:
                    head(n, f, b, k)
                if last:
                    last(n, b)

            unit((0, 0, 0), None, (1, 1, 0))
            with eng.Fori(0, IMAGES - 1) as t:
                unit((t * 2 + 1, 1, t), (t * 2, 0, t), (t * 2 + 2, 0, t + 1))
                unit((t * 2 + 2, 0, t + 1), (t * 2 + 1, 1, t), (t * 2 + 3, 1, t + 1))
            unit((2 * IMAGES - 1, 1, IMAGES - 1), (2 * IMAGES - 2, 0, IMAGES - 1), None)
            with eng.Fori(0, UH) as k:
                head(None, (2 * IMAGES - 1, 1, IMAGES - 1), None, k)

        @block.sync
        def _(sp):
            for counter in counters:
                sp.sem_inc(counter, START)
            sp.dma_start(eye[:, :], ident).then_inc(eye_in, 16)

            def load_q(image, s):
                for g in range(4):
                    for dst, part in ((q_left, g // 2), (q_right, g % 2)):
                        sp.dma_start(dst[s][32 * g:32 * g + HD, :, :],
                                     q_parts[bass.ds(image, 1), s, part, :, :].rearrange("a (k d) n -> d (a k) n", d=HD)).then_inc(q_in[s], 16)

            def load_v(image, s):
                src = v_parts[bass.ds(image, 1), :, :].rearrange("a p (b h w) -> (a p) b h w", b=TB, h=HEADS)
                sp.dma_start(v_sb[s][:, :, :, :], src[:, :, s * UH:(s + 1) * UH, :]).then_inc(v_in[s], 16)

            def store(image, s):
                dst = att[bass.ds(image, 1), :, :, :].rearrange("a p b (s n) -> (a p) b s n", s=2)[:, :, s, :]
                sp.dma_start(dst, att_sb[s][:, :, :, :].rearrange("p b h d -> p b (h d)")).then_inc(att_out[s], 16)

            sp.wait_ge(ones_set, START + 1)
            load_q(0, 0)
            load_q(0, 1)
            load_v(0, 0)
            sp.wait_ge(cos_ready, START + 2 * UH)
            load_q(1, 0)
            sp.wait_ge(cos_ready, START + 2 * UH * 2)
            load_q(1, 1)
            load_v(0, 1)
            with sp.Fori(0, IMAGES - 2) as t:
                for s in range(2):
                    u = t * 2 + s
                    sp.wait_ge(att_ready, START + (u + 1) * UH)
                    store(t, s)
                    sp.wait_ge(cos_ready, START + (u + 3) * (2 * UH))
                    load_q(t + 2, s)
                    sp.wait_ge(pv_ready, START + (u + 1) * UH)
                    load_v(t + 1, s)
            for t, s in ((IMAGES - 2, 0), (IMAGES - 2, 1), (IMAGES - 1, 0), (IMAGES - 1, 1)):
                sp.wait_ge(att_ready, START + (2 * t + s + 1) * UH)
                store(t, s)
                if t == IMAGES - 2:
                    load_v(t + 1, s)
            for s in range(2):
                sp.wait_ge(att_out[s], START + 16 * IMAGES)

        @block.gpsimd
        def _(pool):
            nc.gpsimd.memset(pick[:, :, :], 1.0).then_inc(pick_steps, 1)
            pool.wait_ge(pick_steps, START + 1)
            nc.gpsimd.affine_select(out=pick[:, :, :], in_=pick[:, :, :], compare_op=ALU.is_ge, fill=0.0, base=0,
                                    pattern=[[-3, UH * TB], [0, P]], channel_multiplier=1).then_inc(pick_steps, 1)
            pool.wait_ge(pick_steps, START + 2)
            nc.gpsimd.affine_select(out=pick[:, :, :], in_=pick[:, :, :], compare_op=ALU.is_ge, fill=0.0, base=2,
                                    pattern=[[3, UH * TB], [0, P]], channel_multiplier=-1).then_inc(pick_steps, 1)
            pool.wait_ge(consts, START + 7)

            def head(n, f, b, k):
                if f:
                    F = f[0] * UH + k
                    pool.wait_ge(p_exp, START + F * TB)
                    nc.gpsimd.tensor_tensor(idle_pool[:, 0:1], k_bias[:, :], k_bias[:, :], ALU.add)
                    nc.gpsimd.tensor_tensor(plan[:, :, :].rearrange("p b n -> p (b n)"),
                                            k_h[f[1]][:, bass.ds(k, 1), :].rearrange("p a n -> p (a n)"),
                                            k_l[f[1]][:, bass.ds(k, 1), :].rearrange("p a n -> p (a n)"), ALU.add).then_inc(k_joined, 1)
                    pool.wait_ge(head_max_ready, START + F + 1)
                    nc.gpsimd.tensor_tensor(idle_pool[:, 1:2], k_bias[:, :], k_bias[:, :], ALU.add)
                    nc.gpsimd.partition_all_reduce(all_max[:, :], head_max[:, :], P, RMAX).then_inc(all_max_ready, 1)
                if b:
                    pool.wait_ge(k_high, START + b[0] * UH + k + 1)
                    nc.gpsimd.tensor_tensor(idle_pool[:, 2:3], k_bias[:, :], k_bias[:, :], ALU.add)
                    nc.gpsimd.tensor_tensor(k_l[b[1]][:, bass.ds(k, 1), :].rearrange("p a n -> p (a n)"),
                                            k_new[:, :, :].rearrange("p b n -> p (b n)"),
                                            k_h[b[1]][:, bass.ds(k, 1), :].rearrange("p a n -> p (a n)"), ALU.subtract).then_inc(k_built, 1)

            units(pool, head)

        @block.tensor
        def _(pe):
            pe.wait_ge(consts, START + 7)
            pe.wait_ge(pick_steps, START + 3)

            def product(n, g, m, first=False):
                pe.wait_ge(x_ready[g], START + n[0] * STEPS_X + m)
                if first:
                    pe.wait_ge(sum_steps[g], START + n[0] * STEPS_X + (m - 1))
                for h in range(g * GH, (g + 1) * GH):
                    for i in range(TB):
                        out = kx[g][:, (h - g * GH) * TB + i, :]
                        for j in range(TB):
                            cols = slice(j * TOKENS + i * P, j * TOKENS + (i + 1) * P)
                            x = x_sb[n[1]][:, h * TB + j, :]
                            nc.tensor.matmul(out, k_h[n[1]][:, h, cols], x, start=(j == 0), stop=False)
                            last = nc.tensor.matmul(out, k_l[n[1]][:, h, cols], x, start=False, stop=(j == TB - 1))
                last.then_inc(kx_ready[g], 1)

            def cosines(b, k, half):
                G = b[0] * UH + k
                if half == 0:
                    pe.wait_ge(q_in[b[1]], START + (b[2] + 1) * (8 * 16))
                pe.wait_ge(k_exp, START + G * TB + 2 * half)
                for c in (2 * half, 2 * half + 1):
                    nc.tensor.matmul(cos[:, c % 2, :], q_left[b[1]][:, bass.ds(k, 1), c * P:(c + 1) * P].rearrange("p a n -> p (a n)"),
                                     q_right[b[1]][:, bass.ds(k, 1), :].rearrange("p a n -> p (a n)"), start=True, stop=False)
                    last = nc.tensor.matmul(cos[:, c % 2, c * P:(c + 1) * P], eye_h[:, :], eye_hide[:, :], start=False, stop=True)
                last.then_inc(cos_ready, 1)

            def u_to_rows(f, k):
                F = f[0] * UH + k
                pe.wait_ge(xt_ready, START + f[0] + 1)
                pe.wait_ge(plan_ready, START + F)
                for c in range(TB):
                    last = nc.tensor.matmul(u_rows[:, c * P:(c + 1) * P],
                                            pick[:, bass.ds(k * TB + c, 1), :].rearrange("p a n -> p (a n)"), xt_sb[:, :],
                                            start=True, stop=True)
                last.then_inc(u_rows_ready, 1)

            def times_v(f, k):
                F = f[0] * UH + k
                pe.wait_ge(p_ready, START + F * 2 + 2)
                pe.wait_ge(v_in[f[1]], START + (f[2] + 1) * 16)
                pe.wait_ge(att_ready, START + F)
                for i in range(TB):
                    for j in range(TB):
                        v = v_sb[f[1]][:, j, bass.ds(k, 1), :].rearrange("p a n -> p (a n)")
                        nc.tensor.matmul(pv[:, i, :], p_h[:, j, i * P:(i + 1) * P], v, start=(j == 0), stop=False)
                        nc.tensor.matmul(pv[:, i, :], p_l[:, j, i * P:(i + 1) * P], v, start=False, stop=False)
                    v = v_sb[f[1]][:, i, bass.ds(k, 1), :].rearrange("p a n -> p (a n)")
                    nc.tensor.matmul(pv[:, i, :], lift[:, 0, :], v, start=False, stop=False)
                    last = nc.tensor.matmul(pv[:, i, :], lift[:, 1, :], v, start=False, stop=True)
                last.then_inc(pv_ready, 1)

            def head(n, f, b, k):
                if f:
                    u_to_rows(f, k)
                if n:
                    product(n, 0, k * 3 + 1, True)
                if b:
                    cosines(b, k, 0)
                if n:
                    product(n, 1, k * 3 + 1, True)
                if b:
                    cosines(b, k, 1)
                if n:
                    for m in (2, 3):
                        for g in range(2):
                            product(n, g, k * 3 + m)
                if f:
                    times_v(f, k)

            def last(n, b):
                product(n, 0, STEPS_X)
                pe.wait_ge(xt_ready, START + n[0])
                pe.wait_ge(x_ready[1], START + (n[0] + 1) * STEPS_X)
                nc.tensor.matmul(xt_ps[:, :], x_sb[n[1]][:, :, :].rearrange("p c w -> p (c w)"), eye_bf[:, :],
                                 start=True, stop=True).then_inc(x_turned, 1)
                product(n, 1, STEPS_X)

            units(pe, head, last)

        @block.scalar
        def _(act):
            act.wait_ge(consts, START + 7)

            def head(n, f, b, k):
                if b:
                    G = b[0] * UH + k
                    act.wait_ge(k_built, START + G)
                    for c in range(TB):
                        if c % 2 == 0:
                            act.wait_ge(cos_ready, START + G * 2 + (c // 2 + 1))
                        nc.scalar.activation(k_new[:, c, :], cos[:, c % 2, :], ACT.Exp, bias=k_bias[:, 0:1],
                                             scale=1.0 / (REG * Q_SCALE ** 2),
                                             accum_out=row_sums[b[1]][:, bass.ds(k * TB + c, 1)]).then_inc(k_exp, 1)
                    act.wait_ge(k_exp, START + (G + 1) * TB)
                    if f:
                        act.wait_ge(k_joined, START + f[0] * UH + k + 1)
                    nc.scalar.activation(k_h[b[1]][:, bass.ds(k, 1), :].rearrange("p a n -> p (a n)"),
                                         k_new[:, :, :].rearrange("p b n -> p (b n)"), ACT.Copy).then_inc(k_high, 1)
                if f:
                    F = f[0] * UH + k
                    act.wait_ge(scale_ready, START + F + 1)
                    act.wait_ge(p_ready, START + F * 2)
                    act.wait_ge(pv_ready, START + F)
                    for half in range(2):
                        for c in (2 * half, 2 * half + 1):
                            nc.scalar.activation(probs[:, c, :], plan[:, c, :], ACT.Exp, bias=p_bias[:, 0:1],
                                                 scale=p_scale[:, c:c + 1]).then_inc(p_exp, 1)
                        act.wait_ge(p_exp, START + F * TB + (2 * half + 2))
                        c = slice(2 * half, 2 * half + 2)
                        nc.scalar.activation(p_h[:, c, :], probs[:, c, :], ACT.Copy).then_inc(p_high, 1)

            def last(n, b):
                act.wait_ge(x_turned, START + n[0] + 1)
                act.wait_ge(u_rows_ready, START + n[0] * UH)
                nc.scalar.activation(xt_sb[:, :], xt_ps[:, :], ACT.Copy).then_inc(xt_ready, 1)

            units(act, head, last)

        @block.vector
        def _(dve):
            for s in range(2):
                nc.vector.memset(q_left[s][:, :, :], 0.0)
                nc.vector.memset(q_right[s][:, :, :], 0.0)
            nc.vector.memset(ones[:, :], 1.0).then_inc(ones_set, 1)
            nc.vector.memset(k_bias[:, :], K_SHIFT - 1.0 / REG).then_inc(consts, 1)
            nc.vector.memset(p_bias[:, :], -ATT_SCALE).then_inc(consts, 1)
            dve.wait_ge(eye_in, START + 16)
            on_diag = float(1.0 - np.exp(-ATT_SCALE))
            on_diag_h = float(np.float16(on_diag))
            nc.vector.tensor_copy(eye_h[:, :], eye[:, :]).then_inc(consts, 1)
            nc.vector.tensor_copy(eye_bf[:, :], eye[:, :]).then_inc(consts, 1)
            nc.vector.tensor_scalar(eye_hide[:, :], eye[:, :], HIDE, None, ALU.mult).then_inc(consts, 1)
            nc.vector.tensor_scalar(lift[:, 0, :], eye[:, :], on_diag_h, None, ALU.mult).then_inc(consts, 1)
            nc.vector.tensor_scalar(lift[:, 1, :], eye[:, :], on_diag - on_diag_h, None, ALU.mult).then_inc(consts, 1)
            dve.wait_ge(consts, START + 7)

            def next_x(n, g, m, source, keep=True):
                cols = slice(g * GH * TB, (g + 1) * GH * TB)
                if not keep:
                    nc.vector.reciprocal(v_last[n[1]][:, cols], source)
                    return
                base = n[0] * (4 * STEPS_X) + (m * 4)
                x = x_sb[n[1]]
                nc.vector.reciprocal(recs[g][:, :], source).then_inc(x_steps[g], 1)
                with nc.allow_low_precision("the leading part of three"):
                    nc.vector.reciprocal(x[:, cols, 0], source).then_inc(x_steps[g], 1)
                dve.wait_ge(x_steps[g], START + base + 2)
                nc.vector.tensor_tensor(x[:, cols, 1], recs[g][:, :], x[:, cols, 0], ALU.subtract).then_inc(x_steps[g], 1)
                nc.vector.tensor_tensor(rest[g][:, :], recs[g][:, :], x[:, cols, 0], ALU.subtract).then_inc(x_steps[g], 1)
                dve.wait_ge(x_steps[g], START + base + 4)
                nc.vector.tensor_tensor(x[:, cols, 2], rest[g][:, :], x[:, cols, 1], ALU.subtract).then_inc(x_ready[g], 1)

            def turn(n, g, m, keep=True):
                done = n[0] * STEPS_X + m
                dve.wait_ge(kx_ready[g], START + done)
                nc.vector.tensor_reduce(sums[g][:, :], kx[g][:, :, :], AX_X, ALU.add).then_inc(sum_steps[g], 1)
                dve.wait_ge(sum_steps[g], START + done)
                next_x(n, g, m, sums[g][:, :], keep)

            def first_x(n):
                dve.wait_ge(k_built, START + (n[0] + 1) * UH)
                for g in range(2):
                    next_x(n, g, 0, row_sums[n[1]][:, g * GH * TB:(g + 1) * GH * TB])

            def times_u(f, k, chunks):
                F = f[0] * UH + k
                if chunks[0] == 0:
                    dve.wait_ge(k_joined, START + F + 1)
                    dve.wait_ge(u_rows_ready, START + F + 1)
                    nc.vector.memset(idle[:, :], 0.0)
                for c in chunks:
                    last = nc.vector.tensor_tensor_reduce(plan[:, c, :], plan[:, c, :], u_rows[:, :], 1.0, 0.0,
                                                          ALU.mult, ALU.max, row_max[:, c:c + 1])
                if c == TB - 1:
                    last.then_inc(plan_ready, 1)
                    dve.wait_ge(plan_ready, START + F + 1)
                    nc.vector.tensor_tensor(weighted[:, :], row_max[:, :], v_last[f[1]][:, bass.ds(k * TB, TB)], ALU.mult).then_inc(weighed, 1)
                    dve.wait_ge(weighed, START + F + 1)
                    nc.vector.tensor_reduce(head_max[:, :], weighted[:, :], AX_X, ALU.max).then_inc(head_max_ready, 1)

            def scale_plan(f, k):
                F = f[0] * UH + k
                dve.wait_ge(all_max_ready, START + F + 1)
                nc.vector.reciprocal(inv_max[:, :], all_max[:, :]).then_inc(inv_ready, 1)
                dve.wait_ge(inv_ready, START + F + 1)
                dve.wait_ge(p_exp, START + F * TB)
                nc.vector.tensor_scalar(p_scale[:, :], v_last[f[1]][:, bass.ds(k * TB, TB)], ATT_SCALE, inv_max[:, 0:1],
                                        ALU.mult, ALU.mult).then_inc(scale_ready, 1)

            def p_low_part(f, k, half):
                dve.wait_ge(p_high, START + f[0] * (2 * UH) + k * 2 + (half + 1))
                if half == 0:
                    dve.wait_ge(pv_ready, START + f[0] * UH + k)
                c = slice(half * TB // 2, (half + 1) * TB // 2)
                nc.vector.tensor_tensor(p_l[:, c, :], probs[:, c, :], p_h[:, c, :], ALU.subtract).then_inc(p_ready, 1)

            def normalise(f, k):
                F = f[0] * UH + k
                dve.wait_ge(pv_ready, START + F + 1)
                nc.vector.tensor_reduce(num[:, :, :], pv[:, :, 0:3 * HD].rearrange("p b (w d) -> p b d w", w=3), AX_X,
                                        ALU.add).then_inc(summed_up, 1)
                nc.vector.reciprocal(den[:, :, :], pv[:, :, 3 * HD:VW]).then_inc(summed_up, 1)
                dve.wait_ge(summed_up, START + F * 2 + 2)
                dve.wait_ge(att_out[f[1]], START + f[2] * 16)
                nc.vector.tensor_tensor(att_sb[f[1]][:, :, bass.ds(k, 1), :].rearrange("p b a d -> p b (a d)"), num[:, :, :],
                                        den[:, :, :].to_broadcast([P, TB, HD]), ALU.mult).then_inc(att_ready, 1)

            def head(n, f, b, k):
                if f:
                    times_u(f, k, (0, 1))
                if n:
                    turn(n, 0, k * 3 + 1)
                if f:
                    times_u(f, k, (2, 3))
                if n:
                    turn(n, 1, k * 3 + 1)
                if f:
                    scale_plan(f, k)
                if n:
                    turn(n, 0, k * 3 + 2)
                    turn(n, 1, k * 3 + 2)
                if f:
                    p_low_part(f, k, 0)
                if n:
                    turn(n, 0, k * 3 + 3)
                if f:
                    p_low_part(f, k, 1)
                if n:
                    turn(n, 1, k * 3 + 3)
                if f:
                    normalise(f, k)

            def last(n, b):
                if b:
                    first_x(b)
                for g in range(2):
                    turn(n, g, STEPS_X, keep=False)

            units(dve, head, last, lambda: first_x((0, 0)))

FB = FFN // P
LN_EPS = 1e-5
R = 3


def mix(nc, h, att, ident, w):
    with ExitStack() as ctx:
        sb = lambda name, shape, dt: ctx.enter_context(nc.sbuf_tensor(name, shape, dt))
        ps = lambda name, shape, dt: ctx.enter_context(nc.psum_tensor(name, shape, dt))
        counters = []

        def sem(name):
            counters.append(ctx.enter_context(nc.semaphore(name)))
            return counters[-1]

        REST, HALF = DIM - P, DIM // 2
        raw = sb("raw", [P, EXPERTS * FB * DIM], F32)
        raw1_a = raw[:, 0:EXPERTS * FFN].rearrange("p (e f) -> p e f", e=EXPERTS)
        raw2 = raw[:, :].rearrange("p (e d) -> p e d", d=DIM)
        raw1_b = sb("raw1_b", [P, EXPERTS, FFN], F32)
        w1 = sb("w1", [P, EXPERTS, 3, FFN], F16)
        w2 = sb("w2", [P, EXPERTS * FB, 2, DIM], F16)
        maxes, all_maxes = sb("maxes", [P, 3], F32), sb("all_maxes", [P, 3], F32)
        scale, unscale, tmp = sb("scale4", [P, 2], F32), sb("unscale4", [P, 2], F32), sb("tmp4", [P, 2], F32)
        small = {}
        for name, src in w["small"].items():
            small[name] = sb("c_" + name, list(src.shape), F32)
        eye = sb("eye4", [P, P], F32)
        eps, idle = sb("eps", [P, 1], F32), sb("idle4", [P, 1], F32)
        h_sb, att_sb = sb("h_sb4", [P, TB, DIM], F32), sb("att_sb4", [P, TB, DIM], F32)
        at_a, at_b = sb("at_a", [P, TOKENS], F32), sb("at_b", [REST, TOKENS], F32)
        z = sb("z", [P, TB, DIM], F32)
        stats, mean_var = sb("stats", [P, TB, 6], F32), sb("mean_var", [P, TB, 2], F32)
        std, inv_std = sb("std", [P, TB], F32), sb("inv_std", [P, TB], F32)
        x = sb("x4", [P, TB, 2 * P], F32)
        xt_a, xt_m = sb("xt_a", [P, TOKENS], F32), sb("xt_m", [P, TOKENS], F32)
        xh_a = [sb(f"xh_a{a}", [P, TOKENS], F16) for a in range(2)]
        xl_a = [sb(f"xl_a{a}", [P, TOKENS], F16) for a in range(2)]
        xh_m = [sb(f"xh_m{a}", [P, TOKENS], F16) for a in range(2)]
        xl_m = [sb(f"xl_m{a}", [REST, TOKENS], F16) for a in range(2)]
        hidden = sb("hidden", [HALF, 2, TOKENS], F32)
        score = sb("score", [P, TB, EXPERTS], F32)
        best, where = sb("best", [P, TB, 8], F32), sb("where", [P, TB, 8], U32)
        pick = sb("pick", [P, TB, 2], F32)
        gap, ratio, total = sb("gap", [P, TB], F32), sb("ratio", [P, TB], F32), sb("total", [P, TB], F32)
        share = sb("share", [P, 2, TB], F32)
        route, route2 = sb("route", [P, TB, EXPERTS], F32), sb("route2", [P, TB, EXPERTS], F32)
        route_t = sb("route_t", [EXPERTS, TOKENS], F32)
        gate = [sb(f"gate{a}", [P, TB, EXPERTS], F32) for a in range(2)]
        acc = [sb(f"acc4{a}", [P, TB, DIM], F32) for a in range(2)]
        mid = [sb(f"mid{n}", [P, TOKENS], F32) for n in range(R)]
        mid_h = [sb(f"mid_h{n}", [P, TOKENS], F16) for n in range(R)]
        mid_l = [sb(f"mid_l{n}", [P, TOKENS], F16) for n in range(R)]
        zeros = sb("zeros", [P, 2 * DIM], F16)
        hb_sb = sb("hb_sb", [P, TB, DIM], F32)
        stats2, mean_var2 = sb("stats2", [P, TB, 6], F32), sb("mean_var2", [P, TB, 2], F32)
        std2, inv_std2 = sb("std2", [P, TB], F32), sb("inv_std2", [P, TB], F32)
        out_sb = sb("out_sb", [P, TB, DIM], F32)
        up_ps = [ps(f"up_ps{n}", [P, TOKENS], F32) for n in range(R)]
        down = ps("down", [P, TB, 256], F32)
        misc = ps("misc", [P, 2, 512], F32)
        rows4 = misc[:, :, :].rearrange("p a (b n) -> p (a b) n", b=2)[:, :, 0:DIM]

        raw_in, maxed, all_maxed, own, w_ready, eps_set = (
            sem("raw_in"), sem("maxed4"), sem("all_maxed"), sem("own4"), sem("w_ready4"), sem("eps_set"))
        small_in, w1_split, raw2_in = sem("small_in"), sem("w1_split"), sem("raw2_in")
        h_in, att_in, out_done = sem("h_in4"), sem("att_in4"), sem("out_done")
        turned, turned_read = sem("turned4"), sem("turned_read")
        projected, z_steps, z_ready, std_ready = sem("projected"), sem("z_steps"), sem("z_ready"), sem("std_ready")
        x_steps, x_ready = sem("x_steps4"), sem("x_ready4")
        x_turned, xt_ready, x_split = sem("x_turned"), sem("xt_ready"), sem("x_split")
        hidden_up, hidden_ready, scored, score_steps, gap_ready, ratio_ready = (
            sem("hidden_up"), sem("hidden_ready"), sem("scored"), sem("score_steps"), sem("gap_ready"), sem("ratio_ready"))
        route_steps, route_ready, route_turned, route_t_ready, biased, acc_ready = (
            sem("route_steps"), sem("route_ready"), sem("route_turned"), sem("route_t_ready"), sem("biased"), sem("acc_ready"))
        down_ready = sem("down_ready")
        acc_steps, end_steps, end_var, end_std, out_ready = (
            sem("acc_steps"), sem("end_steps"), sem("end_var"), sem("end_std"), sem("out_ready"))
        hb_ready = sem("hb_ready")
        ring = lambda name: [sem(f"{name}{n}") for n in range(R)]
        up_ready, mid_parts, mid_split, mid_used = ring("up_ready"), ring("mid_parts"), ring("mid_split"), ring("mid_used")
        NB = EXPERTS * FB
        LAPS = NB // R
        block = ctx.enter_context(nc.Block())

        def images(eng, step, front, late):
            for t in sorted(front):
                front[t](0, 0)

            def image(i, a, before=True, ahead=True):
                for t in range(NB):
                    step(i, a, t, ahead)
                    if before and t in late:
                        late[t](i - 1, 1 - a)
                    if ahead and t in front:
                        front[t](i + 1, 1 - a)

            image(0, 0, before=False)
            with eng.Fori(0, IMAGES // 2 - 1) as pair:
                image(pair * 2 + 1, 1)
                image(pair * 2 + 2, 0)
            image(IMAGES - 1, 1, ahead=False)
            for t in sorted(late):
                late[t](IMAGES - 1, 1)

        def parts_used(eng, i, t):
            n, rest = t % R, FB // R
            if n < R - 1:
                eng.wait_ge(mid_used[n], START + i * LAPS + t // R)
            elif (t // R) % rest == 0:
                eng.wait_ge(down_ready, START + i * (EXPERTS * TB // 2) + t // FB * (TB // 2))
            else:
                eng.wait_ge(mid_used[n], START + i * (LAPS - EXPERTS) + (t // FB * (rest - 1) + (t // R) % rest))

        @block.sync
        def _(sp):
            for counter in counters:
                sp.sem_inc(counter, START)
            sp.dma_start(raw[:, 0:EXPERTS * FFN], w["w1_a"]).then_inc(raw_in, 16)
            sp.dma_start(raw1_b[:, :, :].rearrange("p a b -> p (a b)"), w["w1_b"]).then_inc(raw_in, 16)
            for name, src in w["small"].items():
                sp.dma_start(small[name][:, :] if len(src.shape) == 2 else small[name][:, :, :], src).then_inc(small_in, 16)
            sp.dma_start(eye[:, :], ident).then_inc(small_in, 16)

            def load(j):
                sp.dma_start(h_sb[:, :, :], (h[bass.ds(j, 1), :, :, :]).rearrange("a p b d -> (a p) b d")).then_inc(h_in, 16)
                sp.dma_start(att_sb[:, :, :], att[bass.ds(j, 1), :, :, :].rearrange("a p b d -> (a p) b d")).then_inc(att_in, 16)

            def store(i):
                sp.wait_ge(out_ready, START + i + 1)
                sp.dma_start(w["out"][bass.ds(i, 1), :, :, :].rearrange("a p b d -> (a p) b d"), out_sb[:, :, :]).then_inc(out_done, 16)

            load(0)
            sp.wait_ge(w1_split, START + 1)
            sp.dma_start(raw[:, :], w["w2"]).then_inc(raw2_in, 16)
            sp.wait_ge(z_ready, START + 1)
            load(1)
            with sp.Fori(0, IMAGES - 2) as i:
                sp.wait_ge(z_ready, START + i + 2)
                load(i + 2)
                store(i)
            store(IMAGES - 2)
            store(IMAGES - 1)
            sp.wait_ge(out_done, START + 16 * IMAGES)

        @block.gpsimd
        def _(pool):
            pool.wait_ge(maxed, START + 2)
            nc.gpsimd.partition_all_reduce(all_maxes[:, 0:2], maxes[:, 0:2], P, RMAX).then_inc(all_maxed, 1)
            pool.wait_ge(maxed, START + 3)
            nc.gpsimd.partition_all_reduce(all_maxes[:, 2:3], maxes[:, 2:3], P, RMAX).then_inc(all_maxed, 1)
            pool.wait_ge(small_in, START + 16 * (len(small) + 1))
            with pool.Fori(0, IMAGES) as j:
                pool.wait_ge(h_in, START + (j + 1) * 16)
                pool.wait_ge(z_ready, START + j)
                nc.gpsimd.tensor_tensor(hb_sb[:, :, :], h_sb[:, :, :],
                                        small["b_proj"][:, :].unsqueeze(1).to_broadcast([P, TB, DIM]), ALU.add).then_inc(hb_ready, 1)

        @block.tensor
        def _(pe):
            pe.wait_ge(w_ready, START + 1)
            pe.wait_ge(eps_set, START + 2)
            pe.wait_ge(small_in, START + 16 * (len(small) + 1))

            def up(i, a, t):
                e, f, n = t // FB, t % FB, t % R
                if t == 0:
                    pe.wait_ge(x_split, START + (i + 1) * 4)
                pe.wait_ge(mid_parts[n], START + i * (2 * LAPS) + 2 * (t // R))
                cols = slice(f * P, (f + 1) * P)
                nc.tensor.matmul(up_ps[n][:, :], w1[:, e, 0, cols], xh_a[a][:, :], start=True, stop=False)
                nc.tensor.matmul(up_ps[n][:, :], w1[:, e, 0, cols], xl_a[a][:, :], start=False, stop=False)
                nc.tensor.matmul(up_ps[n][:, :], w1[:, e, 1, cols], xh_a[a][:, :], start=False, stop=False)
                nc.tensor.matmul(up_ps[n][:, :], w1[:, e, 2, cols], xh_m[a][:, :], start=False, stop=False)
                nc.tensor.matmul(up_ps[n][:, :], w1[0:REST, e, 2, cols], xl_m[a][:, :], start=False, stop=True).then_inc(up_ready[n], 1)

            def down_block(i, a, t):
                e, f, n = t // FB, t % FB, t % R
                pe.wait_ge(mid_split[n], START + i * LAPS + (t // R + 1))
                for b in range(TB):
                    if f == 0 and b % 2 == 0 and not (isinstance(i, int) and i == 0 and e == 0):
                        pe.wait_ge(acc_steps, START + i * (EXPERTS * TB) + ((e - 1) * TB + b + 2))
                    rows = slice(b * P, (b + 1) * P)
                    out = down[:, b, 0:DIM]
                    if f == 0 and b % 2 == 0:
                        nc.tensor.matmul(down[:, b:b + 2, 0:DIM], zeros[:, 0:P], zeros[:, :], start=True, stop=False)
                    nc.tensor.matmul(out, mid_h[n][:, rows], w2[:, t, 0, :], start=False, stop=False)
                    nc.tensor.matmul(out, mid_h[n][:, rows], w2[:, t, 1, :], start=False, stop=False)
                    last = nc.tensor.matmul(out, mid_l[n][:, rows], w2[:, t, 0, :], start=False, stop=(f == FB - 1 and b % 2 == 1))
                    if f == FB - 1 and b % 2:
                        last.then_inc(down_ready, 1)
                if f < FB - 1:
                    last.then_inc(mid_used[n], 1)

            def step(i, a, t, ahead):
                if isinstance(i, int) and i == 0 and t == 0:
                    up(i, a, 0)
                    up(i, a, 1)
                if t + 2 < NB:
                    up(i, a, t + 2)
                elif ahead:
                    up(i + 1, 1 - a, t + 2 - NB)
                down_block(i, a, t)

            def turn_att(j, a):
                pe.wait_ge(att_in, START + (j + 1) * 16)
                pe.wait_ge(acc_ready, START + j)
                for b in range(TB):
                    nc.tensor.transpose(misc[:, 0, b * P:(b + 1) * P], att_sb[:, b, 0:P], eye[:, :])
                    last = nc.tensor.transpose(misc[0:REST, 1, b * P:(b + 1) * P], att_sb[:, b, P:DIM], eye[:, :])
                last.then_inc(turned, 1)

            def project_att(j, a):
                pe.wait_ge(turned_read, START + j * 2 + 2)
                for b in range(TB):
                    rows = slice(b * P, (b + 1) * P)
                    nc.tensor.matmul(rows4[:, b, :], at_a[:, rows], small["wp_a"][:, :], start=True, stop=False)
                    last = nc.tensor.matmul(rows4[:, b, :], at_b[:, rows], small["wp_b"][:, :], start=False, stop=True)
                last.then_inc(projected, 1)

            def turn_x(j, a):
                pe.wait_ge(x_ready, START + j + 1)
                for b in range(TB):
                    nc.tensor.transpose(misc[:, 0, b * P:(b + 1) * P], x[:, b, 0:P], eye[:, :])
                    last = nc.tensor.transpose(misc[:, 1, b * P:(b + 1) * P], x[:, b, P:2 * P], eye[:, :])
                last.then_inc(x_turned, 1)

            def router_hidden(j, a):
                pe.wait_ge(xt_ready, START + j * 2 + 2)
                for half in range(2):
                    cols = slice(half * HALF, (half + 1) * HALF)
                    nc.tensor.matmul(misc[0:HALF, half, :], small["wr1_a"][:, cols], xt_a[:, :], start=True, stop=False)
                    last = nc.tensor.matmul(misc[0:HALF, half, :], small["wr1_b"][:, cols], xt_m[0:REST, :], start=False, stop=True)
                last.then_inc(hidden_up, 1)

            def router_score(j, a):
                pe.wait_ge(hidden_ready, START + j * 2 + 2)
                for b in range(TB):
                    for half in range(2):
                        last = nc.tensor.matmul(misc[:, 0, b * EXPERTS:(b + 1) * EXPERTS], hidden[:, half, b * P:(b + 1) * P],
                                                small["wr2"][:, half, :], start=(half == 0), stop=(half == 1))
                last.then_inc(scored, 1)

            def turn_route(j, a):
                pe.wait_ge(route_ready, START + j + 1)
                for b in range(TB):
                    last = nc.tensor.transpose(misc[0:EXPERTS, 0, b * P:(b + 1) * P], route[:, b, :], eye[:, :])
                last.then_inc(route_turned, 1)

            def mixed_bias(j, a):
                pe.wait_ge(route_t_ready, START + j + 1)
                for b in range(TB):
                    last = nc.tensor.matmul(rows4[:, b, :], route_t[:, b * P:(b + 1) * P], small["b2"][:, :], start=True, stop=True)
                last.then_inc(biased, 1)

            images(pe, step, {0: turn_att, 6: project_att, 16: turn_x, 20: router_hidden, 25: router_score,
                              34: turn_route, 38: mixed_bias}, {})

        @block.scalar
        def _(act):
            act.wait_ge(w_ready, START + 1)
            act.wait_ge(small_in, START + 16 * (len(small) + 1))

            def step(i, a, t, ahead):
                n = t % R
                act.wait_ge(up_ready[n], START + i * LAPS + (t // R + 1))
                act.wait_ge(mid_split[n], START + i * LAPS + t // R)
                parts_used(act, i, t)
                nc.scalar.activation(mid[n][:, :], up_ps[n][:, :], ACT.Relu, bias=small["b1"][:, t:t + 1],
                                     scale=unscale[:, 0:1]).then_inc(mid_parts[n], 1)
                nc.scalar.activation(mid_h[n][:, :], up_ps[n][:, :], ACT.Relu, bias=small["b1"][:, t:t + 1],
                                     scale=unscale[:, 0:1]).then_inc(mid_parts[n], 1)

            def read_turned(j, a):
                act.wait_ge(turned, START + j + 1)
                act.wait_ge(projected, START + j)
                nc.scalar.activation(at_a[:, :], misc[:, 0, :], ACT.Copy).then_inc(turned_read, 1)
                nc.scalar.activation(at_b[:, :], misc[0:REST, 1, :], ACT.Copy).then_inc(turned_read, 1)

            def deviation(j, a):
                act.wait_ge(z_ready, START + j + 1)
                nc.scalar.activation(std[:, :], mean_var[:, :, 1], ACT.Sqrt, bias=eps[:, 0:1]).then_inc(std_ready, 1)

            def read_x(j, a):
                act.wait_ge(x_turned, START + j + 1)
                act.wait_ge(hidden_up, START + j)
                act.wait_ge(x_split, START + j * 4)
                nc.scalar.activation(xt_a[:, :], misc[:, 0, :], ACT.Copy).then_inc(xt_ready, 1)
                nc.scalar.activation(xt_m[:, :], misc[:, 1, :], ACT.Copy).then_inc(xt_ready, 1)

            def router_relu(j, a):
                act.wait_ge(hidden_up, START + j + 1)
                act.wait_ge(scored, START + j)
                for half in range(2):
                    nc.scalar.activation(hidden[:, half, :], misc[0:HALF, half, :], ACT.Relu,
                                         bias=small["br1"][:, half:half + 1]).then_inc(hidden_ready, 1)

            def gap_exp(j, a):
                act.wait_ge(gap_ready, START + j + 1)
                nc.scalar.activation(ratio[:, :], gap[:, :], ACT.Exp).then_inc(ratio_ready, 1)

            def read_route(j, a):
                act.wait_ge(route_turned, START + j + 1)
                act.wait_ge(biased, START + j)
                nc.scalar.activation(route_t[:, :], misc[0:EXPERTS, 0, :], ACT.Copy).then_inc(route_t_ready, 1)

            def end(i, a):
                act.wait_ge(end_var, START + i + 1)
                nc.scalar.activation(std2[:, :], mean_var2[:, :, 1], ACT.Sqrt, bias=eps[:, 0:1]).then_inc(end_std, 1)

            images(act, step, {3: read_turned, 11: deviation, 18: read_x, 22: router_relu, 29: gap_exp, 36: read_route}, {2: end})

        @block.vector
        def _(dve):
            done = Done(dve, own)
            nc.vector.memset(eps[:, :], LN_EPS).then_inc(eps_set, 1)
            nc.vector.memset(zeros[:, :], 0.0).then_inc(eps_set, 1)
            dve.wait_ge(raw_in, START + 32)
            for c, part in enumerate((raw1_a, raw1_b[:, :, :])):
                nc.vector.tensor_reduce(maxes[:, c:c + 1], part.rearrange("p a b -> p (a b)"), AX_X, ALU.max,
                                        apply_absolute_value=True).then_inc(maxed, 1)
            dve.wait_ge(all_maxed, START + 1)
            done(nc.vector.tensor_tensor(all_maxes[:, 1:2], all_maxes[:, 0:1], all_maxes[:, 1:2], ALU.max))
            power_of_two_scale(nc.vector, done, all_maxes[:, 1:2], scale[:, 0:1], unscale[:, 0:1], tmp[:, 0:1])
            done(nc.vector.tensor_scalar(w1[:, :, 0, :], raw1_a, scale[:, 0:1], None, ALU.mult))
            done(nc.vector.scalar_tensor_tensor(w1[:, :, 1, :], raw1_a, scale[:, 0:1], w1[:, :, 0, :], ALU.mult, ALU.subtract))
            nc.vector.memset(tmp[:, 1:2], 0.0).then_inc(w1_split, 1)
            done(nc.vector.tensor_scalar(w1[:, :, 2, :], raw1_b[:, :, :], scale[:, 0:1], None, ALU.mult))
            done(nc.vector.scalar_tensor_tensor(w1[REST:P, :, 2, :], raw1_b[REST:P, :, :], scale[REST:P, 0:1], w1[REST:P, :, 2, :],
                                                ALU.mult, ALU.subtract))
            dve.wait_ge(raw2_in, START + 16)
            nc.vector.tensor_reduce(maxes[:, 2:3], raw[:, :], AX_X, ALU.max, apply_absolute_value=True).then_inc(maxed, 1)
            dve.wait_ge(all_maxed, START + 2)
            power_of_two_scale(nc.vector, done, all_maxes[:, 2:3], scale[:, 1:2], unscale[:, 1:2], tmp[:, 1:2])
            done(nc.vector.tensor_scalar(w2[:, :, 0, :], raw2, scale[:, 1:2], None, ALU.mult))
            nc.vector.scalar_tensor_tensor(w2[:, :, 1, :], raw2, scale[:, 1:2], w2[:, :, 0, :],
                                           ALU.mult, ALU.subtract).then_inc(w_ready, 1)
            dve.wait_ge(w_ready, START + 1)
            dve.wait_ge(small_in, START + 16 * (len(small) + 1))

            def read_down(i, a, e):
                dve.wait_ge(acc_ready, START + i + 1)
                dve.wait_ge(acc_steps, START + i * (EXPERTS * TB) + e * TB)
                for b in range(TB):
                    if b % 2 == 0:
                        dve.wait_ge(down_ready, START + i * (EXPERTS * TB // 2) + (e * TB // 2 + b // 2 + 1))
                    nc.vector.scalar_tensor_tensor(acc[a][:, b, :], down[:, b, 0:DIM], gate[a][:, b, e:e + 1], acc[a][:, b, :],
                                                   ALU.mult, ALU.add).then_inc(acc_steps, 1)

            def step(i, a, t, ahead):
                n, e = t % R, t // FB
                dve.wait_ge(mid_parts[n], START + i * (2 * LAPS) + 2 * (t // R + 1))
                nc.vector.tensor_tensor(mid_l[n][:, :], mid[n][:, :], mid_h[n][:, :], ALU.subtract).then_inc(mid_split[n], 1)
                if t % FB == 0 and t:
                    read_down(i, a, e - 1)

            def residual(j, a):
                dve.wait_ge(projected, START + j + 1)
                dve.wait_ge(hb_ready, START + j + 1)
                nc.vector.tensor_tensor(z[:, :, :], rows4, hb_sb[:, :, :], ALU.add).then_inc(z_steps, 1)

            def statistics(j, a):
                dve.wait_ge(z_steps, START + j * 5 + 1)
                for b in range(TB):
                    nc.vector.bn_stats(stats[:, b, :], z[:, b, :]).then_inc(z_steps, 1)
                dve.wait_ge(z_steps, START + j * 5 + 5)
                nc.vector.memset(idle[:, :], 0.0)
                for b in range(TB):
                    last = nc.vector.bn_aggr(mean_var[:, b, :], stats[:, b, :])
                last.then_inc(z_ready, 1)
                dve.wait_ge(z_ready, START + j + 1)

            def normalise(j, a):
                dve.wait_ge(std_ready, START + j + 1)
                nc.vector.reciprocal(inv_std[:, :], std[:, :]).then_inc(x_steps, 1)
                dve.wait_ge(x_steps, START + j * 2 + 1)
                dve.wait_ge(x_turned, START + j)
                for b in range(TB):
                    last = nc.vector.tensor_scalar(x[:, b, 0:DIM], z[:, b, :], mean_var[:, b, 0:1], inv_std[:, b:b + 1],
                                                   ALU.subtract, ALU.mult)
                last.then_inc(x_steps, 1)
                dve.wait_ge(x_steps, START + j * 2 + 2)
                nc.vector.tensor_copy(x[:, :, DIM:2 * P], x[:, :, P:DIM]).then_inc(x_ready, 1)

            def split_x(j, a):
                dve.wait_ge(xt_ready, START + j * 2 + 2)
                if not (isinstance(j, int) and j == 0):
                    for n in range(R):
                        dve.wait_ge(up_ready[n], START + (j - 1) * LAPS)
                nc.vector.tensor_copy(xh_a[a][:, :], xt_a[:, :]).then_inc(x_split, 1)
                nc.vector.tensor_copy(xh_m[a][:, :], xt_m[:, :]).then_inc(x_split, 1)

            def split_x_low(j, a):
                dve.wait_ge(x_split, START + j * 4 + 2)
                nc.vector.tensor_tensor(xl_a[a][:, :], xt_a[:, :], xh_a[a][:, :], ALU.subtract).then_inc(x_split, 1)
                nc.vector.tensor_tensor(xl_m[a][:, :], xt_m[0:REST, :], xh_m[a][0:REST, :], ALU.subtract).then_inc(x_split, 1)

            def best_two(j, a):
                S = 10
                dve.wait_ge(scored, START + j + 1)
                nc.vector.tensor_tensor(score[:, :, :], misc[:, 0, 0:TB * EXPERTS].rearrange("p (b e) -> p b e", b=TB),
                                        small["br2"][:, :].unsqueeze(1).to_broadcast([P, TB, EXPERTS]), ALU.add).then_inc(score_steps, 1)
                dve.wait_ge(score_steps, START + j * S + 1)
                nc.vector.memset(idle[:, :], 0.0)
                for b in range(TB):
                    nc.vector.max(best[:, b, :], score[:, b, :]).then_inc(score_steps, 1)

            def best_where(j, a):
                S = 10
                dve.wait_ge(score_steps, START + j * S + 5)
                nc.vector.memset(idle[:, :], 0.0)
                for b in range(TB):
                    nc.vector.max_index(where[:, b, :], best[:, b, :], score[:, b, :]).then_inc(score_steps, 1)
                nc.vector.tensor_tensor(gap[:, :], best[:, :, 1], best[:, :, 0], ALU.subtract).then_inc(gap_ready, 1)
                dve.wait_ge(score_steps, START + j * S + 9)
                nc.vector.tensor_copy(pick[:, :, :], where[:, :, 0:2]).then_inc(score_steps, 1)
                dve.wait_ge(score_steps, START + j * S + 10)

            def routing(j, a):
                S = 5
                dve.wait_ge(ratio_ready, START + j + 1)
                nc.vector.tensor_scalar(total[:, :], ratio[:, :], 1.0, None, ALU.add).then_inc(route_steps, 1)
                dve.wait_ge(route_steps, START + j * S + 1)
                nc.vector.reciprocal(share[:, 0, :], total[:, :]).then_inc(route_steps, 1)
                dve.wait_ge(route_steps, START + j * S + 2)
                nc.vector.tensor_tensor(share[:, 1, :], ratio[:, :], share[:, 0, :], ALU.mult).then_inc(route_steps, 1)
                dve.wait_ge(route_steps, START + j * S + 3)
                for b in range(TB):
                    nc.vector.tensor_scalar(route[:, b, :], small["numbers"][:, :], pick[:, b, 0:1], share[:, 0, b:b + 1],
                                            ALU.is_equal, ALU.mult)
                    last = nc.vector.tensor_scalar(route2[:, b, :], small["numbers"][:, :], pick[:, b, 1:2], share[:, 1, b:b + 1],
                                                   ALU.is_equal, ALU.mult)
                last.then_inc(route_steps, 1)
                dve.wait_ge(route_steps, START + j * S + 4)
                nc.vector.tensor_tensor(route[:, :, :], route[:, :, :], route2[:, :, :], ALU.add).then_inc(route_ready, 1)
                dve.wait_ge(route_ready, START + j + 1)
                nc.vector.tensor_scalar(gate[a][:, :, :], route[:, :, :], unscale[:, 1:2], None, ALU.mult).then_inc(route_steps, 1)

            def begin_acc(j, a):
                dve.wait_ge(biased, START + j + 1)
                nc.vector.tensor_tensor(acc[a][:, :, :], x[:, :, 0:DIM], rows4, ALU.add).then_inc(acc_ready, 1)

            def last_down(i, a):
                read_down(i, a, EXPERTS - 1)

            def end_statistics(i, a):
                S = 5
                dve.wait_ge(acc_steps, START + (i + 1) * (EXPERTS * TB))
                for b in range(TB):
                    nc.vector.bn_stats(stats2[:, b, :], acc[a][:, b, :]).then_inc(end_steps, 1)
                dve.wait_ge(end_steps, START + i * S + 4)
                nc.vector.memset(idle[:, :], 0.0)
                for b in range(TB):
                    last = nc.vector.bn_aggr(mean_var2[:, b, :], stats2[:, b, :])
                last.then_inc(end_var, 1)

            def end_scale(i, a):
                S = 5
                dve.wait_ge(end_std, START + i + 1)
                nc.vector.reciprocal(inv_std2[:, :], std2[:, :]).then_inc(end_steps, 1)
                dve.wait_ge(end_steps, START + i * S + 5)
                dve.wait_ge(out_done, START + i * 16)
                for b in range(TB):
                    last = nc.vector.tensor_scalar(out_sb[:, b, :], acc[a][:, b, :], mean_var2[:, b, 0:1], inv_std2[:, b:b + 1],
                                                   ALU.subtract, ALU.mult)
                last.then_inc(out_ready, 1)

            images(dve, step, {9: residual, 10: statistics, 13: normalise, 20: split_x, 21: split_x_low, 27: best_two,
                               28: best_where, 31: routing, 41: begin_acc},
                   {0: last_down, 1: end_statistics, 4: end_scale})


def tower(nc, x, freqs, w_tok, wqv, ident, mix_w):
    scratch = lambda name, shape, dt: nc.dram_tensor(name, shape, dt, kind="Internal").ap()
    h = scratch("h_tokens", (IMAGES, P, TB, DIM), F32)
    q_parts = scratch("q_parts", (IMAGES, 2, 2, DIM // 2, TOKENS), F16)
    v_parts = scratch("v_parts", (IMAGES, P, TB * HEADS * VW), BF16)
    att = scratch("att_tokens", (IMAGES, P, TB, DIM), F32)
    embed(nc, x, freqs, w_tok, h)
    project(nc, h, wqv, ident, q_parts, v_parts)
    attend(nc, q_parts, v_parts, ident, att)
    mix(nc, h, att, ident, mix_w)


def layouts(x, L0_tok_freq_bands, L0_tok_W, L0_attn_w_qkv, L0_attn_w_proj, L0_attn_b_proj, L0_ffn_W1, L0_ffn_b1,
            L0_ffn_W2, L0_ffn_b2, L0_ffn_Wr1, L0_ffn_br1, L0_ffn_Wr2, L0_ffn_br2):
    whole = np.ascontiguousarray
    xt = x.reshape(IMAGES, TOKENS, PATCH).transpose(0, 2, 1)
    blocks = xt[:, :FULL * P].reshape(IMAGES, FULL, P, TOKENS).transpose(0, 2, 1, 3)
    rest = np.concatenate([xt[:, FULL * P:]] * 2, axis=1)[:, :, None]
    freqs = np.zeros((P, BANDS + BANDS // 2), np.float32)
    freqs[:, :BANDS] = L0_tok_freq_bands
    freqs[:P // 2, BANDS:] = L0_tok_freq_bands[0::2]
    freqs[P // 2:, BANDS:] = L0_tok_freq_bands[1::2]
    w = L0_tok_W.reshape(DIM, PATCH, 2 * BANDS)
    w_tok = []
    for b, s in CHUNKS:
        for t in range(2):
            if s < FULL:
                w_tok.append(w[:, s * P:(s + 1) * P, b + BANDS * t].T)
            else:
                w_tok.append(np.concatenate([w[:, FULL * P:, b - 1 + BANDS * t].T, w[:, FULL * P:, b + BANDS * t].T]))
    w1 = L0_ffn_W1.transpose(2, 0, 1)
    rows = lambda a: whole(np.broadcast_to(a, (P, a.size)))
    return {
        "x": whole(np.concatenate([blocks, rest], axis=2).reshape(IMAGES, P, WIDE)),
        "freqs": freqs,
        "w_tok": whole(np.stack(w_tok, axis=1).reshape(P, NCH * DIM)),
        "wqv": whole(np.concatenate([L0_attn_w_qkv[:DIM], L0_attn_w_qkv[2 * DIM:]]).T),
        "ident": np.eye(P, dtype=np.float32),
        "w1_a": whole(w1[:P].reshape(P, -1)),
        "w1_b": whole(np.concatenate([w1[P:], w1[P:]]).reshape(P, -1)),
        "w2": whole(L0_ffn_W2.reshape(EXPERTS, DIM, FB, P).transpose(3, 0, 2, 1).reshape(P, -1)),
        "small_b1": whole(L0_ffn_b1.reshape(EXPERTS * FB, P).T),
        "small_b2": whole(L0_ffn_b2),
        "small_wp_a": whole(L0_attn_w_proj.T[:P]),
        "small_wp_b": whole(L0_attn_w_proj.T[P:]),
        "small_wr1_a": whole(L0_ffn_Wr1.T[:P]),
        "small_wr1_b": whole(L0_ffn_Wr1.T[P:]),
        "small_br1": whole(L0_ffn_br1.reshape(2, DIM // 2).T),
        "small_wr2": whole(L0_ffn_Wr2.T.reshape(2, DIM // 2, EXPERTS).transpose(1, 0, 2)),
        "small_br2": rows(L0_ffn_br2),
        "small_b_proj": rows(L0_attn_b_proj),
        "small_numbers": rows(np.arange(EXPERTS, dtype=np.float32)),
    }


def kernel(**inputs):
    import concourse.bacc as bacc
    from concourse.bass_utils import run_bass_kernel_spmd as run

    nc = bacc.Bacc("TRN2", target_bir_lowering=False, num_devices=1)
    arrays, aps = {}, {}
    for name, a in layouts(**{n: np.asarray(a) for n, a in inputs.items()}).items():
        arrays[f"in_{name}_dram"] = a
        aps[name] = nc.dram_tensor(f"in_{name}_dram", a.shape, mybir.dt.from_np(a.dtype), kind="ExternalInput").ap()
    out = nc.dram_tensor("out_0_dram", (IMAGES, P, TB, DIM), F32, kind="ExternalOutput").ap()
    mix_w = {n: aps[n] for n in ("w1_a", "w1_b", "w2")}
    mix_w["small"] = {n[len("small_"):]: a for n, a in aps.items() if n.startswith("small_")}
    mix_w["out"] = out
    tower(nc, aps["x"], aps["freqs"], aps["w_tok"], aps["wqv"], aps["ident"], mix_w)
    got = run(nc, [arrays], core_ids=[0]).results[0]["out_0_dram"]
    return got.transpose(0, 2, 1, 3).reshape(IMAGES, TOKENS, DIM)
```

```python
from contextlib import ExitStack

import numpy as np

import concourse.bass as bass
from concourse import mybir

F32 = mybir.dt.float32
F16 = mybir.dt.float16
BF16 = mybir.dt.bfloat16
I32 = mybir.dt.int32
U32 = mybir.dt.uint32
ALU = mybir.AluOpType
ACT = mybir.ActivationFunctionType
AX_X = mybir.AxisListType.X
RMAX = bass.bass_isa.ReduceOp.max

P = 128
START = 1
IMAGES, TOKENS, DIM, HEADS, BANDS = 16, 512, 192, 12, 6
HD = DIM // HEADS
EXPERTS, FFN = 8, 4 * DIM
PATCH = 3 * TOKENS * DIM // TOKENS
VW = 3 * HD + 1
FULL = PATCH // P
TB = TOKENS // P
SLOTS = FULL + 1
CHUNKS = [(b, s) for b in range(BANDS) for s in range(FULL + b % 2)]
NCH = 2 * len(CHUNKS)
WIDE = SLOTS * TOKENS
Q_SCALE = 64.0
TURN = float(np.nextafter(np.float32(2 * np.pi), np.float32(0)))


class Done:

    def __init__(self, engine, sem):
        self.engine, self.sem, self.n = engine, sem, 0

    def __call__(self, instruction):
        self.n += 1
        instruction.then_inc(self.sem, 1)
        self.engine.wait_ge(self.sem, START + self.n)


def power_of_two_scale(vector, done, own, scale, unscale, tmp):
    done(vector.tensor_scalar(tmp.bitcast(I32), own.bitcast(I32), 0x7F800000, None, ALU.bitwise_and))
    done(vector.tensor_scalar(tmp, tmp, 1e-30, None, ALU.max))
    done(vector.tensor_scalar(unscale, tmp, 2.0 ** -13, None, ALU.mult))
    done(vector.reciprocal(scale, unscale))


def embed(nc, x, freqs, w, h):
    with ExitStack() as ctx:
        sb = lambda name, shape, dt: ctx.enter_context(nc.sbuf_tensor(name, shape, dt))
        counters = []

        def sem(name):
            counters.append(ctx.enter_context(nc.semaphore(name)))
            return counters[-1]

        xt = [sb(f"xt{a}", [P, WIDE], F32) for a in range(2)]
        fr = sb("fr", [P, BANDS + BANDS // 2], F32)
        work = sb("work", [P, 8 * WIDE], F32)
        turns = [work[:, i * WIDE:(i + 1) * WIDE] for i in range(2)]
        absturns = [work[:, (2 + i) * WIDE:(3 + i) * WIDE] for i in range(2)]
        waves = [work[:, (4 + 2 * i) * WIDE:(6 + 2 * i) * WIDE].rearrange("p (t n) -> p t n", t=2) for i in range(2)]
        feat_h = [sb(f"feat_h{i}", [P, 2, WIDE], F16) for i in range(2)]
        feat_l = [sb(f"feat_l{i}", [P, 2, WIDE], F16) for i in range(2)]
        w_hl = sb("w_hl", [P, NCH, 2, DIM], F16)
        wabs = sb("wabs", [P, 1], F32)
        wmax = sb("wmax", [P, 1], F32)
        scale = sb("scale", [P, 1], F32)
        unscale = sb("unscale", [P, 1], F32)
        tmp = sb("tmp", [P, 1], F32)
        quarter = sb("quarter", [P, 1], F32)
        h_sb = sb("h_sb", [P, TB, DIM], F32)
        h_lo = sb("h_lo", [P, TB, DIM], F32)
        acc = [ctx.enter_context(nc.psum_tensor(f"acc{i}", [P, TB, 512], F32)) for i in range(2)]

        w_in, fr_in = sem("w_in"), sem("fr_in")
        x_in = [sem(f"x_in{a}") for a in range(2)]
        own, maxed, w_max_ready, w_ready, quarter_ready = (
            sem("own"), sem("maxed"), sem("w_max_ready"), sem("w_ready"), sem("quarter_ready"))
        angle_steps, halves_split = sem("angle_steps"), sem("halves_split")
        turns_ready = [sem(f"turns_ready{i}") for i in range(2)]
        waves_ready = [sem(f"waves_ready{i}") for i in range(2)]
        high_ready = [sem(f"high_ready{i}") for i in range(2)]
        low_sin_ready = [sem(f"low_sin_ready{i}") for i in range(2)]
        low_cos_ready = [sem(f"low_cos_ready{i}") for i in range(2)]
        feat_used = [sem(f"feat_used{i}") for i in range(2)]
        h_ready, h_out = sem("h_ready"), sem("h_out")
        UNITS = BANDS // 2
        w_raw = work[:, 0:NCH * DIM]
        block = ctx.enter_context(nc.Block())

        @block.sync
        def _(sp):
            for counter in counters:
                sp.sem_inc(counter, START)
            sp.dma_start(w_raw, w).then_inc(w_in, 16)
            sp.dma_start(fr[:, :], freqs).then_inc(fr_in, 16)

            def load(i, a):
                sp.dma_start(xt[a][:, :], x[bass.ds(i, 1), :, :].rearrange("a p n -> (a p) n")).then_inc(x_in[a], 16)

            def store(i):
                sp.wait_ge(h_ready, START + i + 1)
                sp.dma_start(h[bass.ds(i, 1), :, :, :].rearrange("a p b d -> (a p) b d"), h_sb[:, :, :]).then_inc(h_out, 16)

            load(0, 0)
            load(1, 1)
            with sp.Fori(0, IMAGES // 2 - 1) as pair:
                for a in range(2):
                    i = pair * 2 + a
                    store(i)
                    sp.wait_ge(angle_steps, START + (i + 1) * (2 * BANDS))
                    load(i + 2, a)
            store(IMAGES - 2)
            store(IMAGES - 1)
            sp.wait_ge(h_out, START + 16 * IMAGES)

        @block.gpsimd
        def _(pool):
            pool.wait_ge(maxed, START + 1)
            nc.gpsimd.partition_all_reduce(wmax[:, :], wabs[:, :], P, RMAX).then_inc(w_max_ready, 1)
            with pool.Fori(0, IMAGES) as i:
                for b in range(BANDS):
                    n, hi = b % 2, (FULL + b % 2) * TOKENS
                    pool.wait_ge(high_ready[n], START + i * UNITS + (b // 2 + 1))
                    pool.wait_ge(feat_used[n], START + i * UNITS + b // 2)
                    nc.gpsimd.tensor_tensor(feat_l[n][:, 1, 0:hi], waves[n][:, 1, 0:hi], feat_h[n][:, 1, 0:hi],
                                            ALU.subtract).then_inc(low_cos_ready[n], 1)

        @block.vector
        def _(dve):
            done = Done(dve, own)
            nc.vector.memset(quarter[:, :], float(np.pi / 2)).then_inc(quarter_ready, 1)
            dve.wait_ge(w_in, START + 16)
            nc.vector.tensor_reduce(wabs[:, :], w_raw, AX_X, ALU.max, apply_absolute_value=True).then_inc(maxed, 1)
            dve.wait_ge(w_max_ready, START + 1)
            power_of_two_scale(nc.vector, done, wmax[:, :], scale[:, :], unscale[:, :], tmp[:, :])
            raw = w_raw.rearrange("p (c d) -> p c d", c=NCH)
            done(nc.vector.tensor_scalar(w_hl[:, :, 0, :], raw, scale[:, 0:1], None, ALU.mult))
            done(nc.vector.scalar_tensor_tensor(w_hl[:, :, 1, :], raw, scale[:, 0:1], w_hl[:, :, 0, :],
                                                ALU.mult, ALU.subtract))
            nc.vector.memset(tmp[:, :], 0.0).then_inc(w_ready, 1)
            dve.wait_ge(fr_in, START + 16)

            def angles(i, a, b):
                n, last = b % 2, None
                parts = [(0, FULL * TOKENS, b)] + ([(FULL * TOKENS, WIDE, BANDS + b // 2)] if b % 2 else [])
                whole = absturns[n].bitcast(I32)
                if b == 0:
                    dve.wait_ge(x_in[a], START + i * 8 + (16 - 8 * a))
                dve.wait_ge(waves_ready[n], START + (i * UNITS + b // 2) * 2)
                for lo, hi, f in parts:
                    last = nc.vector.tensor_scalar(whole[:, lo:hi], xt[a][:, lo:hi], fr[:, f:f + 1], None, ALU.mult)
                last.then_inc(angle_steps, 1)
                dve.wait_ge(angle_steps, START + i * (2 * BANDS) + (2 * b + 1))
                for lo, hi, f in parts:
                    last = nc.vector.scalar_tensor_tensor(turns[n][:, lo:hi], xt[a][:, lo:hi], fr[:, f:f + 1],
                                                          whole[:, lo:hi], ALU.mult, ALU.subtract)
                last.then_inc(angle_steps, 1)
                dve.wait_ge(angle_steps, START + i * (2 * BANDS) + (2 * b + 2))
                hi = parts[-1][1]
                nc.vector.tensor_scalar(whole[:, 0:hi], turns[n].bitcast(I32)[:, 0:hi], 0x7FFFFFFF, None,
                                        ALU.bitwise_and).then_inc(turns_ready[n], 1)

            def low_sines(i, b):
                n, hi = b % 2, (FULL + b % 2) * TOKENS
                dve.wait_ge(high_ready[n], START + i * UNITS + (b // 2 + 1))
                dve.wait_ge(feat_used[n], START + i * UNITS + b // 2)
                nc.vector.tensor_tensor(feat_l[n][:, 0, 0:hi], waves[n][:, 0, 0:hi], feat_h[n][:, 0, 0:hi],
                                        ALU.subtract).then_inc(low_sin_ready[n], 1)

            def tokens(i, a):
                dve.wait_ge(feat_used[1], START + (i + 1) * UNITS)
                dve.wait_ge(h_out, START + i * 16)
                nc.vector.tensor_scalar(h_lo[:, :, :], acc[a][:, :, DIM:2 * DIM], unscale[:, 0:1], None,
                                        ALU.mult).then_inc(halves_split, 1)
                dve.wait_ge(halves_split, START + i + 1)
                nc.vector.scalar_tensor_tensor(h_sb[:, :, :], acc[a][:, :, 0:DIM], unscale[:, 0:1], h_lo[:, :, :],
                                               ALU.mult, ALU.add).then_inc(h_ready, 1)

            def image(i, a, before=True, after=True):
                for b in range(BANDS):
                    if b < BANDS - 1:
                        angles(i, a, b + 1)
                    elif after:
                        angles(i + 1, 1 - a, 0)
                    low_sines(i, b)
                    if before and b == 1:
                        tokens(i - 1, 1 - a)

            angles(0, 0, 0)
            image(0, 0, before=False)
            with dve.Fori(0, IMAGES // 2 - 1) as pair:
                image(pair * 2 + 1, 1)
                image(pair * 2 + 2, 0)
            image(IMAGES - 1, 1, after=False)
            tokens(IMAGES - 1, 1)

        @block.scalar
        def _(act):
            act.wait_ge(quarter_ready, START + 1)
            act.wait_ge(w_ready, START + 1)
            with act.Fori(0, IMAGES) as i:
                for b in range(BANDS):
                    n, hi = b % 2, (FULL + b % 2) * TOKENS
                    act.wait_ge(turns_ready[n], START + i * UNITS + (b // 2 + 1))
                    act.wait_ge(low_sin_ready[n], START + i * UNITS + b // 2)
                    act.wait_ge(low_cos_ready[n], START + i * UNITS + b // 2)
                    nc.scalar.activation(waves[n][:, 0, 0:hi], turns[n][:, 0:hi], ACT.Sin,
                                         scale=TURN).then_inc(waves_ready[n], 1)
                    nc.scalar.activation(waves[n][:, 1, 0:hi], absturns[n][:, 0:hi], ACT.Sin, bias=quarter[:, 0:1],
                                         scale=-TURN).then_inc(waves_ready[n], 1)
                    act.wait_ge(waves_ready[n], START + i * (2 * UNITS) + (2 * (b // 2) + 2))
                    act.wait_ge(feat_used[n], START + i * UNITS + b // 2)
                    nc.scalar.activation(feat_h[n][:, :, 0:hi], waves[n][:, :, 0:hi], ACT.Copy).then_inc(high_ready[n], 1)

        @block.tensor
        def _(pe):
            pe.wait_ge(w_ready, START + 1)
            with pe.Fori(0, IMAGES // 2) as pair:
                for a in range(2):
                    i = pair * 2 + a
                    pe.wait_ge(h_ready, START + i)
                    for b in range(BANDS):
                        n = b % 2
                        chunks = [(2 * k + t, s, t) for k, (band, s) in enumerate(CHUNKS) if band == b for t in range(2)]
                        pe.wait_ge(high_ready[n], START + i * UNITS + (b // 2 + 1))
                        for k, s, t in chunks:
                            for q in range(TB):
                                block_of = feat_h[n][:, t, s * TOKENS + q * P:s * TOKENS + (q + 1) * P]
                                nc.tensor.matmul(acc[a][:, q, 0:2 * DIM], block_of, w_hl[:, k, :, :].rearrange("p a d -> p (a d)"),
                                                 start=(k == 0), stop=False)
                        pe.wait_ge(low_sin_ready[n], START + i * UNITS + (b // 2 + 1))
                        pe.wait_ge(low_cos_ready[n], START + i * UNITS + (b // 2 + 1))
                        for k, s, t in chunks:
                            for q in range(TB):
                                block_of = feat_l[n][:, t, s * TOKENS + q * P:s * TOKENS + (q + 1) * P]
                                last = nc.tensor.matmul(acc[a][:, q, 0:DIM], block_of, w_hl[:, k, 0, :],
                                                        start=False, stop=(k == NCH - 1))
                        last.then_inc(feat_used[n], 1)
    return counters


def project(nc, h, wqv, ident, q_parts, v_parts):
    with ExitStack() as ctx:
        sb = lambda name, shape, dt: ctx.enter_context(nc.sbuf_tensor(name, shape, dt))
        ps = lambda name, shape, dt: ctx.enter_context(nc.psum_tensor(name, shape, dt))
        counters = []

        def sem(name):
            counters.append(ctx.enter_context(nc.semaphore(name)))
            return counters[-1]

        REST, HALF, GROUPS = DIM - P, DIM // 2, TB * HEADS
        two = lambda name, shape, dt: [sb(f"{name}{a}", shape, dt) for a in range(2)]
        eye, eye_h = sb("eye", [P, P], F32), sb("eye_h2", [P, P], F16)
        w_a, w_b = sb("wqv_a", [P, 2 * DIM], F32), sb("wqv_b", [REST, 2 * DIM], F32)
        h_in_sb = two("h_in_sb", [P, TB, DIM], F32)
        ht_a, ht_b = two("ht_a", [P, TOKENS], F32), two("ht_b", [REST, TOKENS], F32)
        q_sb, v_full = two("q_sb", [P, GROUPS, HD], F32), two("v_full", [P, GROUPS, HD], F32)
        squares = sb("squares", [P, GROUPS, HD], F32)
        sums, root, inv = sb("sums2", [P, GROUPS], F32), sb("root", [P, GROUPS], F32), sb("inv", [P, GROUPS, 1], F32)
        qn = sb("qn", [P, GROUPS, HD], F32)
        q_nat = two("q_nat", [P, 2, TB, DIM], F16)
        q_hl = two("q_hl", [HALF, 2, 2, TOKENS], F16)
        v_rest = sb("v_rest", [P, GROUPS, HD], F32)
        v_sb = two("v_sb", [P, GROUPS, VW], BF16)
        pt_a, pt_b = ps("pt_a", [P, TOKENS], F32), ps("pt_b", [REST, TOKENS], F32)
        pqv = ps("pqv", [P, TB, 512], F32)
        pq_t = ps("pq_t", [HALF, 2, 2, TOKENS], F16)

        consts_in, consts_set = sem("consts_in"), sem("consts_set")
        h_in = [sem(f"h_in{a}") for a in range(2)]
        turned, ht_ready, qv_ready, q_out_ps, v_out_ps = (
            sem("turned"), sem("ht_ready"), sem("qv_ready"), sem("q_out_ps"), sem("v_out_ps"))
        squared, summed, rooted, inv_steps, scaled, q_high, q_split = (
            sem("squared"), sem("summed"), sem("rooted"), sem("inv_steps"), sem("scaled"), sem("q_high"), sem("q_split"))
        v_high, v_rest_ready, v_mid, v_split = sem("v_high"), sem("v_rest_ready"), sem("v_mid"), sem("v_split")
        parts_turned, parts_read = sem("parts_turned"), sem("parts_read")
        out = [sem(f"out{a}") for a in range(2)]
        CONSTS = 3
        block = ctx.enter_context(nc.Block())

        def images(eng, *stages):
            full = 2 * (len(stages) // 2)
            for i in range(full):
                for lag in range(min(i + 1, len(stages))):
                    stages[lag](i - lag, (i - lag) % 2)
            with eng.Fori(0, (IMAGES - full) // 2) as pair:
                for a in range(2):
                    for lag in range(len(stages)):
                        stages[lag](pair * 2 + (full + a - lag), (a - lag) % 2)
            for i in range(IMAGES, IMAGES + len(stages) - 1):
                for lag in range(i - IMAGES + 1, len(stages)):
                    stages[lag](i - lag, (i - lag) % 2)

        def nothing(i, a):
            pass

        @block.sync
        def _(sp):
            for counter in counters:
                sp.sem_inc(counter, START)
            for dst, src in ((eye, ident), (w_a, wqv[0:P, :]), (w_b, wqv[P:DIM, :])):
                sp.dma_start(dst[:, :], src).then_inc(consts_in, 16)

            def load(i, a):
                if not (isinstance(i, int) and i < 2):
                    sp.wait_ge(turned, START + i - 1)
                sp.dma_start(h_in_sb[a][:, :, :], h[bass.ds(i, 1), :, :, :].rearrange("a p b d -> (a p) b d")).then_inc(h_in[a], 16)

            def store_v(i, a):
                sp.wait_ge(v_split, START + i + 1)
                sp.dma_start(v_parts[bass.ds(i, 1), :, :].rearrange("a p n -> (a p) n"),
                             v_sb[a][:, :, :].rearrange("p g w -> p (g w)")).then_inc(out[a], 16)

            def store_q(i, a):
                sp.wait_ge(parts_read, START + i * 2 + 2)
                for part in range(2):
                    sp.dma_start(q_parts[bass.ds(i, 1), :, part, :, :].rearrange("a h p n -> p (a h) n"),
                                 q_hl[a][:, part, :, :]).then_inc(out[a], 16)

            images(sp, load, nothing, store_v, store_q)
            for a in range(2):
                sp.wait_ge(out[a], START + 48 * IMAGES // 2)

        def stored(eng, i, a):
            if isinstance(i, int):
                if i >= 2:
                    eng.wait_ge(out[a], START + (i - a) * 24)
            else:
                eng.wait_ge(out[a], START + i * 24 - 24 * a)

        @block.tensor
        def _(pe):
            pe.wait_ge(consts_in, START + 16 * CONSTS)
            pe.wait_ge(consts_set, START + 3)

            def turn(i, a):
                if isinstance(i, int):
                    pe.wait_ge(h_in[a], START + (i - a) * 8 + 16)
                else:
                    pe.wait_ge(h_in[a], START + i * 8 + (16 - 8 * a))
                pe.wait_ge(ht_ready, START + i * 2)
                for b in range(TB):
                    nc.tensor.transpose(pt_a[:, b * P:(b + 1) * P], h_in_sb[a][:, b, 0:P], eye[:, :])
                    last = nc.tensor.transpose(pt_b[:, b * P:(b + 1) * P], h_in_sb[a][:, b, P:DIM], eye[:, :])
                last.then_inc(turned, 1)

            def multiply(i, a):
                pe.wait_ge(ht_ready, START + i * 2 + 2)
                pe.wait_ge(q_out_ps, START + i)
                pe.wait_ge(v_out_ps, START + i)
                for b in range(TB):
                    rows = slice(b * P, (b + 1) * P)
                    nc.tensor.matmul(pqv[:, b, 0:2 * DIM], ht_a[a][:, rows], w_a[:, :], start=True, stop=False)
                    last = nc.tensor.matmul(pqv[:, b, 0:2 * DIM], ht_b[a][:, rows], w_b[:, :], start=False, stop=True)
                last.then_inc(qv_ready, 1)

            def turn_parts(i, a):
                pe.wait_ge(q_split, START + i + 1)
                pe.wait_ge(parts_read, START + i * 2)
                for part in range(2):
                    for half in range(2):
                        for b in range(TB):
                            last = nc.tensor.transpose(pq_t[:, part, half, b * P:(b + 1) * P],
                                                       q_nat[a][:, part, b, half * HALF:(half + 1) * HALF], eye_h[:, :])
                last.then_inc(parts_turned, 1)

            images(pe, turn, multiply, turn_parts)

        @block.scalar
        def _(act):
            def read_turned(i, a):
                act.wait_ge(turned, START + i + 1)
                if not (isinstance(i, int) and i < 2):
                    act.wait_ge(qv_ready, START + i - 1)
                nc.scalar.activation(ht_a[a][:, :], pt_a[:, :], ACT.Copy).then_inc(ht_ready, 1)
                nc.scalar.activation(ht_b[a][:, :], pt_b[:, :], ACT.Copy).then_inc(ht_ready, 1)

            def read_q(i, a):
                act.wait_ge(qv_ready, START + i + 1)
                act.wait_ge(scaled, START + i)
                act.wait_ge(summed, START + i)
                nc.scalar.activation(q_sb[a][:, :, :].rearrange("p (b g) d -> p b (g d)", b=TB), pqv[:, :, 0:DIM],
                                     ACT.Copy).then_inc(q_out_ps, 1)
                act.wait_ge(q_out_ps, START + i + 1)
                nc.scalar.activation(squares[:, :, :], q_sb[a][:, :, :], ACT.Square).then_inc(squared, 1)
                act.wait_ge(summed, START + i + 1)
                act.wait_ge(inv_steps, START + i * 2)
                nc.scalar.activation(root[:, :], sums[:, :], ACT.Sqrt).then_inc(rooted, 1)

            def read_high(i, a):
                act.wait_ge(parts_turned, START + i + 1)
                stored(act, i, a)
                nc.scalar.activation(q_hl[a][:, 0, :, :], pq_t[:, 0, :, :], ACT.Copy).then_inc(parts_read, 1)

            images(act, read_turned, read_q, read_high)

        @block.gpsimd
        def _(pool):
            def v_parts_two(i, a):
                pool.wait_ge(v_high, START + i + 1)
                pool.wait_ge(v_split, START + i)
                nc.gpsimd.tensor_tensor(v_rest[:, :, :], v_full[a][:, :, :], v_sb[a][:, :, 0:HD], ALU.subtract).then_inc(v_rest_ready, 1)
                pool.wait_ge(v_mid, START + i + 1)
                nc.gpsimd.tensor_tensor(v_sb[a][:, :, 2 * HD:3 * HD], v_rest[:, :, :], v_sb[a][:, :, HD:2 * HD],
                                        ALU.subtract).then_inc(v_split, 1)

            images(pool, nothing, v_parts_two, nothing)

        @block.vector
        def _(dve):
            for a in range(2):
                nc.vector.memset(v_sb[a][:, :, 3 * HD:VW], 1.0).then_inc(consts_set, 1)
            dve.wait_ge(consts_in, START + 16 * CONSTS)
            nc.vector.tensor_copy(eye_h[:, :], eye[:, :]).then_inc(consts_set, 1)

            def split(i, a):
                dve.wait_ge(q_out_ps, START + i + 1)
                if not (isinstance(i, int) and i < 2):
                    dve.wait_ge(v_split, START + i - 1)
                nc.vector.tensor_copy(v_full[a][:, :, :].rearrange("p (b g) d -> p b (g d)", b=TB),
                                      pqv[:, :, DIM:2 * DIM]).then_inc(v_out_ps, 1)
                dve.wait_ge(v_out_ps, START + i + 1)
                stored(dve, i, a)
                nc.vector.tensor_copy(v_sb[a][:, :, 0:HD], v_full[a][:, :, :]).then_inc(v_high, 1)
                dve.wait_ge(squared, START + i + 1)
                dve.wait_ge(rooted, START + i)
                nc.vector.tensor_reduce(sums[:, :], squares[:, :, :], AX_X, ALU.add).then_inc(summed, 1)
                dve.wait_ge(v_rest_ready, START + i + 1)
                nc.vector.tensor_copy(v_sb[a][:, :, HD:2 * HD], v_rest[:, :, :]).then_inc(v_mid, 1)
                dve.wait_ge(rooted, START + i + 1)
                nc.vector.tensor_scalar(root[:, :], root[:, :], 1e-8, None, ALU.add).then_inc(inv_steps, 1)
                dve.wait_ge(inv_steps, START + i * 2 + 1)
                nc.vector.reciprocal(inv[:, :, 0], root[:, :]).then_inc(inv_steps, 1)
                dve.wait_ge(inv_steps, START + i * 2 + 2)
                nc.vector.scalar_tensor_tensor(qn[:, :, :], q_sb[a][:, :, :], Q_SCALE, inv[:, :, :].to_broadcast([P, GROUPS, HD]),
                                               ALU.mult, ALU.mult).then_inc(scaled, 1)
                dve.wait_ge(scaled, START + i + 1)
                if not (isinstance(i, int) and i < 2):
                    dve.wait_ge(parts_turned, START + i - 1)
                parts = q_nat[a][:, :, :, :].rearrange("p w b (g d) -> p w (b g) d", d=HD)
                nc.vector.tensor_copy(parts[:, 0], qn[:, :, :]).then_inc(q_high, 1)
                dve.wait_ge(q_high, START + i + 1)
                nc.vector.tensor_tensor(parts[:, 1], qn[:, :, :], parts[:, 0], ALU.subtract).then_inc(q_split, 1)

            def read_low(i, a):
                dve.wait_ge(parts_turned, START + i + 1)
                stored(dve, i, a)
                nc.vector.tensor_copy(q_hl[a][:, 1, :, :], pq_t[:, 1, :, :]).then_inc(parts_read, 1)

            images(dve, nothing, split, read_low)

UH = HEADS // 2
GH = UH // 2
REG, ITERS = 0.1, 10
STEPS_X = 2 * ITERS - 1
K_SHIFT = float(15 * np.log(2))
HIDE = -60000.0
ATT_SCALE = HD ** -0.5


def attend(nc, q_parts, v_parts, ident, att):
    with ExitStack() as ctx:
        sb = lambda name, shape, dt: ctx.enter_context(nc.sbuf_tensor(name, shape, dt))
        ps = lambda name, shape, dt: ctx.enter_context(nc.psum_tensor(name, shape, dt))
        counters = []

        def sem(name):
            counters.append(ctx.enter_context(nc.semaphore(name)))
            return counters[-1]

        eye = sb("eye3", [P, P], F32)
        eye_h, eye_hide = sb("eye_h", [P, P], F16), sb("eye_hide", [P, P], F16)
        eye_bf = sb("eye_bf", [P, P], BF16)
        XR = UH * TB * 3
        pick = sb("pick3", [XR, UH * TB, P], BF16)
        xt_sb = sb("xt_sb", [XR, P], BF16)
        lift = sb("lift", [P, 2, P], F16)
        ones = sb("ones3", [P, P], BF16)
        k_bias, p_bias = sb("k_bias", [P, 1], F32), sb("p_bias", [P, 1], F32)
        q_left = [sb(f"q_left{s}", [P, UH, TOKENS], F16) for s in range(2)]
        q_right = [sb(f"q_right{s}", [P, UH, TOKENS], F16) for s in range(2)]
        v_sb = [sb(f"v_in_sb{s}", [P, TB, UH, VW], BF16) for s in range(2)]
        k_h = [sb(f"k_h{s}", [P, UH, TB * TOKENS], F16) for s in range(2)]
        k_l = [sb(f"k_l{s}", [P, UH, TB * TOKENS], F16) for s in range(2)]
        row_sums = [sb(f"row_sums{s}", [P, UH * TB], F32) for s in range(2)]
        x_sb = [sb(f"x_sb{s}", [P, UH * TB, 3], BF16) for s in range(2)]
        v_last = [sb(f"v_last{s}", [P, UH * TB], F32) for s in range(2)]
        k_new = sb("k_new", [P, TB, TOKENS], F32)
        plan = sb("plan", [P, TB, TOKENS], F32)
        probs = sb("probs", [P, TB, TOKENS], F32)
        p_h, p_l = sb("p_h", [P, TB, TOKENS], F16), sb("p_l", [P, TB, TOKENS], F16)
        sums = [sb(f"sums{g}", [P, GH * TB], F32) for g in range(2)]
        recs = [sb(f"recs{g}", [P, GH * TB], F32) for g in range(2)]
        rest = [sb(f"rest{g}", [P, GH * TB], F32) for g in range(2)]
        idle, idle_pool = sb("idle", [P, 1], F32), sb("idle_pool", [P, 3], F32)
        row_max, weighted = sb("row_max", [P, TB], F32), sb("weighted", [P, TB], F32)
        head_max, all_max, inv_max = sb("head_max", [P, 1], F32), sb("all_max", [P, 1], F32), sb("inv_max", [P, 1], F32)
        p_scale = sb("p_scale", [P, TB], F32)
        num, den = sb("num", [P, TB, HD], F32), sb("den", [P, TB, 1], F32)
        att_sb = [sb(f"att_sb{s}", [P, TB, UH, HD], F32) for s in range(2)]
        kx = [ps(f"kx{g}", [P, GH * TB, 3], F32) for g in range(2)]
        cos = ps("cos", [P, 2, TOKENS], F32)
        u_rows = ps("u_rows", [P, TOKENS], F32)
        xt_ps = ps("xt_ps", [XR, P], F32)
        pv = ps("pv3", [P, TB, VW], F32)

        eye_in, consts, ones_set = sem("eye_in"), sem("consts"), sem("ones3_set")
        q_in = [sem(f"q_in{s}") for s in range(2)]
        v_in = [sem(f"v_in{s}") for s in range(2)]
        att_out = [sem(f"att_out{s}") for s in range(2)]
        kx_ready = [sem(f"kx_ready{g}") for g in range(2)]
        x_ready = [sem(f"x_ready{g}") for g in range(2)]
        sum_steps = [sem(f"sum_steps{g}") for g in range(2)]
        x_steps = [sem(f"x_steps{g}") for g in range(2)]
        cos_ready, k_exp, k_high, k_built = sem("cos_ready"), sem("k_exp"), sem("k_high"), sem("k_built")
        pick_steps, x_turned, xt_ready = sem("pick_steps"), sem("x_turned3"), sem("xt_ready3")
        u_rows_ready, k_joined = sem("u_rows_ready"), sem("k_joined")
        plan_ready, weighed, head_max_ready, all_max_ready = (
            sem("plan_ready"), sem("weighed"), sem("head_max_ready"), sem("all_max_ready"))
        inv_ready, scale_ready, p_exp, p_high, p_ready = (
            sem("inv_ready"), sem("scale_ready"), sem("p_exp"), sem("p_high"), sem("p_ready"))
        pv_ready, summed_up, att_ready = sem("pv_ready"), sem("summed_up"), sem("att_ready")
        block = ctx.enter_context(nc.Block())

        def units(eng, head, last=None, first=None):
            with eng.Fori(0, UH) as k:
                head(None, None, (0, 0, 0), k)
            if first:
                first()

            def unit(n, f, b):
                with eng.Fori(0, UH) as k:
                    head(n, f, b, k)
                if last:
                    last(n, b)

            unit((0, 0, 0), None, (1, 1, 0))
            with eng.Fori(0, IMAGES - 1) as t:
                unit((t * 2 + 1, 1, t), (t * 2, 0, t), (t * 2 + 2, 0, t + 1))
                unit((t * 2 + 2, 0, t + 1), (t * 2 + 1, 1, t), (t * 2 + 3, 1, t + 1))
            unit((2 * IMAGES - 1, 1, IMAGES - 1), (2 * IMAGES - 2, 0, IMAGES - 1), None)
            with eng.Fori(0, UH) as k:
                head(None, (2 * IMAGES - 1, 1, IMAGES - 1), None, k)

        @block.sync
        def _(sp):
            for counter in counters:
                sp.sem_inc(counter, START)
            sp.dma_start(eye[:, :], ident).then_inc(eye_in, 16)

            def load_q(image, s):
                for g in range(4):
                    for dst, part in ((q_left, g // 2), (q_right, g % 2)):
                        sp.dma_start(dst[s][32 * g:32 * g + HD, :, :],
                                     q_parts[bass.ds(image, 1), s, part, :, :].rearrange("a (k d) n -> d (a k) n", d=HD)).then_inc(q_in[s], 16)

            def load_v(image, s):
                src = v_parts[bass.ds(image, 1), :, :].rearrange("a p (b h w) -> (a p) b h w", b=TB, h=HEADS)
                sp.dma_start(v_sb[s][:, :, :, :], src[:, :, s * UH:(s + 1) * UH, :]).then_inc(v_in[s], 16)

            def store(image, s):
                dst = att[bass.ds(image, 1), :, :, :].rearrange("a p b (s n) -> (a p) b s n", s=2)[:, :, s, :]
                sp.dma_start(dst, att_sb[s][:, :, :, :].rearrange("p b h d -> p b (h d)")).then_inc(att_out[s], 16)

            sp.wait_ge(ones_set, START + 1)
            load_q(0, 0)
            load_q(0, 1)
            load_v(0, 0)
            sp.wait_ge(cos_ready, START + 2 * UH)
            load_q(1, 0)
            sp.wait_ge(cos_ready, START + 2 * UH * 2)
            load_q(1, 1)
            load_v(0, 1)
            with sp.Fori(0, IMAGES - 2) as t:
                for s in range(2):
                    u = t * 2 + s
                    sp.wait_ge(att_ready, START + (u + 1) * UH)
                    store(t, s)
                    sp.wait_ge(cos_ready, START + (u + 3) * (2 * UH))
                    load_q(t + 2, s)
                    sp.wait_ge(pv_ready, START + (u + 1) * UH)
                    load_v(t + 1, s)
            for t, s in ((IMAGES - 2, 0), (IMAGES - 2, 1), (IMAGES - 1, 0), (IMAGES - 1, 1)):
                sp.wait_ge(att_ready, START + (2 * t + s + 1) * UH)
                store(t, s)
                if t == IMAGES - 2:
                    load_v(t + 1, s)
            for s in range(2):
                sp.wait_ge(att_out[s], START + 16 * IMAGES)

        @block.gpsimd
        def _(pool):
            nc.gpsimd.memset(pick[:, :, :], 1.0).then_inc(pick_steps, 1)
            pool.wait_ge(pick_steps, START + 1)
            nc.gpsimd.affine_select(out=pick[:, :, :], in_=pick[:, :, :], compare_op=ALU.is_ge, fill=0.0, base=0,
                                    pattern=[[-3, UH * TB], [0, P]], channel_multiplier=1).then_inc(pick_steps, 1)
            pool.wait_ge(pick_steps, START + 2)
            nc.gpsimd.affine_select(out=pick[:, :, :], in_=pick[:, :, :], compare_op=ALU.is_ge, fill=0.0, base=2,
                                    pattern=[[3, UH * TB], [0, P]], channel_multiplier=-1).then_inc(pick_steps, 1)
            pool.wait_ge(consts, START + 7)

            def head(n, f, b, k):
                if f:
                    F = f[0] * UH + k
                    pool.wait_ge(p_exp, START + F * TB)
                    nc.gpsimd.tensor_tensor(idle_pool[:, 0:1], k_bias[:, :], k_bias[:, :], ALU.add)
                    nc.gpsimd.tensor_tensor(plan[:, :, :].rearrange("p b n -> p (b n)"),
                                            k_h[f[1]][:, bass.ds(k, 1), :].rearrange("p a n -> p (a n)"),
                                            k_l[f[1]][:, bass.ds(k, 1), :].rearrange("p a n -> p (a n)"), ALU.add).then_inc(k_joined, 1)
                    pool.wait_ge(head_max_ready, START + F + 1)
                    nc.gpsimd.tensor_tensor(idle_pool[:, 1:2], k_bias[:, :], k_bias[:, :], ALU.add)
                    nc.gpsimd.partition_all_reduce(all_max[:, :], head_max[:, :], P, RMAX).then_inc(all_max_ready, 1)
                if b and n:
                    pool.wait_ge(k_high, START + b[0] * UH + k + 1)
                    nc.gpsimd.tensor_tensor(idle_pool[:, 2:3], k_bias[:, :], k_bias[:, :], ALU.add)
                    nc.gpsimd.tensor_tensor(k_l[b[1]][:, bass.ds(k, 1), :].rearrange("p a n -> p (a n)"),
                                            k_new[:, :, :].rearrange("p b n -> p (b n)"),
                                            k_h[b[1]][:, bass.ds(k, 1), :].rearrange("p a n -> p (a n)"), ALU.subtract).then_inc(k_built, 1)

            units(pool, head)

        @block.tensor
        def _(pe):
            pe.wait_ge(consts, START + 7)
            pe.wait_ge(pick_steps, START + 3)

            def product(n, g, m, first=False):
                pe.wait_ge(x_ready[g], START + n[0] * STEPS_X + m)
                if first:
                    pe.wait_ge(sum_steps[g], START + n[0] * STEPS_X + (m - 1))
                for h in range(g * GH, (g + 1) * GH):
                    for i in range(TB):
                        out = kx[g][:, (h - g * GH) * TB + i, :]
                        for j in range(TB):
                            cols = slice(j * TOKENS + i * P, j * TOKENS + (i + 1) * P)
                            x = x_sb[n[1]][:, h * TB + j, :]
                            nc.tensor.matmul(out, k_h[n[1]][:, h, cols], x, start=(j == 0), stop=False)
                            last = nc.tensor.matmul(out, k_l[n[1]][:, h, cols], x, start=False, stop=(j == TB - 1))
                last.then_inc(kx_ready[g], 1)

            def cosines(b, k, half):
                G = b[0] * UH + k
                if half == 0:
                    pe.wait_ge(q_in[b[1]], START + (b[2] + 1) * (8 * 16))
                pe.wait_ge(k_exp, START + G * TB + 2 * half)
                for c in (2 * half, 2 * half + 1):
                    nc.tensor.matmul(cos[:, c % 2, :], q_left[b[1]][:, bass.ds(k, 1), c * P:(c + 1) * P].rearrange("p a n -> p (a n)"),
                                     q_right[b[1]][:, bass.ds(k, 1), :].rearrange("p a n -> p (a n)"), start=True, stop=False)
                    last = nc.tensor.matmul(cos[:, c % 2, c * P:(c + 1) * P], eye_h[:, :], eye_hide[:, :], start=False, stop=True)
                last.then_inc(cos_ready, 1)

            def u_to_rows(f, k):
                F = f[0] * UH + k
                pe.wait_ge(xt_ready, START + f[0] + 1)
                pe.wait_ge(plan_ready, START + F)
                for c in range(TB):
                    last = nc.tensor.matmul(u_rows[:, c * P:(c + 1) * P],
                                            pick[:, bass.ds(k * TB + c, 1), :].rearrange("p a n -> p (a n)"), xt_sb[:, :],
                                            start=True, stop=True)
                last.then_inc(u_rows_ready, 1)

            def times_v(f, k):
                F = f[0] * UH + k
                pe.wait_ge(p_ready, START + F * 2 + 2)
                pe.wait_ge(v_in[f[1]], START + (f[2] + 1) * 16)
                pe.wait_ge(att_ready, START + F)
                for i in range(TB):
                    for j in range(TB):
                        v = v_sb[f[1]][:, j, bass.ds(k, 1), :].rearrange("p a n -> p (a n)")
                        nc.tensor.matmul(pv[:, i, :], p_h[:, j, i * P:(i + 1) * P], v, start=(j == 0), stop=False)
                        nc.tensor.matmul(pv[:, i, :], p_l[:, j, i * P:(i + 1) * P], v, start=False, stop=False)
                    v = v_sb[f[1]][:, i, bass.ds(k, 1), :].rearrange("p a n -> p (a n)")
                    nc.tensor.matmul(pv[:, i, :], lift[:, 0, :], v, start=False, stop=False)
                    last = nc.tensor.matmul(pv[:, i, :], lift[:, 1, :], v, start=False, stop=True)
                last.then_inc(pv_ready, 1)

            def head(n, f, b, k):
                if f:
                    u_to_rows(f, k)
                if n:
                    product(n, 0, k * 3 + 1, True)
                if b:
                    cosines(b, k, 0)
                if n:
                    product(n, 1, k * 3 + 1, True)
                if b:
                    cosines(b, k, 1)
                if n:
                    for m in (2, 3):
                        for g in range(2):
                            product(n, g, k * 3 + m)
                if f:
                    times_v(f, k)

            def last(n, b):
                product(n, 0, STEPS_X)
                pe.wait_ge(xt_ready, START + n[0])
                pe.wait_ge(x_ready[1], START + (n[0] + 1) * STEPS_X)
                nc.tensor.matmul(xt_ps[:, :], x_sb[n[1]][:, :, :].rearrange("p c w -> p (c w)"), eye_bf[:, :],
                                 start=True, stop=True).then_inc(x_turned, 1)
                product(n, 1, STEPS_X)

            units(pe, head, last)

        @block.scalar
        def _(act):
            act.wait_ge(consts, START + 7)

            def head(n, f, b, k):
                if b:
                    G = b[0] * UH + k
                    act.wait_ge(k_built, START + G)
                    for c in range(TB):
                        if c % 2 == 0:
                            act.wait_ge(cos_ready, START + G * 2 + (c // 2 + 1))
                        nc.scalar.activation(k_new[:, c, :], cos[:, c % 2, :], ACT.Exp, bias=k_bias[:, 0:1],
                                             scale=1.0 / (REG * Q_SCALE ** 2),
                                             accum_out=row_sums[b[1]][:, bass.ds(k * TB + c, 1)]).then_inc(k_exp, 1)
                    act.wait_ge(k_exp, START + (G + 1) * TB)
                    if f:
                        act.wait_ge(k_joined, START + f[0] * UH + k + 1)
                    nc.scalar.activation(k_h[b[1]][:, bass.ds(k, 1), :].rearrange("p a n -> p (a n)"),
                                         k_new[:, :, :].rearrange("p b n -> p (b n)"), ACT.Copy).then_inc(k_high, 1)
                if f:
                    F = f[0] * UH + k
                    act.wait_ge(scale_ready, START + F + 1)
                    act.wait_ge(p_ready, START + F * 2)
                    act.wait_ge(pv_ready, START + F)
                    for half in range(2):
                        for c in (2 * half, 2 * half + 1):
                            nc.scalar.activation(probs[:, c, :], plan[:, c, :], ACT.Exp, bias=p_bias[:, 0:1],
                                                 scale=p_scale[:, c:c + 1]).then_inc(p_exp, 1)
                        act.wait_ge(p_exp, START + F * TB + (2 * half + 2))
                        c = slice(2 * half, 2 * half + 2)
                        nc.scalar.activation(p_h[:, c, :], probs[:, c, :], ACT.Copy).then_inc(p_high, 1)

            def last(n, b):
                act.wait_ge(x_turned, START + n[0] + 1)
                act.wait_ge(u_rows_ready, START + n[0] * UH)
                nc.scalar.activation(xt_sb[:, :], xt_ps[:, :], ACT.Copy).then_inc(xt_ready, 1)

            units(act, head, last)

        @block.vector
        def _(dve):
            for s in range(2):
                nc.vector.memset(q_left[s][:, :, :], 0.0)
                nc.vector.memset(q_right[s][:, :, :], 0.0)
            nc.vector.memset(ones[:, :], 1.0).then_inc(ones_set, 1)
            nc.vector.memset(k_bias[:, :], K_SHIFT - 1.0 / REG).then_inc(consts, 1)
            nc.vector.memset(p_bias[:, :], -ATT_SCALE).then_inc(consts, 1)
            dve.wait_ge(eye_in, START + 16)
            on_diag = float(1.0 - np.exp(-ATT_SCALE))
            on_diag_h = float(np.float16(on_diag))
            nc.vector.tensor_copy(eye_h[:, :], eye[:, :]).then_inc(consts, 1)
            nc.vector.tensor_copy(eye_bf[:, :], eye[:, :]).then_inc(consts, 1)
            nc.vector.tensor_scalar(eye_hide[:, :], eye[:, :], HIDE, None, ALU.mult).then_inc(consts, 1)
            nc.vector.tensor_scalar(lift[:, 0, :], eye[:, :], on_diag_h, None, ALU.mult).then_inc(consts, 1)
            nc.vector.tensor_scalar(lift[:, 1, :], eye[:, :], on_diag - on_diag_h, None, ALU.mult).then_inc(consts, 1)
            dve.wait_ge(consts, START + 7)

            def k_low(b, k):
                dve.wait_ge(k_high, START + b[0] * UH + k + 1)
                nc.vector.tensor_tensor(k_l[b[1]][:, bass.ds(k, 1), :].rearrange("p a n -> p (a n)"),
                                        k_new[:, :, :].rearrange("p b n -> p (b n)"),
                                        k_h[b[1]][:, bass.ds(k, 1), :].rearrange("p a n -> p (a n)"), ALU.subtract).then_inc(k_built, 1)

            def next_x(n, g, m, source, keep=True):
                cols = slice(g * GH * TB, (g + 1) * GH * TB)
                if not keep:
                    nc.vector.reciprocal(v_last[n[1]][:, cols], source)
                    return
                base = n[0] * (4 * STEPS_X) + (m * 4)
                x = x_sb[n[1]]
                nc.vector.reciprocal(recs[g][:, :], source).then_inc(x_steps[g], 1)
                with nc.allow_low_precision("the leading part of three"):
                    nc.vector.reciprocal(x[:, cols, 0], source).then_inc(x_steps[g], 1)
                dve.wait_ge(x_steps[g], START + base + 2)
                nc.vector.tensor_tensor(x[:, cols, 1], recs[g][:, :], x[:, cols, 0], ALU.subtract).then_inc(x_steps[g], 1)
                nc.vector.tensor_tensor(rest[g][:, :], recs[g][:, :], x[:, cols, 0], ALU.subtract).then_inc(x_steps[g], 1)
                dve.wait_ge(x_steps[g], START + base + 4)
                nc.vector.tensor_tensor(x[:, cols, 2], rest[g][:, :], x[:, cols, 1], ALU.subtract).then_inc(x_ready[g], 1)

            def turn(n, g, m, keep=True):
                done = n[0] * STEPS_X + m
                dve.wait_ge(kx_ready[g], START + done)
                nc.vector.tensor_reduce(sums[g][:, :], kx[g][:, :, :], AX_X, ALU.add).then_inc(sum_steps[g], 1)
                dve.wait_ge(sum_steps[g], START + done)
                next_x(n, g, m, sums[g][:, :], keep)

            def first_x(n):
                dve.wait_ge(k_built, START + (n[0] + 1) * UH)
                for g in range(2):
                    next_x(n, g, 0, row_sums[n[1]][:, g * GH * TB:(g + 1) * GH * TB])

            def times_u(f, k, chunks):
                F = f[0] * UH + k
                if chunks[0] == 0:
                    dve.wait_ge(k_joined, START + F + 1)
                    dve.wait_ge(u_rows_ready, START + F + 1)
                    nc.vector.memset(idle[:, :], 0.0)
                for c in chunks:
                    last = nc.vector.tensor_tensor_reduce(plan[:, c, :], plan[:, c, :], u_rows[:, :], 1.0, 0.0,
                                                          ALU.mult, ALU.max, row_max[:, c:c + 1])
                if c == TB - 1:
                    last.then_inc(plan_ready, 1)
                    dve.wait_ge(plan_ready, START + F + 1)
                    nc.vector.tensor_tensor(weighted[:, :], row_max[:, :], v_last[f[1]][:, bass.ds(k * TB, TB)], ALU.mult).then_inc(weighed, 1)
                    dve.wait_ge(weighed, START + F + 1)
                    nc.vector.tensor_reduce(head_max[:, :], weighted[:, :], AX_X, ALU.max).then_inc(head_max_ready, 1)

            def scale_plan(f, k):
                F = f[0] * UH + k
                dve.wait_ge(all_max_ready, START + F + 1)
                nc.vector.reciprocal(inv_max[:, :], all_max[:, :]).then_inc(inv_ready, 1)
                dve.wait_ge(inv_ready, START + F + 1)
                dve.wait_ge(p_exp, START + F * TB)
                nc.vector.tensor_scalar(p_scale[:, :], v_last[f[1]][:, bass.ds(k * TB, TB)], ATT_SCALE, inv_max[:, 0:1],
                                        ALU.mult, ALU.mult).then_inc(scale_ready, 1)

            def p_low_part(f, k, half):
                dve.wait_ge(p_high, START + f[0] * (2 * UH) + k * 2 + (half + 1))
                if half == 0:
                    dve.wait_ge(pv_ready, START + f[0] * UH + k)
                c = slice(half * TB // 2, (half + 1) * TB // 2)
                nc.vector.tensor_tensor(p_l[:, c, :], probs[:, c, :], p_h[:, c, :], ALU.subtract).then_inc(p_ready, 1)

            def normalise(f, k):
                F = f[0] * UH + k
                dve.wait_ge(pv_ready, START + F + 1)
                nc.vector.tensor_reduce(num[:, :, :], pv[:, :, 0:3 * HD].rearrange("p b (w d) -> p b d w", w=3), AX_X,
                                        ALU.add).then_inc(summed_up, 1)
                nc.vector.reciprocal(den[:, :, :], pv[:, :, 3 * HD:VW]).then_inc(summed_up, 1)
                dve.wait_ge(summed_up, START + F * 2 + 2)
                dve.wait_ge(att_out[f[1]], START + f[2] * 16)
                nc.vector.tensor_tensor(att_sb[f[1]][:, :, bass.ds(k, 1), :].rearrange("p b a d -> p b (a d)"), num[:, :, :],
                                        den[:, :, :].to_broadcast([P, TB, HD]), ALU.mult).then_inc(att_ready, 1)

            def head(n, f, b, k):
                if b and not n:
                    k_low(b, k)
                if f:
                    times_u(f, k, (0, 1))
                if n:
                    turn(n, 0, k * 3 + 1)
                if f:
                    times_u(f, k, (2, 3))
                if n:
                    turn(n, 1, k * 3 + 1)
                if f:
                    scale_plan(f, k)
                if n:
                    turn(n, 0, k * 3 + 2)
                    turn(n, 1, k * 3 + 2)
                if f:
                    p_low_part(f, k, 0)
                if n:
                    turn(n, 0, k * 3 + 3)
                if f:
                    p_low_part(f, k, 1)
                if n:
                    turn(n, 1, k * 3 + 3)
                if f:
                    normalise(f, k)

            def last(n, b):
                if b:
                    first_x(b)
                for g in range(2):
                    turn(n, g, STEPS_X, keep=False)

            units(dve, head, last, lambda: first_x((0, 0)))

FB = FFN // P
LN_EPS = 1e-5
R = 3
TOP = 2
PICKS = TOP * TB
TILE = TOKENS
REGION = IMAGES * TOKENS + TILE
TILES = (IMAGES * TOKENS * TOP + EXPERTS * (TILE - 1)) // TILE
LIMITS = IMAGES * TOKENS // TILE


def staged(eng, *stages):
    full = 2 * (len(stages) // 2)
    for i in range(full):
        for lag in range(min(i + 1, len(stages))):
            stages[lag](i - lag, (i - lag) % 2)
    with eng.Fori(0, (IMAGES - full) // 2) as pair:
        for a in range(2):
            for lag in range(len(stages)):
                stages[lag](pair * 2 + (full + a - lag), (a - lag) % 2)
    for i in range(IMAGES, IMAGES + len(stages) - 1):
        for lag in range(i - IMAGES + 1, len(stages)):
            stages[lag](i - lag, (i - lag) % 2)


def nothing(i, a):
    pass


def early(i, n):
    return isinstance(i, int) and i < n


def soft_semaphores(nc, ctx, name):
    return [ctx.enter_context(nc.semaphore(f"{name}{a}")) for a in range(2)]


def soft_in_turn(eng, soft, i, a):
    if isinstance(i, int):
        eng.wait_ge(soft, (i - a) // 2 * (16 * PICKS) + 16 * PICKS)
    else:
        eng.wait_ge(soft, i * (8 * PICKS) + (16 * PICKS - 8 * PICKS * a))


def mix(nc, h, att, ident, w, soft_rows_out, soft_fetched):
    with ExitStack() as ctx:
        sb = lambda name, shape, dt: ctx.enter_context(nc.sbuf_tensor(name, shape, dt))
        keep = {
            "w1": sb("w1", [P, EXPERTS, 3, FFN], F16),
            "w2": sb("w2", [P, EXPERTS * FB, 2, DIM], F16),
            "unscale": sb("unscale4", [P, 2], F32),
            "x_all": sb("x_all", [P, IMAGES * TB, DIM], F32),
            "pick_all": sb("pick_all", [P, IMAGES, PICKS], F32),
            "rank_all": sb("rank_all", [P, IMAGES, PICKS], F32),
            "share_all": sb("share_all", [P, IMAGES, PICKS], F32),
            "tile_row": sb("tile_row", [P, TILES], I32),
            "tile_expert": sb("tile_expert", [P, TILES], I32),
            "first_slot": sb("first_slot", [P, EXPERTS], F32),
            "numbers": sb("numbers", [P, EXPERTS], F32),
            "eps": sb("eps", [P, 1], F32),
        }
        rows = nc.dram_tensor("expert_rows", (EXPERTS * REGION, DIM), F32, kind="Internal").ap()
        results = nc.dram_tensor("expert_results", (TILES * TILE, DIM), F32, kind="Internal").ap()
        prepare(nc, w, keep)
        route(nc, h, att, ident, w["small"], keep, rows, soft_rows_out)
        run_experts(nc, ident, w["small"], keep, rows, results)
        combine(nc, keep, results, w["out"], soft_fetched)


def prepare(nc, w, keep):
    with ExitStack() as ctx:
        sb = lambda name, shape, dt: ctx.enter_context(nc.sbuf_tensor(name, shape, dt))
        counters = []

        def sem(name):
            counters.append(ctx.enter_context(nc.semaphore(name)))
            return counters[-1]

        w1, w2, unscale, eps = keep["w1"], keep["w2"], keep["unscale"], keep["eps"]
        REST = DIM - P
        raw1_a, raw1_b = sb("raw1_a", [P, EXPERTS, FFN], F32), sb("raw1_b", [P, EXPERTS, FFN], F32)
        raw2 = (keep["x_all"][:, :, :].rearrange("p b d -> p (b d)")[:, 0:EXPERTS * FB * DIM]
                .rearrange("p (e d) -> p e d", d=DIM))
        maxes, all_maxes = sb("maxes", [P, 3], F32), sb("all_maxes", [P, 3], F32)
        scale, tmp = sb("scale4", [P, 2], F32), sb("tmp4", [P, 2], F32)
        raw_in, maxed, all_maxed, own = [sem(f"raw_in{c}") for c in range(3)], sem("maxed4"), sem("all_maxed"), sem("own4")
        scaled, high_ready4 = sem("scaled4"), sem("high_ready4")
        block = ctx.enter_context(nc.Block())

        @block.sync
        def _(sp):
            for counter in counters:
                sp.sem_inc(counter, START)
            sp.dma_start(raw1_a[:, :, :].rearrange("p a b -> p (a b)"), w["w1_a"]).then_inc(raw_in[0], 16)
            sp.dma_start(raw1_b[:, :, :].rearrange("p a b -> p (a b)"), w["w1_b"]).then_inc(raw_in[1], 16)
            sp.dma_start(raw2.rearrange("p e d -> p (e d)"), w["w2"]).then_inc(raw_in[2], 16)

        @block.gpsimd
        def _(pool):
            pool.wait_ge(maxed, START + 2)
            nc.gpsimd.partition_all_reduce(all_maxes[:, 0:2], maxes[:, 0:2], P, RMAX).then_inc(all_maxed, 1)
            pool.wait_ge(maxed, START + 3)
            nc.gpsimd.partition_all_reduce(all_maxes[:, 2:3], maxes[:, 2:3], P, RMAX).then_inc(all_maxed, 1)

        @block.scalar
        def _(act):
            act.wait_ge(scaled, START + 1)
            nc.scalar.activation(w1[:, :, 0, :], raw1_a[:, :, :], ACT.Copy, scale=scale[:, 0:1]).then_inc(high_ready4, 1)
            nc.scalar.activation(w1[:, :, 2, :], raw1_b[:, :, :], ACT.Copy, scale=scale[:, 0:1]).then_inc(high_ready4, 1)
            act.wait_ge(scaled, START + 2)
            nc.scalar.activation(w2[:, :, 0, :], raw2, ACT.Copy, scale=scale[:, 1:2]).then_inc(high_ready4, 1)

        @block.vector
        def _(dve):
            done = Done(dve, own)
            nc.vector.memset(eps[:, :], LN_EPS)

            def largest(c, part):
                dve.wait_ge(raw_in[c], START + 16)
                nc.vector.tensor_reduce(maxes[:, c:c + 1], part.rearrange("p a b -> p (a b)"), AX_X, ALU.max,
                                        apply_absolute_value=True).then_inc(maxed, 1)

            largest(0, raw1_a[:, :, :])
            largest(1, raw1_b[:, :, :])
            dve.wait_ge(all_maxed, START + 1)
            done(nc.vector.tensor_tensor(all_maxes[:, 1:2], all_maxes[:, 0:1], all_maxes[:, 1:2], ALU.max))
            power_of_two_scale(nc.vector, done, all_maxes[:, 1:2], scale[:, 0:1], unscale[:, 0:1], tmp[:, 0:1])
            nc.vector.memset(tmp[:, 0:1], 0.0).then_inc(scaled, 1)
            largest(2, raw2)
            dve.wait_ge(all_maxed, START + 2)
            power_of_two_scale(nc.vector, done, all_maxes[:, 2:3], scale[:, 1:2], unscale[:, 1:2], tmp[:, 1:2])
            nc.vector.memset(tmp[:, 1:2], 0.0).then_inc(scaled, 1)
            dve.wait_ge(high_ready4, START + 1)
            done(nc.vector.scalar_tensor_tensor(w1[:, :, 1, :], raw1_a[:, :, :], scale[:, 0:1], w1[:, :, 0, :], ALU.mult, ALU.subtract))
            dve.wait_ge(high_ready4, START + 2)
            done(nc.vector.scalar_tensor_tensor(w1[REST:P, :, 2, :], raw1_b[REST:P, :, :], scale[REST:P, 0:1], w1[REST:P, :, 2, :],
                                                ALU.mult, ALU.subtract))
            dve.wait_ge(high_ready4, START + 3)
            done(nc.vector.scalar_tensor_tensor(w2[:, :, 1, :], raw2, scale[:, 1:2], w2[:, :, 0, :], ALU.mult, ALU.subtract))


def route(nc, h, att, ident, small_in_dram, keep, rows, soft_rows_out):
    with ExitStack() as ctx:
        sb = lambda name, shape, dt: ctx.enter_context(nc.sbuf_tensor(name, shape, dt))
        ps = lambda name, shape, dt: ctx.enter_context(nc.psum_tensor(name, shape, dt))
        counters = []

        def sem(name):
            counters.append(ctx.enter_context(nc.semaphore(name)))
            return counters[-1]

        REST, HALF = DIM - P, DIM // 2
        small = {}
        for name in ("wp_a", "wp_b", "wr1_a", "wr1_b", "br1", "wr2", "br2", "b_proj", "earlier", "limits", "before", "tile_numbers"):
            small[name] = sb("c_" + name, list(small_in_dram[name].shape), F32)
        eye, ones = sb("eye4", [P, P], F32), sb("ones4", [P, P], F32)
        numbers, eps, x_all = keep["numbers"], keep["eps"], keep["x_all"]
        two = lambda name, shape, dt: [sb(f"{name}{a}", shape, dt) for a in range(2)]
        h_sb, att_sb = two("h_sb4", [P, TB, DIM], F32), two("att_sb4", [P, TB, DIM], F32)
        at_a, at_b = sb("at_a", [P, TOKENS], F32), sb("at_b", [REST, TOKENS], F32)
        z = sb("z", [P, TB, DIM], F32)
        stats, mean_var = sb("stats", [P, TB, 6], F32), sb("mean_var", [P, TB, 2], F32)
        std, inv_std = sb("std", [P, TB], F32), sb("inv_std", [P, TB], F32)
        x = two("x4", [P, TB, DIM], F32)
        x_stage = two("x_stage", [P, TB, DIM], F32)
        xt_a, xt_b = sb("xt_a", [P, TOKENS], F32), sb("xt_b", [REST, TOKENS], F32)
        hidden = sb("hidden", [HALF, 2, TOKENS], F32)
        score = sb("score", [P, TB, EXPERTS], F32)
        best, where = sb("best", [P, TB, 8], F32), sb("where", [P, TB, 8], U32)
        pick = sb("pick", [P, TOP, TB], F32)
        gap, ratio, total = sb("gap", [P, TB], F32), sb("ratio", [P, TB], F32), sb("total", [P, TB], F32)
        share = sb("share", [P, TOP, TB], F32)
        chosen = sb("chosen", [P, TOP, TB, EXPERTS], F32)
        mask, seen = sb("mask", [P, TB, EXPERTS], F32), sb("seen", [P, TB + 1, EXPERTS], F32)
        ranked, rank = sb("ranked", [P, TOP, TB, EXPERTS], F32), sb("rank", [P, PICKS], F32)
        slots = two("slots", [P, PICKS], U32)
        idle, idle_pool, padding = sb("idle4", [P, 1], F32), sb("idle_pool4", [P, 1], F32), sb("padding", [P, TB, DIM], F32)
        count, tiles, start = sb("count", [P, EXPERTS], F32), sb("tiles", [P, EXPERTS], F32), sb("start", [P, EXPERTS], F32)
        over, mine = sb("over", [P, EXPERTS, LIMITS], F32), sb("mine", [P, EXPERTS, EXPERTS], F32)
        through = sb("through", [P, EXPERTS], F32)
        passed, passed_tiles = sb("passed", [P, TILES, EXPERTS], F32), sb("passed_tiles", [P, TILES, EXPERTS], F32)
        of, gone, used = sb("of", [P, TILES], F32), sb("gone", [P, TILES], F32), sb("used", [P, TILES], F32)
        pad_row = sb("pad_row", [P, EXPERTS], I32)
        turned_ps, rows_ps = ps("turned_ps", [P, 2, 512], F32), ps("rows_ps", [P, 2, 512], F32)
        rows4 = rows_ps[:, :, :].rearrange("p a (b n) -> p (a b) n", b=2)[:, :, 0:DIM]
        hidden_ps, score_ps, rank_ps = ps("hidden_ps", [HALF, 2, 512], F32), ps("score_ps", [P, 512], F32), ps("rank_ps", [P, 512], F32)

        small_in, consts, wait_taken = sem("small_in"), sem("consts4"), sem("wait_taken")
        h_in, att_in = [sem(f"h_in4{a}") for a in range(2)], [sem(f"att_in4{a}") for a in range(2)]
        turned, turned_read, projected = sem("turned4"), sem("turned_read"), sem("projected")
        z_steps, z_ready, std_ready, x_steps, x_ready, x_kept = (
            sem("z_steps"), sem("z_ready"), sem("std_ready"), sem("x_steps4"), sem("x_ready4"), sem("x_kept"))
        x_turned, xt_ready = sem("x_turned"), sem("xt_ready")
        hidden_up, hidden_ready, scored, score_steps, gap_ready, ratio_ready = (
            sem("hidden_up"), sem("hidden_ready"), sem("scored"), sem("score_steps"), sem("gap_ready"), sem("ratio_ready"))
        route_steps, mask_steps, mask_ready, rank_up, rank_steps, slots_ready = (
            sem("route_steps"), sem("mask_steps"), sem("mask_ready"), sem("rank_up"), sem("rank_steps"), sem("slots_ready"))
        staged_x = sem("staged_x")
        counted, table_steps, pads_ready, pads_out = sem("counted"), sem("table_steps"), sem("pads_ready"), sem("pads_out")
        block = ctx.enter_context(nc.Block())
        IN_COUNT = len(small) + 2

        def in_turn(eng, counter, i, a, per):
            if isinstance(i, int):
                eng.wait_ge(counter, START + (i - a) // 2 * per + per)
            else:
                eng.wait_ge(counter, START + i * (per // 2) + (per - per // 2 * a))

        @block.sync
        def _(sp):
            for counter in counters:
                sp.sem_inc(counter, START)
            for name in small:
                src = small_in_dram[name]
                sp.dma_start(small[name][:, :] if len(src.shape) == 2 else small[name][:, :, :], src).then_inc(small_in, 16)
            sp.dma_start(eye[:, :], ident).then_inc(small_in, 16)
            sp.dma_start(numbers[:, :], small_in_dram["numbers"]).then_inc(small_in, 16)

            def load(i, a):
                if not early(i, 2):
                    sp.wait_ge(turned, START + i - 1)
                    sp.wait_ge(z_ready, START + i - 1)
                sp.dma_start(att_sb[a][:, :, :], att[bass.ds(i, 1), :, :, :].rearrange("a p b d -> (a p) b d")).then_inc(att_in[a], 16)
                sp.dma_start(h_sb[a][:, :, :], h[bass.ds(i, 1), :, :, :].rearrange("a p b d -> (a p) b d")).then_inc(h_in[a], 16)

            staged(sp, load, nothing)
            sp.wait_ge(pads_ready, START + 2)
            for e in range(EXPERTS):
                row = sp.value_load(pad_row[0:1, e:e + 1], min_val=0, max_val=EXPERTS * REGION - TILE)
                sp.dma_start(rows[bass.ds(row, TILE), :].rearrange("(b p) d -> p b d", p=P), padding[:, :, :]).then_inc(pads_out, 16)
            sp.wait_ge(pads_out, START + 16 * EXPERTS)

        @block.gpsimd
        def _(pool):
            pool.wait_ge(consts, START + 3)

            def append(i, a):
                pool.wait_ge(slots_ready, START + i + 1)
                pool.wait_ge(staged_x, START + i + 1)
                pool.wait_ge(wait_taken, START + i)
                nc.gpsimd.tensor_tensor(idle_pool[:, :], eps[:, :], eps[:, :], ALU.add).then_inc(wait_taken, 1)
                for c in range(PICKS):
                    nc.gpsimd.indirect_dma_start(rows, bass.IndirectOffsetOnAxis(ap=slots[a][:, c:c + 1], axis=0),
                                                 x_stage[a][:, c % TB, :], None).then_inc(soft_rows_out[a], 16)

            staged(pool, nothing, nothing, nothing, nothing, nothing, append)
            for a in range(2):
                pool.wait_ge(soft_rows_out[a], 16 * PICKS * IMAGES // 2)

        @block.tensor
        def _(pe):
            pe.wait_ge(small_in, START + 16 * IN_COUNT)
            pe.wait_ge(consts, START + 3)

            def turn_att(i, a):
                in_turn(pe, att_in[a], i, a, 16)
                pe.wait_ge(turned_read, START + i * 2)
                if not early(i, 3):
                    pe.wait_ge(xt_ready, START + i * 2 - 4)
                for b in range(TB):
                    nc.tensor.transpose(turned_ps[:, 0, b * P:(b + 1) * P], att_sb[a][:, b, 0:P], eye[:, :])
                    last = nc.tensor.transpose(turned_ps[0:REST, 1, b * P:(b + 1) * P], att_sb[a][:, b, P:DIM], eye[:, :])
                last.then_inc(turned, 1)

            def project_att(j, a):
                pe.wait_ge(turned_read, START + j * 2 + 2)
                pe.wait_ge(z_ready, START + j)
                for b in range(TB):
                    cols = slice(b * P, (b + 1) * P)
                    nc.tensor.matmul(rows4[:, b, :], at_a[:, cols], small["wp_a"][:, :], start=True, stop=False)
                    last = nc.tensor.matmul(rows4[:, b, :], at_b[:, cols], small["wp_b"][:, :], start=False, stop=True)
                last.then_inc(projected, 1)

            def turn_x(j, a):
                pe.wait_ge(x_ready, START + j + 1)
                both = min(j * 2 + 6, 2 * IMAGES) if isinstance(j, int) else j * 2 + 6
                pe.wait_ge(turned_read, START + both)
                pe.wait_ge(xt_ready, START + j * 2)
                for b in range(TB):
                    nc.tensor.transpose(turned_ps[:, 0, b * P:(b + 1) * P], x[a][:, b, 0:P], eye[:, :])
                    last = nc.tensor.transpose(turned_ps[0:REST, 1, b * P:(b + 1) * P], x[a][:, b, P:DIM], eye[:, :])
                last.then_inc(x_turned, 1)

            def router_hidden(j, a):
                pe.wait_ge(xt_ready, START + j * 2 + 2)
                pe.wait_ge(hidden_ready, START + j * 2)
                for half in range(2):
                    cols = slice(half * HALF, (half + 1) * HALF)
                    nc.tensor.matmul(hidden_ps[:, half, :], small["wr1_a"][:, cols], xt_a[:, :], start=True, stop=False)
                    last = nc.tensor.matmul(hidden_ps[:, half, :], small["wr1_b"][:, cols], xt_b[:, :], start=False, stop=True)
                last.then_inc(hidden_up, 1)

            def router_score(j, a):
                pe.wait_ge(hidden_ready, START + j * 2 + 2)
                pe.wait_ge(gap_ready, START + j)
                for b in range(TB):
                    for half in range(2):
                        last = nc.tensor.matmul(score_ps[:, b * EXPERTS:(b + 1) * EXPERTS], hidden[:, half, b * P:(b + 1) * P],
                                                small["wr2"][:, half, :], start=(half == 0), stop=(half == 1))
                last.then_inc(scored, 1)

            def places(j, a):
                pe.wait_ge(mask_steps, START + j * (TB + 2) + (TB + 2))
                pe.wait_ge(slots_ready, START + j)
                for b in range(TB):
                    out = rank_ps[:, b * EXPERTS:(b + 1) * EXPERTS]
                    nc.tensor.matmul(out, small["earlier"][:, :], mask[:, b, :], start=True, stop=False)
                    last = nc.tensor.matmul(out, ones[:, :], seen[:, b, :], start=False, stop=True)
                last.then_inc(rank_up, 1)

            staged(pe, turn_att, project_att, turn_x, router_hidden, router_score, places)
            pe.wait_ge(slots_ready, START + IMAGES)
            nc.tensor.matmul(rank_ps[:, 0:EXPERTS], ones[:, :], seen[:, TB, :], start=True, stop=True).then_inc(counted, 1)

        @block.scalar
        def _(act):
            act.wait_ge(small_in, START + 16 * IN_COUNT)

            def read_turned(i, a):
                act.wait_ge(turned, START + i + 1)
                act.wait_ge(projected, START + i)
                nc.scalar.activation(at_a[:, :], turned_ps[:, 0, :], ACT.Copy).then_inc(turned_read, 1)
                nc.scalar.activation(at_b[:, :], turned_ps[0:REST, 1, :], ACT.Copy).then_inc(turned_read, 1)

            def deviation(j, a):
                act.wait_ge(z_ready, START + j + 1)
                nc.scalar.activation(std[:, :], mean_var[:, :, 1], ACT.Sqrt, bias=eps[:, 0:1]).then_inc(std_ready, 1)

            def read_x(j, a):
                act.wait_ge(x_turned, START + j + 1)
                act.wait_ge(hidden_up, START + j)
                nc.scalar.activation(xt_a[:, :], turned_ps[:, 0, :], ACT.Copy).then_inc(xt_ready, 1)
                nc.scalar.activation(xt_b[:, :], turned_ps[0:REST, 1, :], ACT.Copy).then_inc(xt_ready, 1)
                nc.scalar.activation(x_all[:, bass.ds(j * TB, TB), :], x[a][:, :, :], ACT.Copy).then_inc(x_kept, 1)

            def router_relu(j, a):
                act.wait_ge(hidden_up, START + j + 1)
                act.wait_ge(scored, START + j)
                for half in range(2):
                    nc.scalar.activation(hidden[:, half, :], hidden_ps[:, half, :], ACT.Relu,
                                         bias=small["br1"][:, half:half + 1]).then_inc(hidden_ready, 1)

            def gap_exp(j, a):
                act.wait_ge(gap_ready, START + j + 1)
                act.wait_ge(route_steps, START + j * 2)
                nc.scalar.activation(ratio[:, :], gap[:, :], ACT.Exp).then_inc(ratio_ready, 1)

            def stage_x(j, a):
                act.wait_ge(x_kept, START + j + 1)
                if not early(j, 2):
                    soft_in_turn(act, soft_rows_out[a], j - 2, a)
                nc.scalar.activation(x_stage[a][:, :, :], x_all[:, bass.ds(j * TB, TB), :], ACT.Copy).then_inc(staged_x, 1)

            staged(act, read_turned, deviation, read_x, router_relu, gap_exp, stage_x, nothing, nothing)

        @block.vector
        def _(dve):
            nc.vector.memset(ones[:, :], 1.0).then_inc(consts, 1)
            nc.vector.memset(seen[:, TB, :], 0.0).then_inc(consts, 1)
            nc.vector.memset(padding[:, :, :], 0.0).then_inc(consts, 1)
            dve.wait_ge(small_in, START + 16 * IN_COUNT)
            dve.wait_ge(consts, START + 3)

            def norm(j, a):
                dve.wait_ge(projected, START + j + 1)
                in_turn(dve, h_in[a], j, a, 16)
                nc.vector.tensor_tensor(z[:, :, :], rows4, h_sb[a][:, :, :], ALU.add).then_inc(z_steps, 1)
                dve.wait_ge(z_steps, START + j * 6 + 1)
                nc.vector.tensor_tensor(z[:, :, :], z[:, :, :], small["b_proj"][:, :].unsqueeze(1).to_broadcast([P, TB, DIM]),
                                        ALU.add).then_inc(z_steps, 1)
                dve.wait_ge(z_steps, START + j * 6 + 2)
                for b in range(TB):
                    nc.vector.bn_stats(stats[:, b, :], z[:, b, :]).then_inc(z_steps, 1)
                dve.wait_ge(z_steps, START + j * 6 + 6)
                nc.vector.memset(idle[:, :], 0.0)
                for b in range(TB):
                    last = nc.vector.bn_aggr(mean_var[:, b, :], stats[:, b, :])
                last.then_inc(z_ready, 1)
                dve.wait_ge(std_ready, START + j + 1)
                nc.vector.reciprocal(inv_std[:, :], std[:, :]).then_inc(x_steps, 1)
                dve.wait_ge(x_steps, START + j + 1)
                if not early(j, 2):
                    dve.wait_ge(x_turned, START + j - 1)
                    dve.wait_ge(x_kept, START + j - 1)
                for b in range(TB):
                    last = nc.vector.tensor_scalar(x[a][:, b, :], z[:, b, :], mean_var[:, b, 0:1], inv_std[:, b:b + 1],
                                                   ALU.subtract, ALU.mult)
                last.then_inc(x_ready, 1)
                dve.wait_ge(x_ready, START + j + 1)

            def choose(j, a):
                S, M = 10, TB + 2
                dve.wait_ge(scored, START + j + 1)
                nc.vector.tensor_tensor(score[:, :, :], score_ps[:, 0:TB * EXPERTS].rearrange("p (b e) -> p b e", b=TB),
                                        small["br2"][:, :].unsqueeze(1).to_broadcast([P, TB, EXPERTS]), ALU.add).then_inc(score_steps, 1)
                dve.wait_ge(score_steps, START + j * S + 1)
                nc.vector.memset(idle[:, :], 0.0)
                for b in range(TB):
                    nc.vector.max(best[:, b, :], score[:, b, :]).then_inc(score_steps, 1)
                dve.wait_ge(score_steps, START + j * S + 5)
                nc.vector.memset(idle[:, :], 0.0)
                for b in range(TB):
                    nc.vector.max_index(where[:, b, :], best[:, b, :], score[:, b, :]).then_inc(score_steps, 1)
                nc.vector.tensor_tensor(gap[:, :], best[:, :, 1], best[:, :, 0], ALU.subtract).then_inc(gap_ready, 1)
                dve.wait_ge(score_steps, START + j * S + 9)
                nc.vector.tensor_copy(pick[:, :, :], where[:, :, 0:TOP].rearrange("p b w -> p w b")).then_inc(score_steps, 1)
                dve.wait_ge(score_steps, START + j * S + 10)
                flat = pick[:, :, :].rearrange("p w b -> p (w b)")
                nc.vector.tensor_copy(keep["pick_all"][:, bass.ds(j, 1), :].rearrange("p a c -> p (a c)"), flat)
                nc.vector.tensor_tensor(chosen[:, :, :, :].rearrange("p w b e -> p (w b) e"),
                                        numbers[:, :].unsqueeze(1).to_broadcast([P, PICKS, EXPERTS]),
                                        flat.unsqueeze(2).to_broadcast([P, PICKS, EXPERTS]), ALU.is_equal).then_inc(mask_steps, 1)
                dve.wait_ge(rank_up, START + j)
                nc.vector.tensor_copy(seen[:, 0, :], seen[:, TB, :]).then_inc(mask_steps, 1)
                dve.wait_ge(mask_steps, START + j * M + 2)
                nc.vector.tensor_tensor(mask[:, :, :], chosen[:, 0, :, :], chosen[:, 1, :, :], ALU.add).then_inc(mask_ready, 1)
                dve.wait_ge(mask_ready, START + j + 1)
                for b in range(TB):
                    nc.vector.tensor_tensor(seen[:, b + 1, :], seen[:, b, :], mask[:, b, :], ALU.add).then_inc(mask_steps, 1)
                    dve.wait_ge(mask_steps, START + j * M + (b + 3))
                dve.wait_ge(ratio_ready, START + j + 1)
                nc.vector.tensor_scalar(total[:, :], ratio[:, :], 1.0, None, ALU.add).then_inc(route_steps, 1)
                dve.wait_ge(route_steps, START + j * 4 + 1)
                nc.vector.reciprocal(share[:, 0, :], total[:, :]).then_inc(route_steps, 1)
                dve.wait_ge(route_steps, START + j * 4 + 2)
                nc.vector.tensor_tensor(share[:, 1, :], ratio[:, :], share[:, 0, :], ALU.mult).then_inc(route_steps, 1)
                dve.wait_ge(route_steps, START + j * 4 + 3)
                nc.vector.tensor_copy(keep["share_all"][:, bass.ds(j, 1), :].rearrange("p a c -> p (a c)"),
                                      share[:, :, :].rearrange("p w b -> p (w b)")).then_inc(route_steps, 1)
                dve.wait_ge(route_steps, START + j * 4 + 4)

            def slots_of(j, a):
                dve.wait_ge(rank_up, START + j + 1)
                nc.vector.tensor_tensor(ranked[:, :, :, :], chosen[:, :, :, :],
                                        rank_ps[:, 0:TB * EXPERTS].rearrange("p (b e) -> p b e", b=TB).unsqueeze(1)
                                        .to_broadcast([P, TOP, TB, EXPERTS]), ALU.mult).then_inc(rank_steps, 1)
                dve.wait_ge(rank_steps, START + j * 3 + 1)
                nc.vector.tensor_reduce(rank[:, :], ranked[:, :, :, :].rearrange("p w b e -> p (w b) e"), AX_X, ALU.add).then_inc(rank_steps, 1)
                dve.wait_ge(rank_steps, START + j * 3 + 2)
                nc.vector.tensor_copy(keep["rank_all"][:, bass.ds(j, 1), :].rearrange("p a c -> p (a c)"), rank[:, :]).then_inc(rank_steps, 1)
                if not early(j, 2):
                    soft_in_turn(dve, soft_rows_out[a], j - 2, a)
                nc.vector.scalar_tensor_tensor(slots[a][:, :], pick[:, :, :].rearrange("p w b -> p (w b)"), float(REGION), rank[:, :],
                                               ALU.mult, ALU.add).then_inc(slots_ready, 1)
                dve.wait_ge(slots_ready, START + j + 1)
                dve.wait_ge(rank_steps, START + j * 3 + 3)

            def slots_then_choice(j, a):
                if not early(j, 1):
                    slots_of(j - 1, 1 - a)
                choose(j, a)

            staged(dve, nothing, norm, nothing, nothing, slots_then_choice, nothing, nothing, nothing)
            slots_of(IMAGES - 1, (IMAGES - 1) % 2)

            done = Done(dve, table_steps)
            dve.wait_ge(counted, START + 1)
            done(nc.vector.tensor_copy(count[:, :], rank_ps[:, 0:EXPERTS]))
            wide = lambda t, shape: t.to_broadcast(shape)
            full = [P, EXPERTS, LIMITS]
            done(nc.vector.tensor_tensor(over[:, :, :], wide(count[:, :].unsqueeze(2), full), wide(small["limits"][:, :].unsqueeze(1), full), ALU.is_gt))
            done(nc.vector.tensor_reduce(tiles[:, :], over[:, :, :], AX_X, ALU.add))
            full = [P, EXPERTS, EXPERTS]
            done(nc.vector.tensor_tensor(mine[:, :, :], wide(tiles[:, :].unsqueeze(1), full), small["before"][:, :, :], ALU.mult))
            done(nc.vector.tensor_reduce(start[:, :], mine[:, :, :], AX_X, ALU.add))
            done(nc.vector.tensor_tensor(through[:, :], start[:, :], tiles[:, :], ALU.add))
            done(nc.vector.tensor_scalar(keep["first_slot"][:, :], start[:, :], float(TILE), None, ALU.mult))
            full = [P, TILES, EXPERTS]
            done(nc.vector.tensor_tensor(passed[:, :, :], wide(through[:, :].unsqueeze(1), full),
                                         wide(small["tile_numbers"][:, :].unsqueeze(2), full), ALU.is_le))
            done(nc.vector.tensor_reduce(of[:, :], passed[:, :, :], AX_X, ALU.add))
            done(nc.vector.tensor_tensor(passed_tiles[:, :, :], passed[:, :, :], wide(tiles[:, :].unsqueeze(1), full), ALU.mult))
            done(nc.vector.tensor_reduce(gone[:, :], passed_tiles[:, :, :], AX_X, ALU.add))
            last_region = float((EXPERTS - 1) * REGION)
            done(nc.vector.tensor_scalar(used[:, :], of[:, :], EXPERTS - 0.5, None, ALU.is_lt))
            done(nc.vector.tensor_tensor(gone[:, :], small["tile_numbers"][:, :], gone[:, :], ALU.subtract))
            done(nc.vector.tensor_scalar(gone[:, :], gone[:, :], float(TILE), -last_region, ALU.mult, ALU.add))
            done(nc.vector.scalar_tensor_tensor(gone[:, :], of[:, :], float(REGION), gone[:, :], ALU.mult, ALU.add))
            done(nc.vector.tensor_tensor(gone[:, :], gone[:, :], used[:, :], ALU.mult))
            done(nc.vector.tensor_scalar(keep["tile_row"][:, :], gone[:, :], last_region, None, ALU.add))
            done(nc.vector.tensor_scalar(keep["tile_expert"][:, :], of[:, :], float(EXPERTS - 1), None, ALU.min))
            done(nc.vector.scalar_tensor_tensor(pad_row[:, :], numbers[:, :], float(REGION), count[:, :], ALU.mult, ALU.add))
            nc.vector.memset(idle[:, :], 0.0).then_inc(pads_ready, 2)


def run_experts(nc, ident, small_in_dram, keep, rows, results):
    with ExitStack() as ctx:
        sb = lambda name, shape, dt: ctx.enter_context(nc.sbuf_tensor(name, shape, dt))
        ps = lambda name, shape, dt: ctx.enter_context(nc.psum_tensor(name, shape, dt))
        counters = []

        def sem(name):
            counters.append(ctx.enter_context(nc.semaphore(name)))
            return counters[-1]

        REST = DIM - P
        w1, w2, unscale, tile_expert, tile_row = (
            keep["w1"], keep["w2"], keep["unscale"], keep["tile_expert"], keep["tile_row"])
        eye = sb("eye5", [P, P], F32)
        b1, b2 = sb("b1", [P, EXPERTS * FB], F32), sb("b2", [P, EXPERTS, DIM], F32)
        zeros = sb("zeros", [P, 2 * DIM], F16)
        two = lambda name, shape, dt: [sb(f"{name}{a}", shape, dt) for a in range(2)]
        x_in_sb = two("x_in_sb", [P, TB, 2 * P], F32)
        xt_a, xt_m = sb("xt_a5", [P, TOKENS], F32), sb("xt_m5", [P, TOKENS], F32)
        xh_a, xl_a, xh_m, xl_m = (two(name, [P, TOKENS], F16) for name in ("xh_a", "xl_a", "xh_m", "xl_m"))
        mid = [sb(f"mid{n}", [P, TOKENS], F32) for n in range(R)]
        mid_h = [sb(f"mid_h{n}", [P, TOKENS], F16) for n in range(R)]
        mid_l = [sb(f"mid_l{n}", [P, TOKENS], F16) for n in range(R)]
        y_sb = two("y_sb", [P, TB, DIM], F32)
        up_ps = [ps(f"up_ps{n}", [P, TOKENS], F32) for n in range(R)]
        down = ps("down", [P, TB, 256], F32)
        turned_ps = ps("turned_ps5", [P, 2, 512], F32)

        consts_in, consts_set = sem("consts_in5"), sem("consts_set5")
        x_in, y_out = [sem(f"x_in5{a}") for a in range(2)], [sem(f"y_out{a}") for a in range(2)]
        x_turned, xt_ready, x_split = sem("x_turned5"), sem("xt_ready5"), sem("x_split")
        ring = lambda name: [sem(f"{name}{n}") for n in range(R)]
        up_ready, mid_parts, mid_split, mid_used = ring("up_ready"), ring("mid_parts"), ring("mid_split"), ring("mid_used")
        down_ready, y_ready = sem("down_ready"), sem("y_ready")
        LAPS = FB // R
        BANKS = TB // 2
        block = ctx.enter_context(nc.Block())

        def tiles(eng, step, front, late, expert):
            for t in sorted(front):
                front[t](0, 0, None)

            def tile(i, a, before=True, ahead=True):
                e = expert(i)
                following = expert(i + 1) if ahead else None
                for t in range(FB):
                    step(i, a, t, e, following)
                    if before and t in late:
                        late[t](i - 1, 1 - a)
                    if ahead and t in front:
                        front[t](i + 1, 1 - a, following)

            tile(0, 0, before=False)
            with eng.Fori(0, (TILES - 3) // 2) as pair:
                tile(pair * 2 + 1, 1)
                tile(pair * 2 + 2, 0)
            tile(TILES - 2, 1)
            tile(TILES - 1, 0, ahead=False)
            for t in sorted(late):
                late[t](TILES - 1, 0)

        def expert_of(eng):
            return lambda i: eng.value_load(tile_expert[0:1, bass.ds(i, 1)], min_val=0, max_val=EXPERTS - 1)

        def no_expert(i):
            return i

        def parts_used(eng, i, t):
            n = t % R
            if n < R - 1:
                eng.wait_ge(mid_used[n], START + i * LAPS + t // R)
            elif t // R == 0:
                eng.wait_ge(down_ready, START + i * BANKS)
            else:
                eng.wait_ge(mid_used[n], START + i * (LAPS - 1) + t // R)

        def in_turn(eng, counter, i, a, per):
            if isinstance(i, int):
                eng.wait_ge(counter, START + (i - a) // 2 * per + per)
            else:
                eng.wait_ge(counter, START + i * (per // 2) + (per - per // 2 * a))

        @block.sync
        def _(sp):
            for counter in counters:
                sp.sem_inc(counter, START)
            for dst, src in ((eye[:, :], ident), (b1[:, :], small_in_dram["b1"]), (b2[:, :, :], small_in_dram["b2"])):
                sp.dma_start(dst, src).then_inc(consts_in, 16)

            def load(i, a):
                if not early(i, 2):
                    sp.wait_ge(x_turned, START + i - 1)
                row = sp.value_load(tile_row[0:1, bass.ds(i, 1)], min_val=0, max_val=EXPERTS * REGION - TILE)
                src = rows[bass.ds(row, TILE), :].rearrange("(b p) d -> p b d", p=P)
                sp.dma_start(x_in_sb[a][:, :, 0:DIM], src).then_inc(x_in[a], 16)
                sp.dma_start(x_in_sb[a][:, :, DIM:2 * P], src[:, :, P:DIM]).then_inc(x_in[a], 16)

            def store(i, a):
                sp.wait_ge(y_ready, START + i * BANKS + BANKS)
                sp.dma_start(results[bass.ds(i * TILE, TILE), :].rearrange("(b p) d -> p b d", p=P), y_sb[a][:, :, :]).then_inc(y_out[a], 16)

            load(0, 0)
            load(1, 1)
            load(2, 0)
            with sp.Fori(0, (TILES - 3) // 2) as pair:
                for a in range(2):
                    i = pair * 2 + a
                    load(i + 3, 1 - a)
                    store(i, a)
            for i in range(TILES - 3, TILES):
                store(i, i % 2)
            sp.wait_ge(y_out[0], START + 16 * (TILES // 2 + 1))
            sp.wait_ge(y_out[1], START + 16 * (TILES // 2))

        @block.tensor
        def _(pe):
            pe.wait_ge(consts_in, START + 16 * 3)
            pe.wait_ge(consts_set, START + 3)

            def turn(j, a, e):
                in_turn(pe, x_in[a], j, a, 32)
                pe.wait_ge(xt_ready, START + j * 2)
                for b in range(TB):
                    nc.tensor.transpose(turned_ps[:, 0, b * P:(b + 1) * P], x_in_sb[a][:, b, 0:P], eye[:, :])
                    last = nc.tensor.transpose(turned_ps[:, 1, b * P:(b + 1) * P], x_in_sb[a][:, b, P:2 * P], eye[:, :])
                last.then_inc(x_turned, 1)

            def up(i, a, f, e):
                n = f % R
                if f == 0:
                    pe.wait_ge(x_split, START + (i + 1) * 4)
                pe.wait_ge(mid_parts[n], START + i * (2 * LAPS) + 2 * (f // R))
                cols = slice(f * P, (f + 1) * P)
                weights = lambda part: w1[:, bass.ds(e, 1), part, cols].rearrange("p a n -> p (a n)")
                nc.tensor.matmul(up_ps[n][:, :], weights(0), xh_a[a][:, :], start=True, stop=False)
                nc.tensor.matmul(up_ps[n][:, :], weights(0), xl_a[a][:, :], start=False, stop=False)
                nc.tensor.matmul(up_ps[n][:, :], weights(1), xh_a[a][:, :], start=False, stop=False)
                nc.tensor.matmul(up_ps[n][:, :], weights(2), xh_m[a][:, :], start=False, stop=False)
                nc.tensor.matmul(up_ps[n][:, :], weights(2), xl_m[a][:, :], start=False, stop=True).then_inc(up_ready[n], 1)

            def down_block(i, f, e):
                n = f % R
                pe.wait_ge(mid_split[n], START + i * LAPS + (f // R + 1))
                weights = lambda part: w2[:, bass.ds(e * FB + f, 1), part, :].rearrange("p a n -> p (a n)")
                for b in range(TB):
                    if f == 0 and b % 2 == 0:
                        if not early(i, 1):
                            pe.wait_ge(y_ready, START + i * BANKS + (b // 2 + 1 - BANKS))
                        nc.tensor.matmul(down[:, b:b + 2, 0:DIM], zeros[:, 0:P], zeros[:, :], start=True, stop=False)
                    cols = slice(b * P, (b + 1) * P)
                    out = down[:, b, 0:DIM]
                    nc.tensor.matmul(out, mid_h[n][:, cols], weights(0), start=False, stop=False)
                    nc.tensor.matmul(out, mid_h[n][:, cols], weights(1), start=False, stop=False)
                    last = nc.tensor.matmul(out, mid_l[n][:, cols], weights(0), start=False, stop=(f == FB - 1 and b % 2 == 1))
                    if f == FB - 1 and b % 2:
                        last.then_inc(down_ready, 1)
                if f < FB - 1:
                    last.then_inc(mid_used[n], 1)

            def step(i, a, t, e, following):
                if early(i, 1) and t == 0:
                    up(i, a, 0, e)
                    up(i, a, 1, e)
                if t + 2 < FB:
                    up(i, a, t + 2, e)
                elif following is not None:
                    up(i + 1, 1 - a, t + 2 - FB, following)
                down_block(i, t, e)

            tiles(pe, step, {0: turn}, {}, expert_of(pe))

        @block.scalar
        def _(act):
            act.wait_ge(consts_in, START + 16 * 3)

            def step(i, a, t, e, following):
                n = t % R
                act.wait_ge(up_ready[n], START + i * LAPS + (t // R + 1))
                act.wait_ge(mid_split[n], START + i * LAPS + t // R)
                parts_used(act, i, t)
                for out in (mid[n], mid_h[n]):
                    nc.scalar.activation(out[:, :], up_ps[n][:, :], ACT.Relu, bias=b1[:, bass.ds(e * FB + t, 1)],
                                         scale=unscale[:, 0:1]).then_inc(mid_parts[n], 1)

            def read_x(j, a, e):
                act.wait_ge(x_turned, START + j + 1)
                act.wait_ge(x_split, START + j * 4)
                nc.scalar.activation(xt_a[:, :], turned_ps[:, 0, :], ACT.Copy).then_inc(xt_ready, 1)
                nc.scalar.activation(xt_m[:, :], turned_ps[:, 1, :], ACT.Copy).then_inc(xt_ready, 1)

            tiles(act, step, {2: read_x}, {}, expert_of(act))

        @block.vector
        def _(dve):
            nc.vector.memset(zeros[:, :], 0.0).then_inc(consts_set, 1)
            for a in range(2):
                nc.vector.memset(xl_m[a][:, :], 0.0).then_inc(consts_set, 1)
            dve.wait_ge(consts_set, START + 3)
            dve.wait_ge(consts_in, START + 16 * 3)

            def step(i, a, t, e, following):
                n = t % R
                dve.wait_ge(mid_parts[n], START + i * (2 * LAPS) + 2 * (t // R + 1))
                nc.vector.tensor_tensor(mid_l[n][:, :], mid[n][:, :], mid_h[n][:, :], ALU.subtract).then_inc(mid_split[n], 1)

            def read_down(i, a):
                e = expert_of(dve)(i)
                if not early(i, 2):
                    in_turn(dve, y_out[a], i - 2, a, 16)
                for bank in range(BANKS):
                    dve.wait_ge(down_ready, START + i * BANKS + (bank + 1))
                    two_blocks = slice(2 * bank, 2 * bank + 2)
                    nc.vector.scalar_tensor_tensor(y_sb[a][:, two_blocks, :], down[:, two_blocks, 0:DIM], unscale[:, 1:2],
                                                   b2[:, bass.ds(e, 1), :].to_broadcast([P, 2, DIM]),
                                                   ALU.mult, ALU.add).then_inc(y_ready, 1)

            def split_x(j, a, e):
                dve.wait_ge(xt_ready, START + j * 2 + 2)
                if not early(j, 1):
                    for n in range(R):
                        dve.wait_ge(up_ready[n], START + (j - 1) * LAPS)
                nc.vector.tensor_copy(xh_a[a][:, :], xt_a[:, :]).then_inc(x_split, 1)
                nc.vector.tensor_copy(xh_m[a][:, :], xt_m[:, :]).then_inc(x_split, 1)

            def split_x_low(j, a, e):
                dve.wait_ge(x_split, START + j * 4 + 2)
                nc.vector.tensor_tensor(xl_a[a][:, :], xt_a[:, :], xh_a[a][:, :], ALU.subtract).then_inc(x_split, 1)
                nc.vector.tensor_tensor(xl_m[a][0:REST, :], xt_m[0:REST, :], xh_m[a][0:REST, :], ALU.subtract).then_inc(x_split, 1)

            tiles(dve, step, {2: split_x, 3: split_x_low}, {0: read_down}, no_expert)


def combine(nc, keep, results, out, soft_fetched):
    with ExitStack() as ctx:
        sb = lambda name, shape, dt: ctx.enter_context(nc.sbuf_tensor(name, shape, dt))
        counters = []

        def sem(name):
            counters.append(ctx.enter_context(nc.semaphore(name)))
            return counters[-1]

        two = lambda name, shape, dt: [sb(f"{name}{a}", shape, dt) for a in range(2)]
        ALL = IMAGES * PICKS
        chosen = sb("chosen6", [P, ALL, EXPERTS], F32)
        slot_all = sb("slot_all", [P, IMAGES, PICKS], F32)
        slots, share = two("slots6", [P, PICKS], U32), two("share6", [P, PICKS], F32)
        y = two("y6", [P, PICKS, DIM], F32)
        acc = two("acc6", [P, TB, DIM], F32)
        stats, mean_var = sb("stats6", [P, TB, 6], F32), sb("mean_var6", [P, TB, 2], F32)
        std, inv_std = sb("std6", [P, TB], F32), sb("inv_std6", [P, TB], F32)
        out_sb = two("out_sb", [P, TB, DIM], F32)
        idle, idle_pool = sb("idle6", [P, 1], F32), sb("idle_pool6", [P, 1], F32)
        steps, slots_ready = sem("steps6"), sem("slots_ready6")
        added, stat_steps, var_ready, std_ready, out_steps, out_ready = (
            sem("added"), sem("stat_steps"), sem("var_ready"), sem("std_ready6"), sem("out_steps"), sem("out_ready"))
        out_done, wait_taken = [sem(f"out_done{a}") for a in range(2)], sem("wait_taken6")
        block = ctx.enter_context(nc.Block())

        def in_turn(eng, counter, i, a, per):
            if isinstance(i, int):
                eng.wait_ge(counter, START + (i - a) // 2 * per + per)
            else:
                eng.wait_ge(counter, START + i * (per // 2) + (per - per // 2 * a))

        @block.sync
        def _(sp):
            for counter in counters:
                sp.sem_inc(counter, START)
            def store(i, a):
                sp.wait_ge(out_ready, START + i + 1)
                sp.dma_start(out[bass.ds(i, 1), :, :, :].rearrange("a p b d -> (a p) b d"), out_sb[a][:, :, :]).then_inc(out_done[a], 16)

            staged(sp, store)
            for a in range(2):
                sp.wait_ge(out_done[a], START + 16 * IMAGES // 2)

        @block.gpsimd
        def _(pool):
            def fetch(i, a):
                pool.wait_ge(slots_ready, START + i * 2 + 2)
                if not early(i, 2):
                    pool.wait_ge(added, START + (i - 1) * PICKS)
                pool.wait_ge(wait_taken, START + i)
                nc.gpsimd.tensor_tensor(idle_pool[:, :], keep["eps"][:, :], keep["eps"][:, :], ALU.add).then_inc(wait_taken, 1)
                for c in range(PICKS):
                    nc.gpsimd.indirect_dma_start(y[a][:, c, :], None, results,
                                                 bass.IndirectOffsetOnAxis(ap=slots[a][:, c:c + 1], axis=0)).then_inc(soft_fetched[a], 16)

            staged(pool, fetch, nothing)

        @block.scalar
        def _(act):
            def deviation(i, a):
                act.wait_ge(var_ready, START + i + 1)
                nc.scalar.activation(std[:, :], mean_var[:, :, 1], ACT.Sqrt, bias=keep["eps"][:, 0:1]).then_inc(std_ready, 1)

            staged(act, deviation)

        @block.vector
        def _(dve):
            done = Done(dve, steps)
            full = [P, ALL, EXPERTS]
            wide = lambda t: t.to_broadcast(full)
            pick = keep["pick_all"][:, :, :].rearrange("p i c -> p (i c)").unsqueeze(2)
            done(nc.vector.tensor_tensor(chosen[:, :, :], wide(keep["numbers"][:, :].unsqueeze(1)), wide(pick), ALU.is_equal))
            done(nc.vector.tensor_tensor(chosen[:, :, :], chosen[:, :, :], wide(keep["first_slot"][:, :].unsqueeze(1)), ALU.mult))
            flat = slot_all[:, :, :].rearrange("p i c -> p (i c)")
            done(nc.vector.tensor_reduce(flat, chosen[:, :, :], AX_X, ALU.add))
            done(nc.vector.tensor_tensor(flat, flat, keep["rank_all"][:, :, :].rearrange("p i c -> p (i c)"), ALU.add))

            def take(i, a):
                if not early(i, 2):
                    soft_in_turn(dve, soft_fetched[a], i - 2, a)
                nc.vector.tensor_copy(slots[a][:, :], slot_all[:, bass.ds(i, 1), :].rearrange("p a c -> p (a c)")).then_inc(slots_ready, 1)
                nc.vector.tensor_copy(share[a][:, :], keep["share_all"][:, bass.ds(i, 1), :].rearrange("p a c -> p (a c)")).then_inc(slots_ready, 1)

            def add(i, a):
                soft_in_turn(dve, soft_fetched[a], i, a)
                taken = min(i * 2 + 4, 2 * IMAGES) if isinstance(i, int) else i * 2 + 4
                dve.wait_ge(slots_ready, START + taken)
                nc.vector.memset(idle[:, :], 0.0)
                for b in range(TB):
                    nc.vector.scalar_tensor_tensor(acc[a][:, b, :], y[a][:, b, :], share[a][:, b:b + 1],
                                                   keep["x_all"][:, bass.ds(i * TB + b, 1), :].rearrange("p a d -> p (a d)"),
                                                   ALU.mult, ALU.add).then_inc(added, 1)
                dve.wait_ge(added, START + i * PICKS + TB)
                for b in range(TB):
                    nc.vector.scalar_tensor_tensor(acc[a][:, b, :], y[a][:, TB + b, :], share[a][:, TB + b:TB + b + 1], acc[a][:, b, :],
                                                   ALU.mult, ALU.add).then_inc(added, 1)
                dve.wait_ge(added, START + i * PICKS + PICKS)
                nc.vector.memset(idle[:, :], 0.0)
                for b in range(TB):
                    nc.vector.bn_stats(stats[:, b, :], acc[a][:, b, :]).then_inc(stat_steps, 1)
                dve.wait_ge(stat_steps, START + i * TB + TB)
                nc.vector.memset(idle[:, :], 0.0)
                for b in range(TB):
                    last = nc.vector.bn_aggr(mean_var[:, b, :], stats[:, b, :])
                last.then_inc(var_ready, 1)
                dve.wait_ge(std_ready, START + i + 1)
                nc.vector.reciprocal(inv_std[:, :], std[:, :]).then_inc(out_steps, 1)
                dve.wait_ge(out_steps, START + i + 1)
                if not early(i, 2):
                    in_turn(dve, out_done[a], i - 2, a, 16)
                for b in range(TB):
                    last = nc.vector.tensor_scalar(out_sb[a][:, b, :], acc[a][:, b, :], mean_var[:, b, 0:1], inv_std[:, b:b + 1],
                                                   ALU.subtract, ALU.mult)
                last.then_inc(out_ready, 1)

            staged(dve, take, add)


def clear(nc, counters):
    block = nc.Block()
    with block:
        @block.sync
        def _(sync):
            for counter in counters:
                sync.sem_clear(counter)


def tower(nc, x, freqs, w_tok, wqv, ident, mix_w):
    scratch = lambda name, shape, dt: nc.dram_tensor(name, shape, dt, kind="Internal").ap()
    h = scratch("h_tokens", (IMAGES, P, TB, DIM), F32)
    q_parts = scratch("q_parts", (IMAGES, 2, 2, DIM // 2, TOKENS), F16)
    v_parts = scratch("v_parts", (IMAGES, P, TB * HEADS * VW), BF16)
    att = scratch("att_tokens", (IMAGES, P, TB, DIM), F32)
    with ExitStack() as ctx:
        soft_rows_out, soft_fetched = soft_semaphores(nc, ctx, "rows_out"), soft_semaphores(nc, ctx, "fetched")
        clear(nc, embed(nc, x, freqs, w_tok, h))
        project(nc, h, wqv, ident, q_parts, v_parts)
        attend(nc, q_parts, v_parts, ident, att)
        mix(nc, h, att, ident, mix_w, soft_rows_out, soft_fetched)


def layouts(x, L0_tok_freq_bands, L0_tok_W, L0_attn_w_qkv, L0_attn_w_proj, L0_attn_b_proj, L0_ffn_W1, L0_ffn_b1,
            L0_ffn_W2, L0_ffn_b2, L0_ffn_Wr1, L0_ffn_br1, L0_ffn_Wr2, L0_ffn_br2):
    whole = np.ascontiguousarray
    xt = x.reshape(IMAGES, TOKENS, PATCH).transpose(0, 2, 1)
    blocks = xt[:, :FULL * P].reshape(IMAGES, FULL, P, TOKENS).transpose(0, 2, 1, 3)
    rest = np.concatenate([xt[:, FULL * P:]] * 2, axis=1)[:, :, None]
    freqs = np.zeros((P, BANDS + BANDS // 2), np.float32)
    freqs[:, :BANDS] = L0_tok_freq_bands
    freqs[:P // 2, BANDS:] = L0_tok_freq_bands[0::2]
    freqs[P // 2:, BANDS:] = L0_tok_freq_bands[1::2]
    w = L0_tok_W.reshape(DIM, PATCH, 2 * BANDS)
    w_tok = []
    for b, s in CHUNKS:
        for t in range(2):
            if s < FULL:
                w_tok.append(w[:, s * P:(s + 1) * P, b + BANDS * t].T)
            else:
                w_tok.append(np.concatenate([w[:, FULL * P:, b - 1 + BANDS * t].T, w[:, FULL * P:, b + BANDS * t].T]))
    w1 = L0_ffn_W1.transpose(2, 0, 1)
    rows = lambda a: whole(np.broadcast_to(a, (P, a.size)))
    return {
        "x": whole(np.concatenate([blocks, rest], axis=2).reshape(IMAGES, P, WIDE)),
        "freqs": freqs,
        "w_tok": whole(np.stack(w_tok, axis=1).reshape(P, NCH * DIM)),
        "wqv": whole(np.concatenate([L0_attn_w_qkv[:DIM], L0_attn_w_qkv[2 * DIM:]]).T),
        "ident": np.eye(P, dtype=np.float32),
        "w1_a": whole(w1[:P].reshape(P, -1)),
        "w1_b": whole(np.concatenate([w1[P:], w1[P:]]).reshape(P, -1)),
        "w2": whole(L0_ffn_W2.reshape(EXPERTS, DIM, FB, P).transpose(3, 0, 2, 1).reshape(P, -1)),
        "small_b1": whole(L0_ffn_b1.reshape(EXPERTS * FB, P).T),
        "small_b2": whole(np.broadcast_to(L0_ffn_b2, (P, EXPERTS, DIM))),
        "small_wp_a": whole(L0_attn_w_proj.T[:P]),
        "small_wp_b": whole(L0_attn_w_proj.T[P:]),
        "small_wr1_a": whole(L0_ffn_Wr1.T[:P]),
        "small_wr1_b": whole(L0_ffn_Wr1.T[P:]),
        "small_br1": whole(L0_ffn_br1.reshape(2, DIM // 2).T),
        "small_wr2": whole(L0_ffn_Wr2.T.reshape(2, DIM // 2, EXPERTS).transpose(1, 0, 2)),
        "small_br2": rows(L0_ffn_br2),
        "small_b_proj": rows(L0_attn_b_proj),
        "small_numbers": rows(np.arange(EXPERTS, dtype=np.float32)),
        "small_tile_numbers": rows(np.arange(TILES, dtype=np.float32)),
        "small_limits": rows(np.arange(LIMITS, dtype=np.float32) * TILE),
        "small_earlier": np.triu(np.ones((P, P), np.float32), 1),
        "small_before": whole(np.broadcast_to(np.tril(np.ones((EXPERTS, EXPERTS), np.float32), -1), (P, EXPERTS, EXPERTS))),
    }


def kernel(**inputs):
    import concourse.bacc as bacc
    from concourse.bass_utils import run_bass_kernel_spmd as run

    nc = bacc.Bacc("TRN2", target_bir_lowering=False, num_devices=1)
    arrays, aps = {}, {}
    for name, a in layouts(**{n: np.asarray(a) for n, a in inputs.items()}).items():
        arrays[f"in_{name}_dram"] = a
        aps[name] = nc.dram_tensor(f"in_{name}_dram", a.shape, mybir.dt.from_np(a.dtype), kind="ExternalInput").ap()
    out = nc.dram_tensor("out_0_dram", (IMAGES, P, TB, DIM), F32, kind="ExternalOutput").ap()
    mix_w = {n: aps[n] for n in ("w1_a", "w1_b", "w2")}
    mix_w["small"] = {n[len("small_"):]: a for n, a in aps.items() if n.startswith("small_")}
    mix_w["out"] = out
    tower(nc, aps["x"], aps["freqs"], aps["w_tok"], aps["wqv"], aps["ident"], mix_w)
    got = run(nc, [arrays], core_ids=[0]).results[0]["out_0_dram"]
    return got.transpose(0, 2, 1, 3).reshape(IMAGES, TOKENS, DIM)
```
